# Optimizing a Trainium2 kernel written in Bass

```python
import numpy as np
import jax
import jax.numpy as jnp

def _softmax(x, axis=-1):
    return jax.nn.softmax(x, axis=axis)

def _gelu(x):
    return jax.nn.gelu(x, approximate=True)

def _silu(x):
    return jax.nn.silu(x)

def _sigmoid(x):
    return jax.nn.sigmoid(x)

def _layernorm(x, axis=-1, eps=1e-05):
    m = jnp.mean(x, axis=axis, keepdims=True)
    v = jnp.var(x, axis=axis, keepdims=True)
    return (x - m) / jnp.sqrt(v + eps)

def _scatter_add(tgt, idx, src, axis=0):
    return tgt.at[idx].add(src)

def _segment_sum(src, seg, n):
    return jax.ops.segment_sum(src, seg, n)
kernel_name = 'mk_conv_attn_hybrid_d4_conv_nchw1024_r4_e5d30c'

def setup_inputs(seed: int=0):
    np.random.seed(seed)
    _w = jnp.asarray

    def _rec_inputs():
        import jax
        import jax.numpy as jnp
        _gk = jax.random.key(seed)
        x = -0.000125 + 0.9999 * jax.random.normal(jax.random.fold_in(_gk, 1), (8, 256, 16, 16), jnp.float32)
        return x
    x = _rec_inputs()

    def _L0_conv_setup():
        import jax, jax.numpy as jnp
        import numpy as np
        C_IN = 256
        C_INTER = 128
        EPS = 1e-05
        STD = 0.01

        def _conv1x1(x, w, b):
            return jnp.einsum('bchw,oc->bohw', x, w) + b[None, :, None, None]
        key = jax.random.key(seed)
        ks = jax.random.split(key, 12)

        def w(k, o, i):
            return jax.random.normal(k, (o, i), jnp.float32) * STD

        def b(k, o):
            return jax.random.normal(k, (o,), jnp.float32) * STD
        return {'x': jax.random.normal(ks[0], (8, C_IN, 16, 16), jnp.float32), 'theta_w': w(ks[1], C_INTER, C_IN), 'theta_b': b(ks[2], C_INTER), 'phi_w': w(ks[3], C_INTER, C_IN), 'phi_b': b(ks[4], C_INTER), 'g_w': w(ks[5], C_INTER, C_IN), 'g_b': b(ks[6], C_INTER), 'wz_w': w(ks[7], C_IN, C_INTER), 'wz_b': b(ks[8], C_IN), 'bn_gamma': jax.random.normal(ks[9], (C_IN,), jnp.float32) * 0.1, 'bn_beta': jax.random.normal(ks[10], (C_IN,), jnp.float32) * 0.1}
    _L0_conv_all = _L0_conv_setup()
    _L0_conv_in = {k: v for k, v in _L0_conv_all.items() if k in ('theta_w', 'theta_b', 'phi_w', 'phi_b', 'g_w', 'g_b', 'wz_w', 'wz_b', 'bn_gamma', 'bn_beta')}
    del _L0_conv_all

    def _L1_conv_setup():
        import jax, jax.numpy as jnp
        import numpy as np
        WEIGHT_BITS = 5
        QUANT_BITS = 16
        BN_EPS = 1e-05

        def _quant_weight_pow2(w):
            shift_min = -(2 ** (WEIGHT_BITS - 1) - 2)
            sign = jnp.sign(w)
            p = jnp.clip(jnp.round(jnp.log2(jnp.abs(w) + 1e-20)), shift_min, 0.0)
            wq = sign * jnp.exp2(p)
            return w + jax.lax.stop_gradient(wq - w)

        def _quant_act(x):
            qmax = 2.0 ** (QUANT_BITS - 1) - 1.0
            scale = jnp.maximum(jnp.max(jnp.abs(x)), 1e-12) / qmax
            xq = jnp.round(x / scale) * scale
            return x + jax.lax.stop_gradient(xq - x)

        def _conv(x, w, stride=1, pad=0, groups=1):
            return jax.lax.conv_general_dilated(x, w, (stride, stride), [(pad, pad), (pad, pad)], dimension_numbers=('NCHW', 'OIHW', 'NCHW'), feature_group_count=groups)

        def _shift_conv(x, w, stride=1, pad=0, groups=1, bias=None):
            y = _conv(_quant_act(x), _quant_weight_pow2(w), stride, pad, groups)
            if bias is not None:
                y = y + bias[None, :, None, None]
            return y

        def _bn(x, g, b, m, v):
            inv = g * jax.lax.rsqrt(v + BN_EPS)
            return x * inv[None, :, None, None] + (b - m * inv)[None, :, None, None]
        key = jax.random.key(seed)
        ks = jax.random.split(key, 8)
        B, C_in, H, W = (32, 256, 32, 32)
        width, C_out = (64, 256)
        inp = {'x': jax.random.normal(ks[0], (B, C_in, H, W), jnp.float32), 'w1': jax.random.normal(ks[1], (width, C_in, 1, 1), jnp.float32) * 0.05, 'peg_w': jax.random.normal(ks[2], (width, 1, 3, 3), jnp.float32) * 0.1, 'peg_b': jax.random.normal(ks[3], (width,), jnp.float32) * 0.01, 'w2': jax.random.normal(ks[4], (width, width, 3, 3), jnp.float32) * 0.05, 'w3': jax.random.normal(ks[5], (C_out, width, 1, 1), jnp.float32) * 0.05, 'bn1_g': jax.random.uniform(ks[6], (width,), jnp.float32, 0.5, 1.5), 'bn1_b': jnp.zeros((width,), jnp.float32), 'bn1_m': jnp.zeros((width,), jnp.float32), 'bn1_v': jnp.ones((width,), jnp.float32), 'bn2_g': jax.random.uniform(ks[7], (width,), jnp.float32, 0.5, 1.5), 'bn2_b': jnp.zeros((width,), jnp.float32), 'bn2_m': jnp.zeros((width,), jnp.float32), 'bn2_v': jnp.ones((width,), jnp.float32), 'bn3_g': jax.random.uniform(jax.random.fold_in(key, 9), (C_out,), jnp.float32, 0.5, 1.5), 'bn3_b': jnp.zeros((C_out,), jnp.float32), 'bn3_m': jnp.zeros((C_out,), jnp.float32), 'bn3_v': jnp.ones((C_out,), jnp.float32)}
        return inp
    _L1_conv_all = _L1_conv_setup()
    _L1_conv_in = {k: v for k, v in _L1_conv_all.items() if k in ('w1', 'peg_w', 'peg_b', 'w2', 'w3', 'bn1_g', 'bn1_b', 'bn1_m', 'bn1_v', 'bn2_g', 'bn2_b', 'bn2_m', 'bn2_v', 'bn3_g', 'bn3_b', 'bn3_m', 'bn3_v')}
    del _L1_conv_all

    def _L2_attn_setup():
        import math
        import jax, jax.numpy as jnp
        import numpy as np
        H = 16

        def get_alibi_slopes(n):

            def pow2_slopes(n):
                start = 2 ** (-2 ** (-(math.log2(n) - 3)))
                return [start * start ** i for i in range(n)]
            if math.log2(n).is_integer():
                return pow2_slopes(n)
            c = 2 ** math.floor(math.log2(n))
            return pow2_slopes(c) + get_alibi_slopes(2 * c)[0::2][:n - c]

        def alibi_bias(num_heads, L, dtype=jnp.float32):
            slopes = jnp.asarray(get_alibi_slopes(num_heads), dtype=dtype)
            pos = jnp.arange(L)
            rel = (pos[None, :] - pos[:, None]).astype(dtype)
            bias = slopes[:, None, None] * rel[None, :, :]
            causal = pos[None, :] <= pos[:, None]
            return jnp.where(causal[None, :, :], bias, -jnp.inf)
        key = jax.random.key(seed)
        ks = jax.random.split(key, 4)
        D = 256
        B, L = (2, 512)
        s_in = 1.0 / math.sqrt(D)
        return {'x': jax.random.normal(ks[0], (B, L, D), dtype=jnp.float32), 'w_in': jax.random.normal(ks[1], (D, 3 * D), dtype=jnp.float32) * s_in, 'b_in': jnp.zeros((3 * D,), dtype=jnp.float32), 'w_out': jax.random.normal(ks[2], (D, D), dtype=jnp.float32) * s_in, 'b_out': jnp.zeros((D,), dtype=jnp.float32)}
    _L2_attn_all = _L2_attn_setup()
    _L2_attn_in = {k: v for k, v in _L2_attn_all.items() if k in ('w_in', 'b_in', 'w_out', 'b_out')}
    del _L2_attn_all

    def _L2_ffn_setup():
        import jax, jax.numpy as jnp
        import numpy as np
        EPS = 1e-05

        @jax.custom_vjp
        def ste_quantize(w):
            scale = jnp.maximum(jnp.mean(jnp.abs(w)), EPS)
            return jnp.clip(jnp.round(w / scale), -1.0, 1.0)

        def _ste_fwd(w):
            return (ste_quantize(w), None)

        def _ste_bwd(_, g):
            return (g,)
        ste_quantize.defvjp(_ste_fwd, _ste_bwd)
        key = jax.random.key(seed)
        k1, k2 = jax.random.split(key)
        x = jax.random.normal(k1, (8, 2048, 256), dtype=jnp.float32)
        weight = jax.random.normal(k2, (256, 256), dtype=jnp.float32) * 0.02
        return {'x': x, 'weight': weight}
    _L2_ffn_all = _L2_ffn_setup()
    _L2_ffn_in = {k: v for k, v in _L2_ffn_all.items() if k in ('weight',)}
    del _L2_ffn_all

    def _L3_attn_setup():
        import jax, jax.numpy as jnp
        import numpy as np
        D_MODEL = 256
        NUM_HEADS = 16
        D_K = D_MODEL // NUM_HEADS
        key = jax.random.key(seed)
        ks = jax.random.split(key, 5)
        b, t = (2, 512)
        scale = 1.0 / np.sqrt(D_MODEL)
        return {'x': jax.random.normal(ks[0], (b, t, D_MODEL), dtype=jnp.float32), 'w_q': jax.random.normal(ks[1], (D_MODEL, D_MODEL), dtype=jnp.float32) * scale, 'w_k': jax.random.normal(ks[2], (D_MODEL, D_MODEL), dtype=jnp.float32) * scale, 'w_v': jax.random.normal(ks[3], (D_MODEL, D_MODEL), dtype=jnp.float32) * scale, 'w_o': jax.random.normal(ks[4], (D_MODEL, D_MODEL), dtype=jnp.float32) * scale}
    _L3_attn_all = _L3_attn_setup()
    _L3_attn_in = {k: v for k, v in _L3_attn_all.items() if k in ('w_q', 'w_k', 'w_v', 'w_o')}
    del _L3_attn_all

    def _L3_ffn_setup():
        import jax, jax.numpy as jnp
        import numpy as np
        TOP_K = 2
        key = jax.random.key(seed)
        ks = jax.random.split(key, 7)
        B, S, D, E = (8, 512, 256, 8)
        scale = 1.0 / np.sqrt(D)
        return {'X': jax.random.normal(ks[0], (B, S, D), dtype=jnp.float32), 'We': jax.random.normal(ks[1], (E, D, D), dtype=jnp.float32) * scale, 'be': jax.random.normal(ks[2], (E, D), dtype=jnp.float32) * scale, 'Wr': jax.random.normal(ks[3], (E, D), dtype=jnp.float32) * scale, 'br': jax.random.normal(ks[4], (E,), dtype=jnp.float32) * scale, 'Wo': jax.random.normal(ks[5], (D, D), dtype=jnp.float32) * scale, 'bo': jax.random.normal(ks[6], (D,), dtype=jnp.float32) * scale}
    _L3_ffn_all = _L3_ffn_setup()
    _L3_ffn_in = {k: v for k, v in _L3_ffn_all.items() if k in ('We', 'be', 'Wr', 'br', 'Wo', 'bo')}
    del _L3_ffn_all
    return {'x': x, 'L0_conv_theta_w': _L0_conv_in['theta_w'], 'L0_conv_theta_b': _L0_conv_in['theta_b'], 'L0_conv_phi_w': _L0_conv_in['phi_w'], 'L0_conv_phi_b': _L0_conv_in['phi_b'], 'L0_conv_g_w': _L0_conv_in['g_w'], 'L0_conv_g_b': _L0_conv_in['g_b'], 'L0_conv_wz_w': _L0_conv_in['wz_w'], 'L0_conv_wz_b': _L0_conv_in['wz_b'], 'L0_conv_bn_gamma': _L0_conv_in['bn_gamma'], 'L0_conv_bn_beta': _L0_conv_in['bn_beta'], 'L1_conv_w1': _L1_conv_in['w1'], 'L1_conv_peg_w': _L1_conv_in['peg_w'], 'L1_conv_peg_b': _L1_conv_in['peg_b'], 'L1_conv_w2': _L1_conv_in['w2'], 'L1_conv_w3': _L1_conv_in['w3'], 'L1_conv_bn1_g': _L1_conv_in['bn1_g'], 'L1_conv_bn1_b': _L1_conv_in['bn1_b'], 'L1_conv_bn1_m': _L1_conv_in['bn1_m'], 'L1_conv_bn1_v': _L1_conv_in['bn1_v'], 'L1_conv_bn2_g': _L1_conv_in['bn2_g'], 'L1_conv_bn2_b': _L1_conv_in['bn2_b'], 'L1_conv_bn2_m': _L1_conv_in['bn2_m'], 'L1_conv_bn2_v': _L1_conv_in['bn2_v'], 'L1_conv_bn3_g': _L1_conv_in['bn3_g'], 'L1_conv_bn3_b': _L1_conv_in['bn3_b'], 'L1_conv_bn3_m': _L1_conv_in['bn3_m'], 'L1_conv_bn3_v': _L1_conv_in['bn3_v'], 'L2_attn_w_in': _L2_attn_in['w_in'], 'L2_attn_b_in': _L2_attn_in['b_in'], 'L2_attn_w_out': _L2_attn_in['w_out'], 'L2_attn_b_out': _L2_attn_in['b_out'], 'L2_ffn_weight': _L2_ffn_in['weight'], 'L3_attn_w_q': _L3_attn_in['w_q'], 'L3_attn_w_k': _L3_attn_in['w_k'], 'L3_attn_w_v': _L3_attn_in['w_v'], 'L3_attn_w_o': _L3_attn_in['w_o'], 'L3_ffn_We': _L3_ffn_in['We'], 'L3_ffn_be': _L3_ffn_in['be'], 'L3_ffn_Wr': _L3_ffn_in['Wr'], 'L3_ffn_br': _L3_ffn_in['br'], 'L3_ffn_Wo': _L3_ffn_in['Wo'], 'L3_ffn_bo': _L3_ffn_in['bo']}

def reference(x, L0_conv_theta_w, L0_conv_theta_b, L0_conv_phi_w, L0_conv_phi_b, L0_conv_g_w, L0_conv_g_b, L0_conv_wz_w, L0_conv_wz_b, L0_conv_bn_gamma, L0_conv_bn_beta, L1_conv_w1, L1_conv_peg_w, L1_conv_peg_b, L1_conv_w2, L1_conv_w3, L1_conv_bn1_g, L1_conv_bn1_b, L1_conv_bn1_m, L1_conv_bn1_v, L1_conv_bn2_g, L1_conv_bn2_b, L1_conv_bn2_m, L1_conv_bn2_v, L1_conv_bn3_g, L1_conv_bn3_b, L1_conv_bn3_m, L1_conv_bn3_v, L2_attn_w_in, L2_attn_b_in, L2_attn_w_out, L2_attn_b_out, L2_ffn_weight, L3_attn_w_q, L3_attn_w_k, L3_attn_w_v, L3_attn_w_o, L3_ffn_We, L3_ffn_be, L3_ffn_Wr, L3_ffn_br, L3_ffn_Wo, L3_ffn_bo):
    import jax
    import jax.numpy as jnp

    def _L0_conv_ref(x, theta_w, theta_b, phi_w, phi_b, g_w, g_b, wz_w, wz_b, bn_gamma, bn_beta):
        import jax, jax.numpy as jnp
        import numpy as np
        C_IN = 256
        C_INTER = 128
        EPS = 1e-05
        STD = 0.01

        def _conv1x1(x, w, b):
            return jnp.einsum('bchw,oc->bohw', x, w) + b[None, :, None, None]
        B, C, H, W = x.shape
        theta = _conv1x1(x, theta_w, theta_b).reshape(B, C_INTER, H * W)
        xp = jax.lax.reduce_window(x, -jnp.inf, jax.lax.max, (1, 1, 2, 2), (1, 1, 2, 2), 'VALID')
        Hp, Wp = (xp.shape[2], xp.shape[3])
        phi = _conv1x1(xp, phi_w, phi_b).reshape(B, C_INTER, Hp * Wp)
        g = _conv1x1(xp, g_w, g_b).reshape(B, C_INTER, Hp * Wp)
        attn = jnp.einsum('bcn,bcm->bnm', theta, phi) * C_INTER ** (-0.5)
        attn = jax.nn.softmax(attn, axis=-1)
        y = jnp.einsum('bcm,bnm->bcn', g, attn).reshape(B, C_INTER, H, W)
        z = _conv1x1(y, wz_w, wz_b)
        mean = z.mean(axis=(0, 2, 3), keepdims=True)
        var = jnp.mean((z - mean) ** 2, axis=(0, 2, 3), keepdims=True)
        z = (z - mean) * jax.lax.rsqrt(var + EPS)
        z = z * bn_gamma[None, :, None, None] + bn_beta[None, :, None, None]
        return x + z

    def _L1_conv_ref(x, w1, peg_w, peg_b, w2, w3, bn1_g, bn1_b, bn1_m, bn1_v, bn2_g, bn2_b, bn2_m, bn2_v, bn3_g, bn3_b, bn3_m, bn3_v):
        import jax, jax.numpy as jnp
        import numpy as np
        WEIGHT_BITS = 5
        QUANT_BITS = 16
        BN_EPS = 1e-05

        def _quant_weight_pow2(w):
            shift_min = -(2 ** (WEIGHT_BITS - 1) - 2)
            sign = jnp.sign(w)
            p = jnp.clip(jnp.round(jnp.log2(jnp.abs(w) + 1e-20)), shift_min, 0.0)
            wq = sign * jnp.exp2(p)
            return w + jax.lax.stop_gradient(wq - w)

        def _quant_act(x):
            qmax = 2.0 ** (QUANT_BITS - 1) - 1.0
            scale = jnp.maximum(jnp.max(jnp.abs(x)), 1e-12) / qmax
            xq = jnp.round(x / scale) * scale
            return x + jax.lax.stop_gradient(xq - x)

        def _conv(x, w, stride=1, pad=0, groups=1):
            return jax.lax.conv_general_dilated(x, w, (stride, stride), [(pad, pad), (pad, pad)], dimension_numbers=('NCHW', 'OIHW', 'NCHW'), feature_group_count=groups)

        def _shift_conv(x, w, stride=1, pad=0, groups=1, bias=None):
            y = _conv(_quant_act(x), _quant_weight_pow2(w), stride, pad, groups)
            if bias is not None:
                y = y + bias[None, :, None, None]
            return y

        def _bn(x, g, b, m, v):
            inv = g * jax.lax.rsqrt(v + BN_EPS)
            return x * inv[None, :, None, None] + (b - m * inv)[None, :, None, None]
        residual = x
        h = _shift_conv(x, w1)
        h = _shift_conv(h, peg_w, stride=1, pad=1, groups=64, bias=peg_b)
        h = jax.nn.relu(_bn(h, bn1_g, bn1_b, bn1_m, bn1_v))
        h = _shift_conv(h, w2, stride=1, pad=1)
        h = jax.nn.relu(_bn(h, bn2_g, bn2_b, bn2_m, bn2_v))
        h = _shift_conv(h, w3)
        h = _bn(h, bn3_g, bn3_b, bn3_m, bn3_v)
        return jax.nn.relu(h + residual)

    def _L2_attn_ref(x, w_in, b_in, w_out, b_out):
        import math
        import jax, jax.numpy as jnp
        import numpy as np
        H = 16

        def get_alibi_slopes(n):

            def pow2_slopes(n):
                start = 2 ** (-2 ** (-(math.log2(n) - 3)))
                return [start * start ** i for i in range(n)]
            if math.log2(n).is_integer():
                return pow2_slopes(n)
            c = 2 ** math.floor(math.log2(n))
            return pow2_slopes(c) + get_alibi_slopes(2 * c)[0::2][:n - c]

        def alibi_bias(num_heads, L, dtype=jnp.float32):
            slopes = jnp.asarray(get_alibi_slopes(num_heads), dtype=dtype)
            pos = jnp.arange(L)
            rel = (pos[None, :] - pos[:, None]).astype(dtype)
            bias = slopes[:, None, None] * rel[None, :, :]
            causal = pos[None, :] <= pos[:, None]
            return jnp.where(causal[None, :, :], bias, -jnp.inf)
        B, L, D = x.shape
        dh = D // H
        qkv = x @ w_in + b_in
        q, k, v = jnp.split(qkv, 3, axis=-1)

        def heads(t):
            return t.reshape(B, L, H, dh).transpose(0, 2, 1, 3)
        q, k, v = (heads(q), heads(k), heads(v))
        scores = jnp.einsum('bhqd,bhkd->bhqk', q, k) / math.sqrt(dh)
        scores = scores + alibi_bias(H, L, scores.dtype)[None]
        attn = jax.nn.softmax(scores, axis=-1)
        out = jnp.einsum('bhqk,bhkd->bhqd', attn, v)
        out = out.transpose(0, 2, 1, 3).reshape(B, L, D)
        return out @ w_out + b_out

    def _L2_ffn_ref(x, weight):
        import jax, jax.numpy as jnp
        import numpy as np
        EPS = 1e-05

        @jax.custom_vjp
        def ste_quantize(w):
            scale = jnp.maximum(jnp.mean(jnp.abs(w)), EPS)
            return jnp.clip(jnp.round(w / scale), -1.0, 1.0)

        def _ste_fwd(w):
            return (ste_quantize(w), None)

        def _ste_bwd(_, g):
            return (g,)
        ste_quantize.defvjp(_ste_fwd, _ste_bwd)
        w_ternary = ste_quantize(weight)
        scale = jnp.maximum(jnp.mean(jnp.abs(weight)), EPS)
        return jnp.einsum('bsi,oi->bso', x, w_ternary * scale)

    def _L3_attn_ref(x, w_q, w_k, w_v, w_o):
        import jax, jax.numpy as jnp
        import numpy as np
        D_MODEL = 256
        NUM_HEADS = 16
        D_K = D_MODEL // NUM_HEADS
        b, t, _ = x.shape
        h, d_k = (NUM_HEADS, D_K)
        q = (x @ w_q.T).reshape(b, t, h, d_k).transpose(0, 2, 1, 3)
        k = (x @ w_k.T).reshape(b, t, h, d_k).transpose(0, 2, 1, 3)
        v = (x @ w_v.T).reshape(b, t, h, d_k).transpose(0, 2, 1, 3)
        scores = jnp.einsum('bhqd,bhkd->bhqk', q, k) / jnp.sqrt(jnp.asarray(d_k, x.dtype))
        causal = jnp.tril(jnp.ones((t, t), dtype=bool))
        scores = jnp.where(causal, scores, jnp.asarray(-jnp.inf, scores.dtype))
        attn = jax.nn.softmax(scores, axis=-1)
        y = jnp.einsum('bhqk,bhkd->bhqd', attn, v)
        y = y.transpose(0, 2, 1, 3).reshape(b, t, h * d_k)
        return y @ w_o.T

    def _L3_ffn_ref(X, We, be, Wr, br, Wo, bo):
        import jax, jax.numpy as jnp
        import numpy as np
        TOP_K = 2
        router_logits = jnp.einsum('bsd,ed->bse', X, Wr) + br
        router_weights = jax.nn.softmax(router_logits, axis=-1)
        top_k_weights, top_k_indices = jax.lax.top_k(router_weights, TOP_K)
        expert_outputs = jnp.einsum('bsd,ehd->bseh', X, We) + be
        gathered = jnp.take_along_axis(expert_outputs, top_k_indices[..., None], axis=2)
        combined = jnp.sum(top_k_weights[..., None] * gathered, axis=2)
        out = jnp.einsum('bsd,hd->bsh', combined, Wo) + bo
        return out

    def _gn(v, G=32, eps=1e-05):
        B_, C_, H_, W_ = v.shape
        g = v.reshape(B_, G, C_ // G, H_, W_)
        m = jnp.mean(g, axis=(2, 3, 4), keepdims=True)
        s = jnp.var(g, axis=(2, 3, 4), keepdims=True)
        return ((g - m) / jnp.sqrt(s + eps)).reshape(v.shape)

    def _ln_c(v, eps=1e-06):
        m = jnp.mean(v, axis=1, keepdims=True)
        s = jnp.var(v, axis=1, keepdims=True)
        return (v - m) / jnp.sqrt(s + eps)

    def _ln_t(v, eps=1e-05):
        m = jnp.mean(v, axis=-1, keepdims=True)
        s = jnp.var(v, axis=-1, keepdims=True)
        return (v - m) / jnp.sqrt(s + eps)

    def _to_tokens(v):
        B_, C_, H_, W_ = v.shape
        return v.reshape(B_, C_, H_ * W_).transpose(0, 2, 1)

    def _from_tokens(t, like):
        B_, C_, H_, W_ = like.shape
        return t.transpose(0, 2, 1).reshape(B_, C_, H_, W_)
    x = _L0_conv_ref(x, L0_conv_theta_w, L0_conv_theta_b, L0_conv_phi_w, L0_conv_phi_b, L0_conv_g_w, L0_conv_g_b, L0_conv_wz_w, L0_conv_wz_b, L0_conv_bn_gamma, L0_conv_bn_beta)
    x = _L1_conv_ref(x, L1_conv_w1, L1_conv_peg_w, L1_conv_peg_b, L1_conv_w2, L1_conv_w3, L1_conv_bn1_g, L1_conv_bn1_b, L1_conv_bn1_m, L1_conv_bn1_v, L1_conv_bn2_g, L1_conv_bn2_b, L1_conv_bn2_m, L1_conv_bn2_v, L1_conv_bn3_g, L1_conv_bn3_b, L1_conv_bn3_m, L1_conv_bn3_v)
    t = _to_tokens(x)
    t = t + _L2_attn_ref(_ln_t(t), L2_attn_w_in, L2_attn_b_in, L2_attn_w_out, L2_attn_b_out)
    t = t + _L2_ffn_ref(_ln_t(t), L2_ffn_weight)
    t = t + _L3_attn_ref(_ln_t(t), L3_attn_w_q, L3_attn_w_k, L3_attn_w_v, L3_attn_w_o)
    t = t + _L3_ffn_ref(_ln_t(t), L3_ffn_We, L3_ffn_be, L3_ffn_Wr, L3_ffn_br, L3_ffn_Wo, L3_ffn_bo)
    x = _from_tokens(t, x)
    return x

_drawn_inputs = setup_inputs


def setup_inputs(seed=0):
    import zlib

    import numpy as np

    out = dict(_drawn_inputs(seed))
    spreads = {'L1_conv_bn1_b': (0.0, 0.1),
     'L1_conv_bn1_m': (0.0, 0.1),
     'L1_conv_bn1_v': (1.0, 0.2),
     'L1_conv_bn2_b': (0.0, 0.1),
     'L1_conv_bn2_m': (0.0, 0.1),
     'L1_conv_bn2_v': (1.0, 0.2),
     'L1_conv_bn3_b': (0.0, 0.1),
     'L1_conv_bn3_m': (0.0, 0.1),
     'L1_conv_bn3_v': (1.0, 0.2),
     'L2_attn_b_in': (0.0, 0.1),
     'L2_attn_b_out': (0.0, 0.1)}
    factors = {'L0_conv_theta_w': 7.294,
     'L0_conv_theta_b': 27.295,
     'L0_conv_phi_w': 7.813,
     'L0_conv_phi_b': 64.0,
     'L0_conv_g_b': 64.0,
     'L0_conv_wz_b': 64.0,
     'L1_conv_peg_b': 3.968}
    for name, (base, spread) in spreads.items():
        noise = np.random.default_rng([zlib.crc32(name.encode()), seed]).standard_normal(out[name].shape)
        drawn = base * np.exp(spread * noise) if base else spread * noise
        out[name] = jnp.asarray(drawn.astype(out[name].dtype))
    for name, factor in factors.items():
        out[name] = (out[name] * factor).astype(out[name].dtype)
    return out
```

```python
from contextlib import ExitStack

import concourse.bass as bass
from concourse import mybir

F32 = mybir.dt.float32
BF16 = mybir.dt.bfloat16
I32 = mybir.dt.int32
ALU = mybir.AluOpType
ACT = mybir.ActivationFunctionType
AX = mybir.AxisListType

P = 128
BATCH, CH, IMG = 8, 256, 16
PIX = IMG * IMG
TOK = BATCH * PIX
NC2 = CH // P
INTER = 128
POOLED = PIX // 4
QUART = TOK // 4
WID = 64
PAD = IMG + 2
HEADS, DH = 16, 16
GROUPS = 4
EXPERTS = 8
SLOT = 32
PAIRS = BATCH // 2

QMAX = 2.0 ** 15 - 1.0
MIN_ABS = 1e-12
ROUND_1 = 1.5 * 2.0 ** 23
ROUND_256 = 1.5 * 2.0 ** 31
SQRT2 = 1.4142135
EPS = 1e-5
MASKED = -1e30



def columns(*fields):
    at, out = 0, {}
    for name, width in fields:
        out[name] = (at, width)
        at += width
    return out, at


FIX, FIX_N = columns(("ident", P), ("ones", P), ("stack", P), ("parity", 2), ("tie", 2 * EXPERTS),
                     ("low_half", 1), ("half_sign", 1), ("half_shift", 1), ("minus_half", 2))
FIXB, FIXB_N = columns(("ident", P), ("tri0", 4 * P), ("tri1", 2 * P), ("pos", 2 * P), ("alibi", 3 * GROUPS * 4 * P))
W0, W0_N = columns(("theta", NC2 * INTER), ("phi", NC2 * INTER), ("g", NC2 * INTER), ("wz", CH), ("g_b", INTER),
                   ("theta_b", 1), ("phi_b", 1), ("wz_b", NC2), ("gamma", NC2), ("beta", NC2))
W1, W1_N = columns(("w1", NC2 * P), ("w2", 9 * P), ("w3", CH), ("peg", 9), ("peg_b", 1),
                   ("g1", 1), ("b1", 1), ("m1", 1), ("v1", 1), ("g2", 1), ("b2", 1), ("m2", 1), ("v2", 1),
                   ("g3", 2), ("b3", 2), ("m3", 2), ("v3", 2))
QUANT = W1["peg_b"][0]
WT, WT_N = columns(("in0", NC2 * 3 * CH), ("out0", NC2 * CH), ("in1", NC2 * 3 * CH), ("out1", NC2 * CH),
                   ("tern", NC2 * CH), ("bv0", CH), ("bo0", CH), ("bq0", NC2), ("bk0", NC2))
WM, WM_N = columns(("We", NC2 * EXPERTS * CH), ("Wr", NC2 * EXPERTS), ("Wo", NC2 * CH), ("be", CH), ("bo", NC2),
                   ("br", 2 * EXPERTS))

UNITS = 3 * GROUPS
RING = 6


def head(g, j):
    return 8 * (j // 2) + 2 * g + j % 2


def loop_jobs():
    jobs = []
    for s in range(4):
        jobs += [("T", s, a) for a in range(2)]
        if s in (0, 2):
            jobs += [(k, s, a) for a in range(2) for k in "QKV"]
            for t in range(2 * UNITS + 6):
                if t < 2 * UNITS:
                    jobs.append(("S", s, t))
                if 3 <= t < 2 * UNITS + 3:
                    jobs.append(("PT", s, t - 3))
                if t >= 8 and (t - 8) % 3 == 0:
                    jobs.append(("OX", s, (t - 8) // 3))
                if t == 19:
                    jobs.append(("AT", s, 0))
                if t == 21:
                    jobs.append(("PR", s, 0))
            jobs += [("AT", s, 1), ("PR", s, 1)]
        if s == 1:
            jobs += [("FF", s, a) for a in range(2)]
        if s == 3:
            for a in range(2):
                jobs.append(("R", s, a))
            for a in range(2):
                jobs += [("E", s, a, n) for n in range(4)]
                jobs += [("GT", s, a), ("GB", s, a)]
                jobs += [("E", s, a, n) for n in range(4, 8)]
            for a in range(2):
                jobs += [("CT", s, a), ("FO", s, a)]
    return jobs


def bank_plan():
    where, used = {}, [0] * RING
    for n, job in enumerate(loop_jobs()):
        b = n % RING
        where[job] = (b, used[b])
        used[b] += 1
    return where, used


PLAN, PER_BANK = bank_plan()


def build(nc, x_in, fix_in, fixb_in, w0_in, w1_in, wt_in, wm_in, out):
    ctx = ExitStack()
    with ctx:
        def sb(name, shape, dt=F32, c=ctx):
            return c.enter_context(nc.sbuf_tensor(name, shape, dt))

        def sem(name):
            return ctx.enter_context(nc.semaphore(name))

        ps = ctx.enter_context(nc.psum_tensor("ps", [P, 8, 512], F32))

        fix = sb("fix", [P, FIX_N])
        fixb = sb("fixb", [P, FIXB_N], BF16)
        wt = sb("wt", [P, WT_N])
        wm = sb("wm", [P, WM_N])
        X = sb("X", [P, 2 * BATCH, CH])

        def F(name, lo=0, n=None):
            at, w = FIX[name]
            return fix[:, at + lo:at + lo + (w - lo if n is None else n)]

        def FB(name, lo=0, n=None):
            at, w = FIXB[name]
            return fixb[:, at + lo:at + lo + (w - lo if n is None else n)]

        def T(name, lo=0, n=None):
            at, w = WT[name]
            return wt[:, at + lo:at + lo + (w - lo if n is None else n)]

        def M(name, lo=0, n=None):
            at, w = WM[name]
            return wm[:, at + lo:at + lo + (w - lo if n is None else n)]

        fix_loaded = sem("fix_loaded")
        fixb_loaded = sem("fixb_loaded")
        w0_loaded = sem("w0_loaded")
        w1_loaded = sem("w1_loaded")
        x_loaded = [sem(f"x_loaded{q}") for q in range(4)]
        wt_loaded = sem("wt_loaded")
        wm_loaded = sem("wm_loaded")
        stored = sem("stored")
        dve_done = sem("dve_done")
        tern_summed = sem("tern_summed")

        with ExitStack() as c1:
            def eb(name, shape, dt=F32):
                return sb(name, shape, dt, c1)

            w0 = eb("w0", [P, W0_N])
            w1 = eb("w1", [P, W1_N])
            xc = eb("xc", [P, NC2, TOK])
            z = eb("z", [P, NC2, TOK])
            x1 = eb("x1", [P, NC2, TOK])
            th = eb("th", [P, TOK])
            ys = eb("ys", [P, TOK])
            pool_w = eb("pool_w", [P, NC2, QUART // 2])
            xp = eb("xp", [P, NC2, BATCH * POOLED])
            ph = eb("ph", [P, BATCH * POOLED])
            gt = eb("gt", [P, 4, INTER])
            sc = eb("sc", [P, 2, BATCH, POOLED])
            at = eb("at", [P, 4, PIX])
            sc_max = eb("sc_max", [P, 2 * BATCH])
            sc_sum = eb("sc_sum", [P, 2 * BATCH])
            sc_inv = eb("sc_inv", [P, 2 * BATCH])
            zst = eb("zst", [P, NC2, 4, 6])
            zmv = eb("zmv", [P, NC2, 2])
            small = eb("small", [P, 96])
            tern_sum = eb("tern_sum", [P, 1])
            qbits = eb("qbits", [P, QUANT])
            qsign = eb("qsign", [P, QUANT])
            w1q = eb("w1q", [P, NC2, P], BF16)
            w2q = eb("w2q", [P, 9, P], BF16)
            w3q = eb("w3q", [P, CH], BF16)
            pegq = eb("pegq", [P, 9])
            dwq = eb("dwq", [P, 9, P], BF16)
            hp1 = eb("hp1", [P, BATCH, PAD, PAD], BF16)
            hp2 = eb("hp2", [P, BATCH, PAD, PAD], BF16)
            hq3 = eb("hq3", [P, TOK], BF16)

            hi = ys[:, :].bitcast(BF16)
            lo = th[:, :].bitcast(BF16)
            r1 = z
            r256 = xc
            n1 = z[:, 0, :]
            n256 = z[:, 1, :]
            h = xc[:, 0, :]
            pre = xc
            x2 = z

            def A0(name, lo_=0, n=None):
                a_, w_ = W0[name]
                return w0[:, a_ + lo_:a_ + lo_ + (w_ - lo_ if n is None else n)]

            def A1(name, lo_=0, n=None):
                a_, w_ = W1[name]
                return w1[:, a_ + lo_:a_ + lo_ + (w_ - lo_ if n is None else n)]

            cols = iter(range(96))

            def col(n=1):
                c = [next(cols) for _ in range(n)]
                return small[:, c[0]:c[0] + n]

            z_ve, z_rstd, z_a, z_b = col(2), col(2), col(2), col(2)
            z_t = col(2)
            inv_ve = [col(1), col(1), col(2)]
            inv_rs = [col(1), col(1), col(2)]
            inv_g = [col(1), col(1), col(2)]
            mi = [col(1), col(1), col(2)]
            bnb = [col(1), col(1), col(2)]
            pb1 = col(1)
            aff_a = [col(1), col(1), col(2)]
            maxes = [col(4) for _ in range(4)]
            gmax = [col(1) for _ in range(4)]
            gone = [col(1) for _ in range(4)]
            scl = [col(1) for _ in range(4)]
            isc = [col(1) for _ in range(4)]
            fac = [col(1) for _ in range(4)]
            facn = col(1), col(1), col(1), col(1)

            theta_done = sem("theta_done")
            theta_out = sem("theta_out")
            pooled = sem("pooled")
            phi_done = sem("phi_done")
            phi_out = sem("phi_out")
            g_done = sem("g_done")
            g_out = sem("g_out")
            scores_done = sem("scores_done")
            shifted = sem("shifted")
            exped = sem("exped")
            weights_ready = sem("weights_ready")
            turned = sem("turned")
            turned_out_dve = sem("turned_out_dve")
            turned_out_act = sem("turned_out_act")
            y_done = sem("y_done")
            y_out = sem("y_out")
            z_done = sem("z_done")
            z_out = sem("z_out")
            z_var = sem("z_var")
            z_pow = sem("z_pow")
            z_affine = sem("z_affine")
            x1_part = sem("x1_part")
            x1_ready = sem("x1_ready")
            signs = sem("signs")
            wq_ready = sem("wq_ready")
            padded_zero = sem("padded_zero")
            bn_ve = sem("bn_ve")
            bn_pow = sem("bn_pow")
            max_ready = sem("max_ready")
            max_row = sem("max_row")
            max_one = sem("max_one")
            max_all = sem("max_all")
            scale_ready = sem("scale_ready")
            rounded = sem("rounded")
            parts_ready = sem("parts_ready")
            conv_done = sem("conv_done")
            relu_out = sem("relu_out")
            res_added = sem("res_added")
            x2_ready = sem("x2_ready")
            tok_done = sem("tok_done")
            tok_out_dve = sem("tok_out_dve")
            tok_out_act = sem("tok_out_act")

            block = c1.enter_context(nc.Block())

            @block.sync
            def _(sp):
                sp.dma_start(w0[:], w0_in).then_inc(w0_loaded, 16)
                for q in range(4):
                    for c in range(NC2):
                        sp.dma_start(
                            xc[:, c, q * QUART:(q + 1) * QUART].rearrange("p (b n) -> p b n", b=2),
                            x_in[2 * q:2 * q + 2, c * P:(c + 1) * P, :].rearrange("b p n -> p b n"),
                        ).then_inc(x_loaded[q], 16)
                sp.dma_start(fix[:], fix_in).then_inc(fix_loaded, 16)
                sp.dma_start(w1[:], w1_in).then_inc(w1_loaded, 16)
                sp.dma_start(fixb[:], fixb_in.bitcast(BF16)).then_inc(fixb_loaded, 16)
                sp.dma_start(wt[:], wt_in).then_inc(wt_loaded, 16)
                sp.dma_start(wm[:], wm_in).then_inc(wm_loaded, 16)

            @block.gpsimd
            def _(pool):
                pool.memset(hp1[:], 0.0).then_inc(padded_zero, 1)
                pool.memset(hp2[:], 0.0).then_inc(padded_zero, 1)
                pool.wait_ge(fix_loaded, 16)
                pool.wait_ge(bn_ve, 3)
                for k in range(3):
                    pool.tensor_tensor(inv_rs[k], inv_ve[k], F("minus_half", 0, 2 if k == 2 else 1),
                                       ALU.pow).then_inc(bn_pow, 1)
                pool.wait_ge(z_var, 1)
                pool.tensor_tensor(z_rstd, z_ve, F("minus_half"), ALU.pow).then_inc(z_pow, 1)

            @block.tensor
            def _(pe):
                pe.wait_ge(w0_loaded, 16)
                for q in range(4):
                    pe.wait_ge(x_loaded[q], 32)
                    for c in range(NC2):
                        mm = pe.matmul(ps[:, q, :], A0("theta", c * P, P), xc[:, c, q * QUART:(q + 1) * QUART],
                                       start=(c == 0), stop=(c == 1))
                    mm.then_inc(theta_done, 1)
                pe.wait_ge(pooled, 4)
                for c in range(NC2):
                    mm = pe.matmul(ps[:, 4, :], A0("phi", c * P, P), xp[:, c, :], start=(c == 0), stop=(c == 1))
                mm.then_inc(phi_done, 1)
                for q in range(4):
                    for c in range(NC2):
                        mm = pe.matmul(ps[:, 5, q * P:(q + 1) * P], xp[:, c, q * P:(q + 1) * P], A0("g", c * P, P),
                                       start=(c == 0), stop=(c == 1))
                mm.then_inc(g_done, 1)
                pe.wait_ge(theta_out, 4)
                pe.wait_ge(phi_out, 1)
                for n in range(2):
                    for b in range(BATCH):
                        mm = pe.matmul(ps[:, 6 + n, b * POOLED:(b + 1) * POOLED],
                                       th[:, b * PIX + n * P:b * PIX + (n + 1) * P],
                                       ph[:, b * POOLED:(b + 1) * POOLED], start=True, stop=True)
                    mm.then_inc(scores_done, 1)
                pe.wait_ge(weights_ready, 1)
                pe.wait_ge(fix_loaded, 16)
                for p in range(4):
                    for n in range(2):
                        mm = pe.transpose(ps[:, p // 2, (p % 2) * PIX + n * P:(p % 2) * PIX + (n + 1) * P],
                                          sc[:, n, 2 * p:2 * p + 2, :].rearrange("p b m -> p (b m)"), F("ident"))
                    if p % 2:
                        mm.then_inc(turned, 1)
                pe.wait_ge(g_out, 1)
                for hb in range(2):
                    pe.wait_ge(turned_out_act if hb else turned_out_dve, 1)
                    for k in range(2):
                        p = 2 * hb + k
                        for par in range(2):
                            r = par * POOLED
                            mm = pe.matmul(ps[:, 2 + 2 * par + hb, k * PIX:(k + 1) * PIX],
                                           gt[r:r + POOLED, p, :], at[r:r + POOLED, p, :], start=True, stop=True)
                    mm.then_inc(y_done, 1)
                pe.wait_ge(y_out, 4)
                for o in range(NC2):
                    for q in range(4):
                        pe.matmul(ps[:, (6 + 4 * o + q) % 8, :], A0("wz", o * P, P), ys[:, q * QUART:(q + 1) * QUART],
                                  start=True, stop=True).then_inc(z_done, 1)

                def all_max(k, ready):
                    pe.wait_ge(max_ready, ready)
                    pe.matmul(ps[0:1, 7, 0:P], gmax[k], F("ident"), start=True, stop=True).then_inc(max_row, 1)
                    pe.wait_ge(max_one, ready)
                    pe.matmul(ps[:, 7, 256:257], F("ones")[0:1, :], gone[k][0:1, :], start=True,
                              stop=True).then_inc(max_all, 1)

                pe.wait_ge(z_out, 8)
                all_max(0, 1)
                pe.wait_ge(wq_ready, 1)
                for q in range(4):
                    pe.wait_ge(parts_ready, q + 1)
                    k = 0
                    for part in (hi, lo):
                        for c in range(NC2):
                            o = c * TOK + q * QUART
                            mm = pe.matmul(ps[:, q, :], w1q[:, c, :], part[:, o:o + QUART], start=(k == 0), stop=(k == 3))
                            k += 1
                    mm.then_inc(conv_done, 1)
                all_max(1, 2)
                for k, (src, wgt) in enumerate(((hp1, dwq), (hp2, w2q))):
                    for q in range(4):
                        pe.wait_ge(parts_ready, 4 + 4 * k + q + 1)
                        for tap in range(9):
                            dy, dx = divmod(tap, 3)
                            mm = pe.matmul(ps[:, 4 * (1 - k) + q, :], wgt[:, tap, :],
                                           src[:, 2 * q:2 * q + 2, dy:dy + IMG, dx:dx + IMG],
                                           start=(tap == 0), stop=(tap == 8))
                        mm.then_inc(conv_done, 1)
                    all_max(2 + k, 3 + k)
                for q in range(4):
                    pe.wait_ge(parts_ready, 12 + q + 1)
                    for o in range(NC2):
                        n = 2 * q + o
                        pe.matmul(ps[:, (4 + n) % 8, :], w3q[:, o * P:(o + 1) * P], hq3[:, q * QUART:(q + 1) * QUART],
                                  start=True, stop=True).then_inc(conv_done, 1)
                for n in range(8):
                    pe.wait_ge(x2_ready, 2 * (n // 2) + 2)
                    for k in range(2):
                        t = 2 * n + k
                        for c in range(NC2):
                            mm = pe.transpose(ps[:, (4 + n) % 8, k * CH + c * P:k * CH + (c + 1) * P],
                                              x2[:, c, t * P:(t + 1) * P], F("ident"))
                    mm.then_inc(tok_done, 1)
                pe.wait_ge(tern_summed, 1)
                pe.wait_ge(tok_out_act, 1)
                pe.matmul(ps[:, 4, 0:1], F("ones"), tern_sum[:], start=True, stop=True).then_inc(tern_summed, 1)

            @block.scalar
            def _(act):
                act.wait_ge(w0_loaded, 16)
                for q in range(4):
                    act.wait_ge(theta_done, q + 1)
                    act.activation(th[:, q * QUART:(q + 1) * QUART], ps[:, q, :], ACT.Identity,
                                   bias=A0("theta_b")).then_inc(theta_out, 1)
                act.wait_ge(phi_done, 1)
                act.activation(ph[:, :], ps[:, 4, :], ACT.Identity, bias=A0("phi_b")).then_inc(phi_out, 1)
                act.wait_ge(w1_loaded, 16)
                act.activation(qsign[:], w1[:, 0:QUANT], ACT.Sign).then_inc(signs, 1)
                act.wait_ge(shifted, 1)
                act.activation(sc[:].rearrange("p n b m -> p (n b m)"), sc[:].rearrange("p n b m -> p (n b m)"), ACT.Exp,
                               scale=float(INTER) ** -0.5).then_inc(exped, 1)
                act.wait_ge(turned, 2)
                act.activation(at[:, 2:4, :].rearrange("p a n -> p (a n)"), ps[:, 1, :], ACT.Copy).then_inc(turned_out_act, 1)
                yb = ys[:, :].rearrange("p (h k r n) -> p h r k n", h=2, k=2, r=2)
                for hb in range(2):
                    act.wait_ge(y_done, hb + 1)
                    for par in range(2):
                        act.activation(yb[:, hb, par], ps[:, 2 + 2 * par + hb, :].rearrange("p (k n) -> p k n", k=2),
                                       ACT.Copy).then_inc(y_out, 1)
                for o in range(NC2):
                    for q in range(4):
                        act.wait_ge(z_done, 4 * o + q + 1)
                        act.activation(z[:, o, q * QUART:(q + 1) * QUART], ps[:, (6 + 4 * o + q) % 8, :], ACT.Identity,
                                       bias=A0("wz_b", o, 1)).then_inc(z_out, 1)
                act.wait_ge(z_affine, 1)
                for q in range(4):
                    for o in range(NC2):
                        sl = slice(q * QUART, (q + 1) * QUART)
                        act.wait_ge(x1_part, 2 * q + o + 1)
                        act.activation(x1[:, o, sl], x1[:, o, sl], ACT.Identity,
                                       bias=z_b[:, o:o + 1]).then_inc(x1_ready, 1)
                act.wait_ge(scale_ready, 1)
                for q in range(4):
                    sl = slice(q * QUART, (q + 1) * QUART)
                    act.activation(r256[:, :, sl], x1[:, :, sl], ACT.Copy, bias=ROUND_256, scale=isc[0]).then_inc(rounded, 1)
                    act.activation(r1[:, :, sl], x1[:, :, sl], ACT.Copy, bias=ROUND_1, scale=isc[0]).then_inc(rounded, 1)
                for k in range(1, 4):
                    act.wait_ge(scale_ready, k + 1)
                    for q in range(4):
                        sl = slice(q * QUART, (q + 1) * QUART)
                        src = ps[:, q, :] if k == 1 else h[:, sl]
                        act.activation(n256[:, sl], src, ACT.Copy, bias=ROUND_256, scale=fac[k]).then_inc(rounded, 1)
                        act.activation(n1[:, sl], src, ACT.Copy, bias=ROUND_1, scale=facn[k]).then_inc(rounded, 1)
                    if k < 3:
                        for q in range(4):
                            sl = slice(q * QUART, (q + 1) * QUART)
                            act.wait_ge(conv_done, 4 * k + q + 1)
                            act.activation(h[:, sl], ps[:, 4 * (2 - k) + q, :], ACT.Relu, bias=bnb[k - 1],
                                           scale=aff_a[k - 1]).then_inc(relu_out, 1)
                for q in range(4):
                    sl = slice(q * QUART, (q + 1) * QUART)
                    for o in range(NC2):
                        act.wait_ge(res_added, 2 * q + o + 1)
                        act.activation(x2[:, o, sl], pre[:, o, sl], ACT.Relu, bias=bnb[2][:, o:o + 1]).then_inc(x2_ready, 1)
                for n in range(0, 8, 2):
                    act.wait_ge(tok_done, n + 1)
                    act.activation(X[:, 2 * n:2 * n + 2, :].rearrange("p a n -> p (a n)"), ps[:, (4 + n) % 8, :],
                                   ACT.Copy).then_inc(tok_out_act, 1)

            @block.vector
            def _(dve):
                steps = [0]

                def settle(ins):
                    steps[0] += 1
                    ins.then_inc(dve_done, 1)
                    dve.wait_ge(dve_done, steps[0])

                for q in range(4):
                    dve.wait_ge(x_loaded[q], 32)
                    xq = xc[:, :, q * QUART:(q + 1) * QUART].rearrange("p c (n two) -> p c n two", two=2)
                    settle(dve.tensor_tensor(pool_w[:], xq[:, :, :, 0], xq[:, :, :, 1], ALU.max))
                    for c in range(NC2):
                        pw = pool_w[:, c, :].rearrange("p (g two w) -> p g two w", two=2, w=IMG // 2)
                        op = dve.tensor_tensor(
                            xp[:, c, q * P:(q + 1) * P].rearrange("p (g w) -> p g w", w=IMG // 2),
                            pw[:, :, 0, :], pw[:, :, 1, :], ALU.max)
                        if c == 0:
                            settle(op)
                        else:
                            op.then_inc(pooled, 1)
                    dve.wait_ge(pooled, q + 1)
                dve.wait_ge(w0_loaded, 16)
                dve.wait_ge(g_done, 1)
                dve.tensor_tensor(gt[:], ps[:, 5, :].rearrange("p (a n) -> p a n", a=4),
                                  A0("g_b").unsqueeze(1).broadcast_to([P, 4, INTER]), ALU.add).then_inc(g_out, 1)
                dve.wait_ge(scores_done, 2)
                s_ps = ps[:, 6:8, :].rearrange("p n (b m) -> p (n b) m", m=POOLED)
                sc3 = sc[:].rearrange("p n b m -> p (n b) m")
                wide = [P, 2 * BATCH, POOLED]
                settle(dve.tensor_reduce(sc_max[:], s_ps, AX.X, ALU.max))
                dve.tensor_tensor(sc3, s_ps, sc_max[:].unsqueeze(2).broadcast_to(wide), ALU.subtract).then_inc(shifted, 1)
                dve.wait_ge(w1_loaded, 16)
                settle(dve.tensor_scalar(qbits[:], w1[:, 0:QUANT], SQRT2, None, ALU.mult))
                settle(dve.tensor_scalar(qbits[:].bitcast(I32), qbits[:].bitcast(I32), 0x7F800000, None, ALU.bitwise_and))
                settle(dve.tensor_scalar(qbits[:], qbits[:], 2.0 ** -14, 1.0, ALU.max, ALU.min))
                dve.wait_ge(exped, 1)
                settle(dve.tensor_reduce(sc_sum[:], sc3, AX.X, ALU.add))
                settle(dve.reciprocal(sc_inv[:], sc_sum[:]))
                dve.tensor_tensor(sc3, sc3, sc_inv[:].unsqueeze(2).broadcast_to(wide), ALU.mult).then_inc(weights_ready, 1)
                dve.wait_ge(signs, 1)
                dve.wait_ge(fix_loaded, 16)

                def quantised(name, dst):
                    a_, n_ = W1[name]
                    m_, s_ = qbits[:, a_:a_ + n_], qsign[:, a_:a_ + n_]
                    return dve.tensor_tensor(dst, m_, s_, ALU.mult)

                quantised("w1", w1q[:].rearrange("p a n -> p (a n)"))
                quantised("w2", w2q[:].rearrange("p a n -> p (a n)"))
                quantised("w3", w3q[:])
                settle(quantised("peg", pegq[:]))
                for tap in range(9):
                    op = dve.tensor_scalar(dwq[:, tap, :], F("stack"), pegq[:, tap:tap + 1], None, ALU.mult)
                op.then_inc(wq_ready, 1)
                dve.wait_ge(turned, 1)
                dve.tensor_copy(at[:, 0:2, :].rearrange("p a n -> p (a n)"), ps[:, 0, :]).then_inc(turned_out_dve, 1)
                for k, v_ in enumerate(("v1", "v2", "v3")):
                    dve.tensor_scalar(inv_ve[k], A1(v_), EPS, None, ALU.add).then_inc(bn_ve, 1)
                dve.wait_ge(bn_pow, 3)
                for k in range(3):
                    op = dve.tensor_tensor(inv_g[k], inv_rs[k], A1(f"g{k + 1}"), ALU.mult)
                settle(op)
                for k in range(3):
                    op = dve.tensor_tensor(mi[k], inv_g[k], A1(f"m{k + 1}"), ALU.mult)
                settle(op)
                for k in range(3):
                    op = dve.tensor_tensor(bnb[k], A1(f"b{k + 1}"), mi[k], ALU.subtract)
                settle(op)
                settle(dve.tensor_tensor(pb1, inv_g[0], A1("peg_b"), ALU.mult))
                settle(dve.tensor_tensor(bnb[0], bnb[0], pb1, ALU.add))
                for o in range(NC2):
                    for q in range(4):
                        dve.wait_ge(z_out, 4 * o + q + 1)
                        op = dve.bn_stats(zst[:, o, q, :], z[:, o, q * QUART:(q + 1) * QUART])
                settle(op)
                for o in range(NC2):
                    op = dve.bn_aggr(zmv[:, o, :], zst[:, o].rearrange("p a n -> p (a n)"))
                settle(op)
                dve.tensor_scalar(z_ve, zmv[:, :, 1], EPS, None, ALU.add).then_inc(z_var, 1)
                dve.wait_ge(z_pow, 1)
                settle(dve.tensor_tensor(z_a, z_rstd, A0("gamma"), ALU.mult))
                settle(dve.tensor_tensor(z_t, z_a, zmv[:, :, 0], ALU.mult))
                dve.tensor_tensor(z_b, A0("beta"), z_t, ALU.subtract).then_inc(z_affine, 1)
                for q in range(4):
                    for o in range(NC2):
                        sl = slice(q * QUART, (q + 1) * QUART)
                        dve.scalar_tensor_tensor(x1[:, o, sl], z[:, o, sl], z_a[:, o:o + 1], xc[:, o, sl],
                                                 ALU.mult, ALU.add).then_inc(x1_part, 1)

                def scale_of(k, n, acc_scale=None):
                    dve.wait_ge(max_row, k + 1)
                    dve.tensor_reduce(gone[k][0:1, :], ps[0:1, 7, 0:P], AX.X, ALU.max).then_inc(max_one, 1)
                    dve.wait_ge(max_all, k + 1)
                    if acc_scale is not None:
                        settle(dve.tensor_tensor(scl[k], ps[:, 7, 256:257], acc_scale, ALU.mult))
                        settle(dve.tensor_scalar(scl[k], scl[k], MIN_ABS, 1.0 / QMAX, ALU.max, ALU.mult))
                    else:
                        settle(dve.tensor_scalar(scl[k], ps[:, 7, 256:257], MIN_ABS, 1.0 / QMAX, ALU.max, ALU.mult))
                    settle(dve.reciprocal(isc[k], scl[k]))
                    if k > 0:
                        if acc_scale is not None:
                            settle(dve.tensor_tensor(fac[k], isc[k], acc_scale, ALU.mult))
                        else:
                            settle(dve.tensor_copy(fac[k], isc[k]))
                        settle(dve.tensor_tensor(facn[k], fac[k], F("low_half"), ALU.mult))
                    if k in (1, 2):
                        settle(dve.tensor_tensor(aff_a[k - 1], inv_g[k - 1], scl[k], ALU.mult))
                    if k == 3:
                        settle(dve.tensor_scalar(aff_a[2], inv_g[2], scl[k], None, ALU.mult))

                for q in range(4):
                    dve.wait_ge(x1_ready, 2 * q + 2)
                    op = dve.tensor_reduce(maxes[0][:, q:q + 1], x1[:, :, q * QUART:(q + 1) * QUART], AX.XY, ALU.max,
                                           apply_absolute_value=True)
                settle(op)
                dve.tensor_reduce(gmax[0], maxes[0], AX.X, ALU.max).then_inc(max_ready, 1)
                scale_of(0, 1)
                dve.tensor_copy(fac[0], isc[0]).then_inc(scale_ready, 1)
                hi3 = hi.rearrange("p (c n) -> p c n", c=NC2)
                lo3 = lo.rearrange("p (c n) -> p c n", c=NC2)
                for q in range(4):
                    sl = slice(q * QUART, (q + 1) * QUART)
                    dve.wait_ge(rounded, 2 * q + 1)
                    settle(dve.tensor_scalar(hi3[:, :, sl], r256[:, :, sl], ROUND_256, None, ALU.subtract))
                    dve.wait_ge(rounded, 2 * q + 2)
                    dve.scalar_tensor_tensor(lo3[:, :, sl], r1[:, :, sl], ROUND_1, hi3[:, :, sl],
                                             ALU.subtract, ALU.subtract).then_inc(parts_ready, 1)
                dve.wait_ge(padded_zero, 2)
                for k in range(1, 4):
                    for q in range(4):
                        sl = slice(q * QUART, (q + 1) * QUART)
                        if k == 1:
                            dve.wait_ge(conv_done, q + 1)
                            op = dve.tensor_reduce(maxes[k][:, q:q + 1], ps[:, q, :], AX.X, ALU.max,
                                                   apply_absolute_value=True)
                        else:
                            dve.wait_ge(relu_out, 4 * (k - 2) + q + 1)
                            op = dve.tensor_reduce(maxes[k][:, q:q + 1], h[:, sl], AX.X, ALU.max,
                                                   apply_absolute_value=True)
                    settle(op)
                    dve.tensor_reduce(gmax[k], maxes[k], AX.X, ALU.max).then_inc(max_ready, 1)
                    scale_of(k, 1, scl[0] if k == 1 else None)
                    dve.tensor_copy(fac[0], fac[k]).then_inc(scale_ready, 1)
                    for q in range(4):
                        sl = slice(q * QUART, (q + 1) * QUART)
                        dve.wait_ge(rounded, 8 * k + 2 * q + 1)
                        settle(dve.tensor_scalar(n256[:, sl], n256[:, sl], F("half_sign"), F("half_shift"),
                                                 ALU.mult, ALU.add))
                        dve.wait_ge(rounded, 8 * k + 2 * q + 2)
                        if k == 3:
                            dve.tensor_tensor(hq3[:, sl], n1[:, sl], n256[:, sl], ALU.add).then_inc(parts_ready, 1)
                        else:
                            dst = (hp1 if k == 1 else hp2)[:, 2 * q:2 * q + 2, 1:1 + IMG, 1:1 + IMG]
                            shape = "p (b h w) -> p b h w"
                            dve.tensor_tensor(dst, n1[:, sl].rearrange(shape, b=2, h=IMG),
                                              n256[:, sl].rearrange(shape, b=2, h=IMG), ALU.add).then_inc(parts_ready, 1)
                for q in range(4):
                    sl = slice(q * QUART, (q + 1) * QUART)
                    for o in range(NC2):
                        n = 2 * q + o
                        dve.wait_ge(conv_done, 12 + n + 1)
                        dve.scalar_tensor_tensor(pre[:, o, sl], ps[:, (4 + n) % 8, :], aff_a[2][:, o:o + 1], x1[:, o, sl],
                                                 ALU.mult, ALU.add).then_inc(res_added, 1)
                for n in range(1, 8, 2):
                    dve.wait_ge(tok_done, n + 1)
                    dve.tensor_copy(X[:, 2 * n:2 * n + 2, :].rearrange("p a n -> p (a n)"), ps[:, (4 + n) % 8, :])\
                       .then_inc(tok_out_dve, 1)
                dve.wait_ge(wt_loaded, 16)
                dve.tensor_reduce(tern_sum[:], T("tern"), AX.X, ALU.add, apply_absolute_value=True)\
                   .then_inc(tern_summed, 1)
                dve.wait_ge(tern_summed, 2)
                tsc, tinv = gone[0], gone[1]
                settle(dve.tensor_scalar(tsc, ps[:, 4, 0:1], 1.0 / (CH * CH), EPS, ALU.mult, ALU.max))
                settle(dve.reciprocal(tinv, tsc))
                settle(dve.tensor_scalar(T("tern"), T("tern"), tinv, ROUND_1, ALU.mult, ALU.add))
                settle(dve.tensor_scalar(T("tern"), T("tern"), ROUND_1, -1.0, ALU.subtract, ALU.max))
                settle(dve.tensor_scalar(T("tern"), T("tern"), 1.0, tsc, ALU.min, ALU.mult))
                P1_STEPS[0] = steps[0]

        with ExitStack() as c2:
            def lb(name, shape, dt=F32):
                return sb(name, shape, dt, c2)

            xt = lb("xt", [P, 2, 2, CH])
            xb = lb("xb", [P, 2, 2, CH])
            xn = lb("xn", [P, 2, 2, CH])
            xnT = lb("xnT", [P, 2, NC2, PIX])
            stats = lb("stats", [P, 8, 2, 6])
            mv = lb("mv", [P, 8, 2, 2])
            ve = lb("ve", [P, 8, 2])
            rstd = lb("rstd", [P, 8, 2])
            bqs = lb("bqs", [P, 2, NC2])
            Qe = lb("Qe", [P, 2, 2, NC2, PIX])
            K = lb("K", [P, 2, NC2, PIX])
            V = lb("V", [P, 2, 2, HEADS, SLOT])
            nmax = lb("nmax", [P, 2 * UNITS, 4])
            Pr = lb("Pr", [P, 3, 512])
            PT = lb("PT", [P, 6, 512])
            OT = lb("OT", [P, 2, PIX])
            oinv = lb("oinv", [P, 2, 2, 4])
            attn = lb("attn", [P, 2, 2, CH])
            turn = lb("turn", [P, 2, NC2, PIX])
            lg = lb("lg", [P, 12, 2, EXPERTS])
            l1 = lb("l1", [P, 8, 2])
            gate = lb("gate", [P, 2, 2, EXPERTS])
            gateT = lb("gateT", [EXPERTS, 2, 2, P])
            acc = lb("acc", [P, 2, 2, CH])
            res = lb("res", [P, 2, NC2, PIX])

            bank_full = [sem(f"bank_full{b}") for b in range(8)]
            bank_drained = [sem(f"bank_drained{b}") for b in range(8)]
            part2_ready = sem("part2_ready")
            x_biased = sem("x_biased")
            var_ready = sem("var_ready")
            rstd_ready = sem("rstd_ready")
            xn_ready = sem("xn_ready")
            unit_max = sem("unit_max")
            router_shifted = sem("router_shifted")
            router_exp = sem("router_exp")
            gates_ready = sem("gates_ready")
            bias_in_acc = sem("bias_in_acc")
            acc_ready = sem("acc_ready")

            O_PER = 8 * 2 // 2

            block = c2.enter_context(nc.Block())

            def full(eng, job, i):
                b, n = PLAN[job]
                eng.wait_ge(bank_full[b], i * PER_BANK[b] + n + 1)

            def drained(eng, job, i):
                b, n = PLAN[job]
                eng.wait_ge(bank_drained[b], i * PER_BANK[b] + n + 2)

            def bank(job):
                return ps[:, PLAN[job][0], :]

            @block.sync
            def _(sp):
                with sp.Fori(0, PAIRS) as i:
                    for a in range(2):
                        drained(sp, ("FO", 3, a), i)
                        sp.dma_start(out[bass.ds(i * 2 + a, 1), :, :].rearrange("b (c p) n -> p (b c) n", p=P),
                                     res[:, a, :, :]).then_inc(stored, 16)
                sp.wait_ge(stored, 16 * BATCH + 16)

            @block.gpsimd
            def _(pool):
                pool.memset(V[:], 0.0).then_inc(part2_ready, 1)
                pool.wait_ge(part2_ready, 1)
                pool.memset(V[:].rearrange("p a t h s -> p (a t h) s")[:, :, DH:DH + 1], 1.0).then_inc(part2_ready, 1)
                with pool.Fori(0, PAIRS) as i:
                    for s in range(4):
                        for a in range(2):
                            if s == 0:
                                pool.tensor_tensor(xb[:, a], X[:, bass.ds(i * 4 + 2 * a, 2), :],
                                                   T("bo0").unsqueeze(1).broadcast_to([P, 2, CH]),
                                                   ALU.add).then_inc(x_biased, 1)
                            n = 2 * s + a
                            pool.wait_ge(var_ready, i * 8 + n + 1)
                            pool.tensor_tensor(rstd[:, n, :], ve[:, n, :], F("minus_half"), ALU.pow)\
                                .then_inc(rstd_ready, 1)

            @block.tensor
            def _(pe):
                pe.wait_ge(part2_ready, 2)
                for b in range(8):
                    pe.sem_inc(bank_drained[b], 1)
                with pe.Fori(0, PAIRS) as i:
                    def take(job):
                        b, n = PLAN[job]
                        pe.wait_ge(bank_drained[b], i * PER_BANK[b] + n + 1)
                        return ps[:, b, :]

                    def give(job, mm):
                        mm.then_inc(bank_full[PLAN[job][0]], 1)

                    def turn4(job, src):
                        d = take(job)
                        for c in range(NC2):
                            for t in range(2):
                                mm = pe.transpose(d[:, c * PIX + t * P:c * PIX + (t + 1) * P],
                                                  src[:, t, c * P:(c + 1) * P], F("ident"))
                        give(job, mm)

                    def rows(job, w, wstep, w_at, src, n_out=2):
                        d = take(job)
                        for o in range(n_out):
                            for c in range(NC2):
                                mm = pe.matmul(d[:, o * PIX:(o + 1) * PIX],
                                               w[:, c * wstep + w_at + o * P:c * wstep + w_at + (o + 1) * P],
                                               src[:, c, :], start=(c == 0), stop=(c == 1))
                        give(job, mm)

                    def toks(job, w, wstep, w_at, src, n=CH):
                        d = take(job)
                        for t in range(2):
                            for c in range(NC2):
                                mm = pe.matmul(d[:, t * n:(t + 1) * n], src[:, c, t * P:(t + 1) * P],
                                               w[:, c * wstep + w_at:c * wstep + w_at + n],
                                               start=(c == 0), stop=(c == 1))
                        give(job, mm)

                    def scores(s, t):
                        a, g, kind = t // UNITS, t % UNITS // 3, t % 3
                        d = take(("S", s, t))
                        rows_ = slice(32 * g, 32 * g + 32)
                        first = True
                        if s == 0:
                            k0 = (3 * g + kind) * 4 * P
                            pe.matmul(d, FB("pos", P * (kind > 0), P), FB("alibi", k0, 4 * P), start=True, stop=False,
                                      skip_group_check=True)
                            first = False
                        if kind == 0:
                            pe.matmul(d, FB("ident"), FB("tri0"), start=first, stop=False, skip_group_check=True)
                            for j in range(4):
                                mm = pe.matmul(d[:, j * P:(j + 1) * P], Qe[rows_, j % 2, a, j // 2, 0:P],
                                               K[rows_, a, j // 2, 0:P], start=False, stop=(j == 3), skip_group_check=True)
                        else:
                            pe.matmul(d.rearrange("p (j k n) -> p j k n", j=2, k=2)[:, :, 1, :], FB("ident"),
                                      FB("tri1").rearrange("p (j n) -> p j n", j=2), start=first, stop=False,
                                      skip_group_check=True)
                            for jj in range(2):
                                j = 2 * (kind - 1) + jj
                                mm = pe.matmul(d[:, jj * PIX:(jj + 1) * PIX], Qe[rows_, j % 2, a, j // 2, P:2 * P],
                                               K[rows_, a, j // 2, :], start=False, stop=(jj == 1), skip_group_check=True)
                        give(("S", s, t), mm)

                    def turn_probs(s, t):
                        d = take(("PT", s, t))
                        drained(pe, ("S", s, t), i)
                        for n in range(4):
                            mm = pe.transpose(d[:, n * P:(n + 1) * P], Pr[:, t % 3, n * P:(n + 1) * P], F("ident"))
                        give(("PT", s, t), mm)

                    def values0(s, t):
                        gg, a = t // 3, t // UNITS
                        b, n = 6 + gg % 2, (4 * (s // 2) + gg // 2)
                        drained(pe, ("PT", s, t), i)
                        pe.wait_ge(bank_drained[b], i * O_PER + n + 1)
                        for j in range(4):
                            pe.matmul(ps[32 * j:32 * j + 32, b, 0:P], V[:, a, 0, head(gg % 4, j), :],
                                      PT[:, t % 6, j * P:(j + 1) * P], start=True, stop=True)

                    def values1(s, t):
                        gg, a = t // 3, t // UNITS
                        b = 6 + gg % 2
                        drained(pe, ("PT", s, t - 1), i)
                        drained(pe, ("PT", s, t), i)
                        for kt in range(2):
                            for j in range(4):
                                seg = 2 * (j % 2) + kt
                                mm = pe.matmul(ps[32 * j:32 * j + 32, b, P:2 * P], V[:, a, kt, head(gg % 4, j), :],
                                               PT[:, (t - 1 + j // 2) % 6, seg * P:(seg + 1) * P],
                                               start=(kt == 0), stop=(kt == 1))
                        mm.then_inc(bank_full[b], 1)

                    def turn_out(s, gg):
                        d = take(("OX", s, gg))
                        b, n = 6 + gg % 2, (4 * (s // 2) + gg // 2)
                        pe.wait_ge(bank_drained[b], i * O_PER + n + 2)
                        for t in range(2):
                            mm = pe.transpose(d[:, t * P:(t + 1) * P], OT[:, gg % 2, t * P:(t + 1) * P], F("ident"))
                        give(("OX", s, gg), mm)

                    for s in range(4):
                        if s == 0:
                            pe.wait_ge(wt_loaded, 16)
                            pe.wait_ge(fixb_loaded, 16)
                        if s == 3:
                            pe.wait_ge(wm_loaded, 16)
                        for a in range(2):
                            pe.wait_ge(xn_ready, i * 8 + 2 * s + a + 1)
                            turn4(("T", s, a), xn[:, a])
                        if s in (0, 2):
                            w = T("in0" if s == 0 else "in1")
                            for a in range(2):
                                drained(pe, ("T", s, a), i)
                                rows(("Q", s, a), w, 3 * CH, 0, xnT[:, a])
                                rows(("K", s, a), w, 3 * CH, CH, xnT[:, a])
                                toks(("V", s, a), w, 3 * CH, 2 * CH, xnT[:, a])
                            for t in range(2 * UNITS + 6):
                                if t < 2 * UNITS:
                                    if t % UNITS == 0:
                                        for k in "QK":
                                            drained(pe, (k, s, t // UNITS), i)
                                    scores(s, t)
                                if 3 <= t < 2 * UNITS + 3:
                                    turn_probs(s, t - 3)
                                v = t - 4
                                if 0 <= v < 2 * UNITS and v % 3 == 0:
                                    if v % UNITS == 0:
                                        drained(pe, ("V", s, v // UNITS), i)
                                    values0(s, v)
                                if 0 <= v < 2 * UNITS and v % 3 == 2:
                                    values1(s, v)
                                if t >= 8 and (t - 8) % 3 == 0:
                                    turn_out(s, (t - 8) // 3)
                                w = T("out0" if s == 0 else "out1")
                                if t == 19:
                                    drained(pe, ("OX", s, 3), i)
                                    turn4(("AT", s, 0), attn[:, 0])
                                if t == 21:
                                    drained(pe, ("AT", s, 0), i)
                                    toks(("PR", s, 0), w, CH, 0, turn[:, 0])
                            drained(pe, ("OX", s, 7), i)
                            turn4(("AT", s, 1), attn[:, 1])
                            drained(pe, ("AT", s, 1), i)
                            toks(("PR", s, 1), w, CH, 0, turn[:, 1])
                        if s == 1:
                            for a in range(2):
                                drained(pe, ("T", s, a), i)
                                toks(("FF", s, a), T("tern"), CH, 0, xnT[:, a])
                        if s == 3:
                            for a in range(2):
                                drained(pe, ("T", s, a), i)
                                toks(("R", s, a), M("Wr"), EXPERTS, 0, xnT[:, a], EXPERTS)

                            def experts(a, n):
                                d = take(("E", s, a, n))
                                t, e = n // 4, n % 4
                                for c in range(NC2):
                                    o = c * EXPERTS * CH + e * 2 * CH
                                    mm = pe.matmul(d, xnT[:, a, c, t * P:(t + 1) * P], M("We", o, 2 * CH),
                                                   start=(c == 0), stop=(c == 1))
                                give(("E", s, a, n), mm)

                            for a in range(2):
                                for n in range(4):
                                    experts(a, n)
                                pe.wait_ge(gates_ready, i * 2 + a + 1)
                                d = take(("GT", s, a))
                                for t in range(2):
                                    mm = pe.transpose(d[0:EXPERTS, t * P:(t + 1) * P], gate[:, a, t, :], F("ident"))
                                give(("GT", s, a), mm)
                                drained(pe, ("GT", s, a), i)
                                d = take(("GB", s, a))
                                for t in range(2):
                                    mm = pe.matmul(d[:, t * CH:(t + 1) * CH], gateT[:, a, t, :], M("be")[0:EXPERTS, :],
                                                   start=True, stop=True)
                                give(("GB", s, a), mm)
                                for n in range(4, 8):
                                    experts(a, n)
                            for a in range(2):
                                pe.wait_ge(acc_ready, i * 2 + a + 1)
                                turn4(("CT", s, a), acc[:, a])
                                drained(pe, ("CT", s, a), i)
                                d = take(("FO", s, a))
                                for o in range(NC2):
                                    for c in range(NC2):
                                        pe.matmul(d[:, o * PIX:(o + 1) * PIX], M("Wo", c * CH + o * P, P),
                                                  turn[:, a, c, :], start=(c == 0), stop=False)
                                    for t in range(2):
                                        mm = pe.matmul(d[:, o * PIX + t * P:o * PIX + (t + 1) * P],
                                                       xt[:, a, t, o * P:(o + 1) * P], F("ident"), start=False,
                                                       stop=(t == 1))
                                give(("FO", s, a), mm)

            @block.scalar
            def _(act):
                act.sem_inc(stored, 16)
                with act.Fori(0, PAIRS) as i:
                    def copy_out(job, dst):
                        full(act, job, i)
                        act.activation(dst, bank(job), ACT.Copy).then_inc(bank_drained[PLAN[job][0]], 1)

                    for s in range(4):
                        for a in range(2):
                            copy_out(("T", s, a), xnT[:, a].rearrange("p c n -> p (c n)"))
                        if s in (0, 2):
                            for a in range(2):
                                job = ("Q", s, a)
                                full(act, job, i)
                                for par in range(2):
                                    for c in range(NC2):
                                        dst, src = Qe[:, par, a, c, :], bank(job)[:, c * PIX:(c + 1) * PIX]
                                        if s == 0:
                                            op = act.activation(dst, src, ACT.Identity, scale=F("parity", par, 1),
                                                                bias=bqs[:, par, c:c + 1])
                                        else:
                                            op = act.activation(dst, src, ACT.Copy, scale=F("parity", par, 1))
                                op.then_inc(bank_drained[PLAN[job][0]], 1)
                            for t in range(2 * UNITS + 8):
                                if t < 2 * UNITS:
                                    job = ("S", s, t)
                                    act.wait_ge(unit_max, i * 4 * UNITS + (s // 2) * 2 * UNITS + t + 1)
                                    if t >= 3:
                                        full(act, ("PT", s, t - 3), i)
                                    w_ = P if t % 3 == 0 else PIX
                                    for n in range(512 // w_):
                                        op = act.activation(Pr[:, t % 3, n * w_:(n + 1) * w_], bank(job)[:, n * w_:(n + 1) * w_],
                                                            ACT.Exp, bias=nmax[:, t, n:n + 1])
                                    op.then_inc(bank_drained[PLAN[job][0]], 1)
                                if t >= 6 and (t - 6) % 3 == 0 and (t - 6) // 3 < 8:
                                    gg = (t - 6) // 3
                                    b, n = 6 + gg % 2, 4 * (s // 2) + gg // 2
                                    act.wait_ge(bank_full[b], i * O_PER + n + 1)
                                    act.activation(OT[:, gg % 2, :], ps[:, b, 0:PIX], ACT.Copy).then_inc(bank_drained[b], 1)
                                if t == 20:
                                    copy_out(("AT", s, 0), turn[:, 0].rearrange("p c n -> p (c n)"))
                            copy_out(("AT", s, 1), turn[:, 1].rearrange("p c n -> p (c n)"))
                        if s == 3:
                            for a in range(2):
                                act.wait_ge(router_shifted, i * 2 + a + 1)
                                act.activation(lg[:, 6 * a + 5], lg[:, 6 * a + 1], ACT.Exp).then_inc(router_exp, 1)
                            for a in range(2):
                                job = ("GT", s, a)
                                full(act, job, i)
                                act.activation(gateT[:, a].rearrange("p t n -> p (t n)"), bank(job)[0:EXPERTS, 0:2 * P],
                                               ACT.Copy).then_inc(bank_drained[PLAN[job][0]], 1)
                                copy_out(("GB", s, a), acc[:, a].rearrange("p t n -> p (t n)"))
                            for a in range(2):
                                copy_out(("CT", s, a), turn[:, a].rearrange("p c n -> p (c n)"))
                                job = ("FO", s, a)
                                full(act, job, i)
                                act.wait_ge(stored, i * 32 + 16)
                                for o in range(NC2):
                                    op = act.activation(res[:, a, o, :], bank(job)[:, o * PIX:(o + 1) * PIX], ACT.Identity,
                                                        bias=M("bo", o, 1))
                                op.then_inc(bank_drained[PLAN[job][0]], 1)

            @block.vector
            def _(dve):
                steps = [P1_STEPS[0]]
                for par in range(2):
                    steps[0] += 1
                    dve.tensor_scalar(bqs[:, par, :], T("bq0"), F("parity", par, 1), None, ALU.mult).then_inc(dve_done, 1)
                dve.wait_ge(dve_done, steps[0])
                base = steps[0]
                with dve.Fori(0, PAIRS) as i:
                    local = [0]

                    def settle(ins):
                        local[0] += 1
                        ins.then_inc(dve_done, 1)
                        dve.wait_ge(dve_done, i * DVE_STEPS + (base + local[0]))

                    def normalise(s, a):
                        n = 2 * s + a
                        src = X[:, bass.ds(i * 4 + 2 * a, 2), :] if s == 0 else xt[:, a]
                        for t in range(2):
                            op = dve.bn_stats(stats[:, n, t, :], src[:, t, :])
                        settle(op)
                        dve.memset(ve[:, n, :], EPS)
                        for t in range(2):
                            op = dve.bn_aggr(mv[:, n, t, :], stats[:, n, t, :])
                        settle(op)
                        dve.tensor_tensor(ve[:, n, :], ve[:, n, :], mv[:, n, :, 1], ALU.add).then_inc(var_ready, 1)
                        dve.wait_ge(rstd_ready, i * 8 + n + 1)
                        for t in range(2):
                            op = dve.tensor_scalar(xn[:, a, t, :], src[:, t, :], mv[:, n, t, 0:1], rstd[:, n, t:t + 1],
                                                   ALU.subtract, ALU.mult)
                        op.then_inc(xn_ready, 1)

                    def add_to(job, a, old):
                        full(dve, job, i)
                        op = dve.tensor_tensor(xt[:, a].rearrange("p t n -> p (t n)"), bank(job),
                                               old.rearrange("p t n -> p (t n)"), ALU.add)
                        op.then_inc(bank_drained[PLAN[job][0]], 1)
                        dve.wait_ge(bank_drained[PLAN[job][0]], i * PER_BANK[PLAN[job][0]] + PLAN[job][1] + 2)

                    for s in range(4):
                        for a in range(2):
                            normalise(s, a)
                        if s in (0, 2):
                            for a in range(2):
                                job = ("K", s, a)
                                full(dve, job, i)
                                kk = K[:, a]
                                src = bank(job).rearrange("p (c n) -> p c n", c=NC2)
                                if s == 0:
                                    op = dve.tensor_tensor(kk, src, T("bk0").unsqueeze(2).broadcast_to([P, NC2, PIX]), ALU.add)
                                else:
                                    op = dve.tensor_copy(kk, src)
                                op.then_inc(bank_drained[PLAN[job][0]], 1)
                                job = ("V", s, a)
                                full(dve, job, i)
                                for t in range(2):
                                    dst = V[:, a, t, :, 0:DH]
                                    src = bank(job)[:, t * CH:(t + 1) * CH].rearrange("p (h d) -> p h d", d=DH)
                                    if s == 0:
                                        op = dve.tensor_tensor(dst, src, T("bv0").rearrange("p (h d) -> p h d", d=DH), ALU.add)
                                    else:
                                        op = dve.tensor_copy(dst, src)
                                op.then_inc(bank_drained[PLAN[job][0]], 1)
                            for t in range(2 * UNITS + 6):
                                if t < 2 * UNITS:
                                    job = ("S", s, t)
                                    full(dve, job, i)
                                    w_ = P if t % 3 == 0 else PIX
                                    dve.tensor_reduce(nmax[:, t, 0:512 // w_], bank(job).rearrange("p (j n) -> p j n", n=w_),
                                                      AX.X, ALU.max, negate=True).then_inc(unit_max, 1)
                                if 3 <= t < 2 * UNITS + 3:
                                    job = ("PT", s, t - 3)
                                    full(dve, job, i)
                                    if t - 3 >= 6:
                                        gg = (t - 9) // 3
                                        dve.wait_ge(bank_full[6 + gg % 2], i * O_PER + 4 * (s // 2) + gg // 2 + 1)
                                    dve.tensor_copy(PT[:, (t - 3) % 6, :], bank(job)).then_inc(bank_drained[PLAN[job][0]], 1)
                                if t >= 8 and (t - 8) % 3 == 0:
                                    gg = (t - 8) // 3
                                    a, g = gg // 4, gg % 4
                                    job = ("OX", s, gg)
                                    full(dve, job, i)
                                    o4 = bank(job)[:, 0:2 * P].rearrange("p (t j s) -> p t j s", t=2, j=4)
                                    settle(dve.reciprocal(oinv[:, gg % 2], o4[:, :, :, DH]))
                                    av = attn[:, a].rearrange("p t (c g r d) -> p t c g r d", c=2, g=4, r=2)
                                    for c in range(2):
                                        op = dve.tensor_tensor(
                                            av[:, :, c, g, :, :], o4[:, :, 2 * c:2 * c + 2, 0:DH],
                                            oinv[:, gg % 2, :, 2 * c:2 * c + 2].unsqueeze(3).broadcast_to([P, 2, 2, DH]),
                                            ALU.mult)
                                    op.then_inc(bank_drained[PLAN[job][0]], 1)
                                if t == 22:
                                    if s == 0:
                                        dve.wait_ge(x_biased, i * 2 + 1)
                                    add_to(("PR", s, 0), 0, xb[:, 0] if s == 0 else xt[:, 0])
                            if s == 0:
                                dve.wait_ge(x_biased, i * 2 + 2)
                            add_to(("PR", s, 1), 1, xb[:, 1] if s == 0 else xt[:, 1])
                        if s == 1:
                            for a in range(2):
                                add_to(("FF", s, a), a, xt[:, a])
                        if s == 3:
                            shape = [P, 2, EXPERTS]

                            def wide(v):
                                return v.unsqueeze(2).broadcast_to(shape)

                            def logits(a):
                                L, D = lg[:, 6 * a], lg[:, 6 * a + 1]
                                job = ("R", s, a)
                                full(dve, job, i)
                                op = dve.tensor_tensor(L, bank(job)[:, 0:2 * EXPERTS].rearrange("p (t e) -> p t e", t=2),
                                                       M("br").rearrange("p (t e) -> p t e", t=2), ALU.add)
                                op.then_inc(bank_drained[PLAN[job][0]], 1)
                                dve.wait_ge(bank_drained[PLAN[job][0]], i * PER_BANK[PLAN[job][0]] + PLAN[job][1] + 2)
                                settle(dve.tensor_reduce(l1[:, 4 * a, :], L, AX.X, ALU.max))
                                dve.tensor_tensor(D, L, wide(l1[:, 4 * a, :]), ALU.subtract).then_inc(router_shifted, 1)

                            def first_largest(D, C, m, one):
                                settle(dve.scalar_tensor_tensor(C, D, 0.0, F("tie").rearrange("p (t e) -> p t e", t=2),
                                                                ALU.is_equal, ALU.mult))
                                settle(dve.tensor_reduce(m, C, AX.X, ALU.max))
                                settle(dve.tensor_tensor(one, C, wide(m), ALU.is_equal))

                            def top2(a):
                                D, C, one, two, E = (lg[:, 6 * a + k] for k in (1, 2, 3, 4, 5))
                                m, su = l1[:, 4 * a + 1, :], l1[:, 4 * a + 2, :]
                                dve.wait_ge(router_shifted, i * 2 + a + 1)
                                first_largest(D, C, m, one)
                                dve.wait_ge(router_exp, i * 2 + a + 1)
                                D2 = lg[:, 6 * a]
                                settle(dve.scalar_tensor_tensor(D2, one, MASKED, D, ALU.mult, ALU.add))
                                settle(dve.tensor_reduce(m, D2, AX.X, ALU.max))
                                settle(dve.tensor_tensor(D2, D2, wide(m), ALU.subtract))
                                first_largest(D2, C, m, two)
                                settle(dve.tensor_tensor(one, one, two, ALU.add))
                                settle(dve.tensor_reduce(su, E, AX.X, ALU.add))
                                settle(dve.reciprocal(m, su))
                                settle(dve.tensor_tensor(one, one, E, ALU.mult))
                                dve.tensor_tensor(gate[:, a], one, wide(m), ALU.mult).then_inc(gates_ready, 1)
                                dve.wait_ge(gates_ready, i * 2 + a + 1)

                            for a in range(2):
                                logits(a)
                            for a in range(2):
                                top2(a)
                            for a in range(2):
                                drained(dve, ("GB", s, a), i)
                                for n in range(8):
                                    job = ("E", s, a, n)
                                    full(dve, job, i)
                                    t, e = n // 4, n % 4
                                    for k in range(2):
                                        op = dve.scalar_tensor_tensor(acc[:, a, t, :], bank(job)[:, k * CH:(k + 1) * CH],
                                                                      gate[:, a, t, 2 * e + k:2 * e + k + 1], acc[:, a, t, :],
                                                                      ALU.mult, ALU.add)
                                        if k == 0:
                                            settle(op)
                                    op.then_inc(bank_drained[PLAN[job][0]], 1)
                                    dve.wait_ge(bank_drained[PLAN[job][0]], i * PER_BANK[PLAN[job][0]] + PLAN[job][1] + 2)
                                dve.tensor_copy(l1[:, 3, 0:1], acc[:, a, 0, 0:1]).then_inc(acc_ready, 1)
                    assert local[0] == DVE_STEPS, local[0]


P1_STEPS = [0]
DVE_STEPS = 8 * 2 + 16 + 2 * (1 + 13) + 2 * 8




def bf16_bits(np, v):
    u = np.ascontiguousarray(v, np.float32).view(np.uint32)
    return ((u + 0x7FFF + (u >> 16 & 1)) >> 16).astype(np.uint16)


def _fixed(np):
    fix = np.zeros((P, FIX_N), np.float32)

    def put(name, v):
        a, n = FIX[name]
        fix[:, a:a + n] = v

    r = np.arange(P)
    put("ident", np.eye(P))
    put("ones", 1.0)
    lower = (r >= WID)[:, None]
    put("stack", (r[:, None] % WID) == (r[None, :] % WID))
    put("parity", np.stack([(r // DH % 2 == par) * DH ** -0.5 for par in range(2)], 1))
    put("tie", np.tile(EXPERTS - np.arange(EXPERTS), 2)[None, :])
    put("low_half", lower)
    put("half_sign", np.where(lower, -1.0, 1.0))
    put("half_shift", np.where(lower, 1.0, -1.0) * ROUND_256 - ROUND_1)
    put("minus_half", -0.5)

    fb = np.zeros((P, FIXB_N), np.float32)

    def putb(name, v):
        a, n = FIXB[name]
        fb[:v.shape[0], a:a + n] = v

    tri = np.where(r[None, :] <= r[:, None], 0.0, MASKED)
    putb("ident", np.eye(P))
    putb("tri0", np.tile(tri, (1, 4)))
    putb("tri1", np.tile(tri, (1, 2)))
    q = np.concatenate([r, r + P])
    putb("pos", np.concatenate([np.ones((3, 2 * P)), -np.tile(q, (3, 1))]))

    def parts(v):
        out, v = [], np.asarray(v, np.float32)
        for _ in range(3):
            h = (bf16_bits(np, v).astype(np.uint32) << 16).view(np.float32)
            out.append(h)
            v = v - h
        return np.stack(out)

    first = 2.0 ** -(2.0 ** -(np.log2(HEADS) - 3))
    slopes = np.asarray([first * first ** h for h in range(HEADS)], np.float32)
    units = []
    for g in range(GROUPS):
        for kind in range(3):
            heads = [head(g, j) for j in (range(4) if kind == 0 else range(2 * kind - 2, 2 * kind))]
            keys = np.arange(P if kind == 0 else PIX, dtype=np.float32)
            bias = np.concatenate([slopes[h] * keys for h in heads])
            sl = np.concatenate([np.full(len(keys), slopes[h]) for h in heads])
            units.append(np.concatenate([parts(bias), parts(sl)]))
    putb("alibi", np.concatenate(units, 1))
    return fix, bf16_bits(np, fb)


def kernel(**inputs):
    import numpy as np
    import concourse.bacc as _bacc
    from concourse import mybir as _mybir
    from concourse.bass_utils import run_bass_kernel_spmd as _run

    v = {k: np.asarray(a) for k, a in inputs.items()}
    f32 = np.float32

    def chunks(w):
        return w.reshape(-1, P, w.shape[1]).transpose(1, 0, 2).reshape(P, -1)

    def cols(vec):
        return vec.reshape(-1, P).T

    def twice(a):
        return np.concatenate([a, a], 0)

    def pack(layout, total, **parts):
        buf = np.zeros((P, total), f32)
        for name, a in parts.items():
            at, n = layout[name]
            buf[:, at:at + n] = a
        return buf

    w0 = pack(W0, W0_N, theta=chunks(v["L0_conv_theta_w"].T), phi=chunks(v["L0_conv_phi_w"].T),
              g=chunks(v["L0_conv_g_w"].T), wz=v["L0_conv_wz_w"].T, g_b=v["L0_conv_g_b"][None, :],
              theta_b=cols(v["L0_conv_theta_b"]), phi_b=cols(v["L0_conv_phi_b"]), wz_b=cols(v["L0_conv_wz_b"]),
              gamma=cols(v["L0_conv_bn_gamma"]), beta=cols(v["L0_conv_bn_beta"]))
    c1 = v["L1_conv_w1"].reshape(WID, CH).T
    c2 = v["L1_conv_w2"].transpose(1, 2, 3, 0).reshape(WID, 9, WID)
    inner = {}
    for k in (1, 2):
        for p in "gbmv":
            inner[f"{p}{k}"] = twice(v[f"L1_conv_bn{k}_{p}"][:, None])
    for p in "gbmv":
        inner[f"{p}3"] = cols(v[f"L1_conv_bn3_{p}"])
    w1 = pack(W1, W1_N, w1=chunks(np.concatenate([c1, c1], 1)),
              w2=twice(np.concatenate([c2, c2], 2).reshape(WID, -1)),
              w3=twice(v["L1_conv_w3"].reshape(CH, WID).T), peg=twice(v["L1_conv_peg_w"].reshape(WID, 9)),
              peg_b=twice(v["L1_conv_peg_b"][:, None]), **inner)
    b_in = v["L2_attn_b_in"]
    wt = pack(WT, WT_N, in0=chunks(v["L2_attn_w_in"]), out0=chunks(v["L2_attn_w_out"]),
              in1=chunks(np.concatenate([v[f"L3_attn_w_{p}"].T for p in "qkv"], 1)),
              out1=chunks(v["L3_attn_w_o"].T), tern=chunks(v["L2_ffn_weight"].T), bv0=b_in[None, 2 * CH:],
              bo0=v["L2_attn_b_out"][None, :], bq0=cols(b_in[:CH]), bk0=cols(b_in[CH:2 * CH]))
    be = np.zeros((P, CH), f32)
    be[:EXPERTS] = v["L3_ffn_be"]
    wm = pack(WM, WM_N, We=chunks(v["L3_ffn_We"].transpose(2, 0, 1).reshape(CH, EXPERTS * CH)),
              Wr=chunks(v["L3_ffn_Wr"].T), Wo=chunks(v["L3_ffn_Wo"].T), be=be, bo=cols(v["L3_ffn_bo"]),
              br=np.tile(v["L3_ffn_br"], 2)[None, :])
    fix, fixb = _fixed(np)
    arrays = {"x_dram": np.ascontiguousarray(v["x"].reshape(BATCH, CH, PIX)), "fix_dram": fix, "fixb_dram": fixb,
              "w0_dram": w0, "w1_dram": w1, "wt_dram": wt, "wm_dram": wm}

    nc = _bacc.Bacc("TRN2", target_bir_lowering=False, num_devices=1)
    args = [nc.dram_tensor(n, a.shape, _mybir.dt.from_np(a.dtype), kind="ExternalInput").ap() for n, a in arrays.items()]
    out = nc.dram_tensor("out_dram", (BATCH, CH, PIX), _mybir.dt.float32, kind="ExternalOutput").ap()
    build(nc, *args, out)
    r = _run(nc, [arrays], core_ids=[0])
    return r.results[0]["out_dram"].reshape(BATCH, CH, IMG, IMG)
```

```python
from contextlib import ExitStack

import concourse.bass as bass
from concourse import mybir

F32 = mybir.dt.float32
BF16 = mybir.dt.bfloat16
I32 = mybir.dt.int32
ALU = mybir.AluOpType
ACT = mybir.ActivationFunctionType
AX = mybir.AxisListType

P = 128
BATCH, CH, IMG = 8, 256, 16
PIX = IMG * IMG
TOK = BATCH * PIX
NC2 = CH // P
INTER = 128
POOLED = PIX // 4
QUART = TOK // 4
WID = 64
PAD = IMG + 2
HEADS, DH = 16, 16
GROUPS = 4
EXPERTS = 8
SLOT = 32

QMAX = 2.0 ** 15 - 1.0
MIN_ABS = 1e-12
ROUND_1 = 1.5 * 2.0 ** 23
ROUND_256 = 1.5 * 2.0 ** 31
SQRT2 = 1.4142135
EPS = 1e-5
MASKED = -1e30



def columns(*fields):
    at, out = 0, {}
    for name, width in fields:
        out[name] = (at, width)
        at += width
    return out, at


FIX, FIX_N = columns(("ident", P), ("ones", P), ("stack", P), ("tie", 2 * EXPERTS),
                     ("low_half", 1), ("half_sign", 1), ("half_shift", 1), ("minus_half", 2))
FIXB, FIXB_N = columns(("ident", P), ("tri0", 4 * P), ("tri1", 2 * P))
W0, W0_N = columns(("theta", NC2 * INTER), ("phi", NC2 * INTER), ("g", NC2 * INTER), ("wz", CH), ("g_b", INTER),
                   ("theta_b", 1), ("phi_b", 1), ("wz_b", NC2), ("gamma", NC2), ("beta", NC2))
W1, W1_N = columns(("w1", NC2 * P), ("w2", 9 * P), ("w3", CH), ("peg", 9), ("peg_b", 1),
                   ("g1", 1), ("b1", 1), ("m1", 1), ("v1", 1), ("g2", 1), ("b2", 1), ("m2", 1), ("v2", 1),
                   ("g3", 2), ("b3", 2), ("m3", 2), ("v3", 2))
QUANT = W1["peg_b"][0]
WT, WT_N = columns(("in0", NC2 * 3 * CH), ("out0", NC2 * CH), ("in1", NC2 * 3 * CH), ("out1", NC2 * CH),
                   ("tern", NC2 * CH), ("bv0", CH), ("bo0", CH), ("bq0", NC2), ("bk0", NC2))
WM, WM_N = columns(("We", NC2 * EXPERTS * CH), ("Wr", NC2 * EXPERTS), ("Wo", NC2 * CH), ("be", CH), ("bo", NC2),
                   ("br", 2 * EXPERTS))

UNITS = 3 * GROUPS
RING = 6
LEAD, TAIL = 1, 1
OUT_LEAD = 2
PR_RING, PT_RING = 4, 6
PT_BY_ACT = (1,)
Q_PARTS = (0, 0, 1, 1, 0, 2)
K_PARTS = (0, 1, 0, 1, 2, 0)
STACK = DH * len(Q_PARTS)
BIAS_ROWS = 6



def attention_slots(s):
    slots = []
    for t in range(UNITS):
        p = [("S", s, 0, t)]

        def late(kind, step, index):
            p.append((kind, s, 0 if step < UNITS else -1, index))

        u = (t - 3) % UNITS
        late("P", u + 3, u)
        v = (t - 4) % UNITS
        if v % 3 == 0:
            late("O0", v + 4, v // 3)
        if v % 3 == 2:
            late("O1", v + 4, v // 3)
        g, r = divmod((t - 8) % UNITS, 3)
        if r == 0:
            late("OX", 3 * g + 8, g)
        slots.append(p)
    return slots


def body(s):
    slots = attention_slots(s)

    def put(t, kind, stage, delta, index=0):
        slots[t].append((kind, stage, delta, index))

    put(0, "LNa", s, 1)
    put(1, "LNb", s, 1)
    if s == 0:
        put(1, "XB", s, 1)
    put(3, "T", s, 1)
    put(4, "Q", s, 1)
    put(5, "K", s, 1)
    put(5, "SPLIT", s, 1)
    put(6, "V", s, 1)
    put(6, "AT", s, -1)
    put(7, "PR", s, -1)
    put(7, "LNa", s + 1, -1)
    put(8, "LNb", s + 1, -1)
    if s == 0:
        put(10, "T", 1, -1)
        put(11, "FF", 1, -1)
    else:
        put(9, "T", 3, -1)
        put(10, "R", 3, -1)
        put(11, "RT", 3, -1)
        put(1, "GT", 3, -2)
        put(2, "GB", 3, -2)
        for n, t in enumerate((3, 4, 5, 6, 7, 8, 9, 9)):
            put(t, "E", 3, -2, n)
        put(10, "CT", 3, -2)
        put(11, "FO", 3, -2)
    return [p for t in slots for p in t]


def start(s):
    return [(k, st, 0, n) for k, st, d, n in body(s) if d == 1]


def finish(s):
    return [(k, st, BATCH - 1 + later + d, n) for later in (1, 2) for k, st, d, n in body(s) if d <= -later]


def in_turns(a, b):
    out = []
    for n in range(max(len(a), len(b))):
        out += a[n:n + 1] + b[n:n + 1]
    return out


JOBS = ("S", "P", "OX", "T", "Q", "K", "V", "AT", "PR", "FF", "R", "GT", "GB", "E", "CT", "FO")
SETTLED = {"LNa": 2, "OX": 1, "SPLIT": 1, "R": 1, "RT": 13, "E": 1}
TRANSFERS = ("parts_stored", "stack_loaded", "out_stored")


def signals(piece, bank):
    kind, n = piece[0], piece[3]
    out = []
    if kind in JOBS:
        out += [(f"bank_full{bank}", 1), (f"bank_drained{bank}", 1)]
    if kind == "O1":
        out += [(f"bank_full{6 + n % 2}", 1), (f"bank_drained{6 + n % 2}", 1)]
    if kind in SETTLED:
        out.append(("dve_step", SETTLED[kind]))
    out += {"LNa": [("var_ready", 1), ("rstd_ready", 1)], "LNb": [("xn_ready", 1)], "XB": [("x_biased", 1)],
            "S": [("unit_max", 1)], "FO": [("out_stored", 16)],
            "SPLIT": [("rest_ready", 1), ("part1_ready", 1), ("part2_ready", 1), ("parts_stored", 32),
                      ("stack_loaded", 16 * 2 * len(Q_PARTS))],
            "R": [("router_shifted", 1)], "RT": [("router_exp", 1), ("gates_ready", 1)]}.get(kind, [])
    return out


class Phase:

    def __init__(self, pieces, counts, bodies=0):
        self.pieces, self.base, self.bodies = pieces, dict(counts), bodies
        self.bank, self.after, self.per = {}, {}, {}
        jobs = 0
        for p in pieces:
            if p[0] in JOBS:
                self.bank[p] = jobs % RING
                jobs += 1
            for name, k in signals(p, self.bank.get(p)):
                self.per[name] = self.per.get(name, 0) + k
                self.after[p, name] = self.per[name]
        assert not bodies or jobs % RING == 0
        for name, k in self.per.items():
            counts[name] = counts.get(name, 0) + k * max(bodies, 1)


def phases():
    credit = {}
    for s in (0, 2):
        for name, k in Phase(body(s), {}).per.items():
            credit[name] = max(credit.get(name, 0), 2 * k)
    counts = dict(credit)
    return [Phase(start(0), counts),
            Phase(body(0), counts, BATCH),
            Phase(in_turns(start(2), finish(0)), counts),
            Phase(body(2), counts, BATCH),
            Phase(finish(2), counts)], credit, counts


class Spot:

    def __init__(self, phase, i=None, half=0):
        self.phase, self.i, self.half = phase, i, half

    def parity(self, batch):
        return (self.half + batch) % 2

    def tiles(self, batch):
        if self.i is None:
            return slice(2 * (batch + LEAD), 2 * (batch + LEAD) + 2)
        return bass.ds(self.i * 4 + 2 * (self.half + batch + LEAD), 2)

    def rows_out(self, batch):
        if self.i is None:
            return slice(batch + OUT_LEAD, batch + OUT_LEAD + 1)
        return bass.ds(self.i * 2 + (self.half + batch + OUT_LEAD), 1)

    def bank_of(self, piece):
        kind, stage, batch, n = piece
        for back in range(4):
            if (kind, stage, batch + back, n) in self.phase.bank:
                return self.phase.bank[kind, stage, batch + back, n]
        return None

    def count(self, name, piece, less=0):
        ph = self.phase
        kind, stage, batch, n = piece
        for back in range(1 if self.i is None else 4):
            key = (kind, stage, batch + back, n), name
            if key in ph.after:
                per = ph.per[name]
                const = ph.base.get(name, 0) + (self.half - back) * per + ph.after[key] - less
                if self.i is None:
                    return ph.base.get(name, 0) + ph.after[key] - less
                assert const >= 1, (name, piece)
                return self.i * (2 * per) + const
        if name in TRANSFERS:
            return ph.base[name]
        return None


def build(nc, x_in, fix_in, fixb_in, bias_in, w0_in, w1_in, wt_in, wm_in, parts_dram, out):
    ctx = ExitStack()
    with ctx:
        def sb(name, shape, dt=F32, c=ctx):
            return c.enter_context(nc.sbuf_tensor(name, shape, dt))

        def sem(name):
            return ctx.enter_context(nc.semaphore(name))

        ps = ctx.enter_context(nc.psum_tensor("ps", [P, 8, 512], F32))

        fix = sb("fix", [P, FIX_N])
        fixb = sb("fixb", [P, FIXB_N], BF16)
        wt = sb("wt", [P, WT_N])
        wm = sb("wm", [P, WM_N])
        X_all = sb("X", [P, 2 * (LEAD + BATCH + TAIL), CH])
        X = X_all[:, 2 * LEAD:2 * (LEAD + BATCH), :]

        def F(name, lo=0, n=None):
            at, w = FIX[name]
            return fix[:, at + lo:at + lo + (w - lo if n is None else n)]

        def FB(name, lo=0, n=None):
            at, w = FIXB[name]
            return fixb[:, at + lo:at + lo + (w - lo if n is None else n)]

        def T(name, lo=0, n=None):
            at, w = WT[name]
            return wt[:, at + lo:at + lo + (w - lo if n is None else n)]

        def M(name, lo=0, n=None):
            at, w = WM[name]
            return wm[:, at + lo:at + lo + (w - lo if n is None else n)]

        fix_loaded = sem("fix_loaded")
        fixb_loaded = sem("fixb_loaded")
        w0_loaded = sem("w0_loaded")
        w1_loaded = sem("w1_loaded")
        x_loaded = [sem(f"x_loaded{q}") for q in range(4)]
        wt_loaded = sem("wt_loaded")
        wm_loaded = sem("wm_loaded")
        dve_done = sem("dve_done")
        tern_summed = sem("tern_summed")

        with ExitStack() as c1:
            def eb(name, shape, dt=F32):
                return sb(name, shape, dt, c1)

            w0 = eb("w0", [P, W0_N])
            w1 = eb("w1", [P, W1_N])
            xc = eb("xc", [P, NC2, TOK])
            z = eb("z", [P, NC2, TOK])
            x1 = eb("x1", [P, NC2, TOK])
            th = eb("th", [P, TOK])
            ys = eb("ys", [P, TOK])
            pool_w = eb("pool_w", [P, NC2, QUART // 2])
            xp = eb("xp", [P, NC2, BATCH * POOLED])
            ph = eb("ph", [P, BATCH * POOLED])
            gt = eb("gt", [P, 4, INTER])
            sc = eb("sc", [P, 2, BATCH, POOLED])
            at = eb("at", [P, 4, PIX])
            sc_max = eb("sc_max", [P, 2 * BATCH])
            sc_sum = eb("sc_sum", [P, 2 * BATCH])
            sc_inv = eb("sc_inv", [P, 2 * BATCH])
            zst = eb("zst", [P, NC2, 4, 6])
            zmv = eb("zmv", [P, NC2, 2])
            small = eb("small", [P, 96])
            tern_sum = eb("tern_sum", [P, 1])
            qbits = eb("qbits", [P, QUANT])
            qsign = eb("qsign", [P, QUANT])
            w1q = eb("w1q", [P, NC2, P], BF16)
            w2q = eb("w2q", [P, 9, P], BF16)
            w3q = eb("w3q", [P, CH], BF16)
            pegq = eb("pegq", [P, 9])
            dwq = eb("dwq", [P, 9, P], BF16)
            hp1 = eb("hp1", [P, BATCH, PAD, PAD], BF16)
            hp2 = eb("hp2", [P, BATCH, PAD, PAD], BF16)
            hq3 = eb("hq3", [P, TOK], BF16)

            hi = ys[:, :].bitcast(BF16)
            lo = th[:, :].bitcast(BF16)
            r1 = z
            r256 = xc
            n1 = z[:, 0, :]
            n256 = z[:, 1, :]
            h = xc[:, 0, :]
            pre = xc
            x2 = z

            def A0(name, lo_=0, n=None):
                a_, w_ = W0[name]
                return w0[:, a_ + lo_:a_ + lo_ + (w_ - lo_ if n is None else n)]

            def A1(name, lo_=0, n=None):
                a_, w_ = W1[name]
                return w1[:, a_ + lo_:a_ + lo_ + (w_ - lo_ if n is None else n)]

            cols = iter(range(96))

            def col(n=1):
                c = [next(cols) for _ in range(n)]
                return small[:, c[0]:c[0] + n]

            z_ve, z_rstd, z_a, z_b = col(2), col(2), col(2), col(2)
            z_t = col(2)
            inv_ve = [col(1), col(1), col(2)]
            inv_rs = [col(1), col(1), col(2)]
            inv_g = [col(1), col(1), col(2)]
            mi = [col(1), col(1), col(2)]
            bnb = [col(1), col(1), col(2)]
            pb1 = col(1)
            aff_a = [col(1), col(1), col(2)]
            maxes = [col(4) for _ in range(4)]
            gmax = [col(1) for _ in range(4)]
            gone = [col(1) for _ in range(4)]
            scl = [col(1) for _ in range(4)]
            isc = [col(1) for _ in range(4)]
            fac = [col(1) for _ in range(4)]
            facn = col(1), col(1), col(1), col(1)

            theta_done = sem("theta_done")
            theta_out = sem("theta_out")
            pooled = sem("pooled")
            phi_done = sem("phi_done")
            phi_out = sem("phi_out")
            g_done = sem("g_done")
            g_out = sem("g_out")
            scores_done = sem("scores_done")
            shifted = sem("shifted")
            exped = sem("exped")
            weights_ready = sem("weights_ready")
            turned = sem("turned")
            turned_out_dve = sem("turned_out_dve")
            turned_out_act = sem("turned_out_act")
            y_done = sem("y_done")
            y_out = sem("y_out")
            z_done = sem("z_done")
            z_out = sem("z_out")
            z_var = sem("z_var")
            z_pow = sem("z_pow")
            z_affine = sem("z_affine")
            x1_part = sem("x1_part")
            x1_ready = sem("x1_ready")
            signs = sem("signs")
            wq_ready = sem("wq_ready")
            padded_zero = sem("padded_zero")
            bn_ve = sem("bn_ve")
            bn_pow = sem("bn_pow")
            max_ready = sem("max_ready")
            max_row = sem("max_row")
            max_one = sem("max_one")
            max_all = sem("max_all")
            scale_ready = sem("scale_ready")
            rounded = sem("rounded")
            parts_ready = sem("parts_ready")
            conv_done = sem("conv_done")
            relu_out = sem("relu_out")
            res_added = sem("res_added")
            x2_ready = sem("x2_ready")
            tok_done = sem("tok_done")
            tok_out_dve = sem("tok_out_dve")
            tok_out_act = sem("tok_out_act")

            block = c1.enter_context(nc.Block())

            @block.sync
            def _(sp):
                sp.dma_start(w0[:], w0_in).then_inc(w0_loaded, 16)
                for q in range(4):
                    for c in range(NC2):
                        sp.dma_start(
                            xc[:, c, q * QUART:(q + 1) * QUART].rearrange("p (b n) -> p b n", b=2),
                            x_in[2 * q:2 * q + 2, c * P:(c + 1) * P, :].rearrange("b p n -> p b n"),
                        ).then_inc(x_loaded[q], 16)
                sp.dma_start(fix[:], fix_in).then_inc(fix_loaded, 16)
                sp.dma_start(w1[:], w1_in).then_inc(w1_loaded, 16)
                sp.dma_start(fixb[:], fixb_in.bitcast(BF16)).then_inc(fixb_loaded, 16)
                sp.dma_start(wt[:], wt_in).then_inc(wt_loaded, 16)
                sp.dma_start(wm[:], wm_in).then_inc(wm_loaded, 16)

            @block.gpsimd
            def _(pool):
                pool.memset(hp1[:], 0.0).then_inc(padded_zero, 1)
                pool.memset(hp2[:], 0.0).then_inc(padded_zero, 1)
                pool.wait_ge(fix_loaded, 16)
                pool.wait_ge(bn_ve, 3)
                for k in range(3):
                    pool.tensor_tensor(inv_rs[k], inv_ve[k], F("minus_half", 0, 2 if k == 2 else 1),
                                       ALU.pow).then_inc(bn_pow, 1)
                pool.wait_ge(z_var, 1)
                pool.tensor_tensor(z_rstd, z_ve, F("minus_half"), ALU.pow).then_inc(z_pow, 1)

            @block.tensor
            def _(pe):
                pe.wait_ge(w0_loaded, 16)
                for q in range(4):
                    pe.wait_ge(x_loaded[q], 32)
                    for c in range(NC2):
                        mm = pe.matmul(ps[:, q, :], A0("theta", c * P, P), xc[:, c, q * QUART:(q + 1) * QUART],
                                       start=(c == 0), stop=(c == 1))
                    mm.then_inc(theta_done, 1)
                pe.wait_ge(pooled, 4)
                for c in range(NC2):
                    mm = pe.matmul(ps[:, 4, :], A0("phi", c * P, P), xp[:, c, :], start=(c == 0), stop=(c == 1))
                mm.then_inc(phi_done, 1)
                for q in range(4):
                    for c in range(NC2):
                        mm = pe.matmul(ps[:, 5, q * P:(q + 1) * P], xp[:, c, q * P:(q + 1) * P], A0("g", c * P, P),
                                       start=(c == 0), stop=(c == 1))
                mm.then_inc(g_done, 1)
                pe.wait_ge(theta_out, 4)
                pe.wait_ge(phi_out, 1)
                for n in range(2):
                    for b in range(BATCH):
                        mm = pe.matmul(ps[:, 6 + n, b * POOLED:(b + 1) * POOLED],
                                       th[:, b * PIX + n * P:b * PIX + (n + 1) * P],
                                       ph[:, b * POOLED:(b + 1) * POOLED], start=True, stop=True)
                    mm.then_inc(scores_done, 1)
                pe.wait_ge(weights_ready, 1)
                pe.wait_ge(fix_loaded, 16)
                for p in range(4):
                    for n in range(2):
                        mm = pe.transpose(ps[:, p // 2, (p % 2) * PIX + n * P:(p % 2) * PIX + (n + 1) * P],
                                          sc[:, n, 2 * p:2 * p + 2, :].rearrange("p b m -> p (b m)"), F("ident"))
                    if p % 2:
                        mm.then_inc(turned, 1)
                pe.wait_ge(g_out, 1)
                for hb in range(2):
                    pe.wait_ge(turned_out_act if hb else turned_out_dve, 1)
                    for k in range(2):
                        p = 2 * hb + k
                        for par in range(2):
                            r = par * POOLED
                            mm = pe.matmul(ps[:, 2 + 2 * par + hb, k * PIX:(k + 1) * PIX],
                                           gt[r:r + POOLED, p, :], at[r:r + POOLED, p, :], start=True, stop=True)
                    mm.then_inc(y_done, 1)
                pe.wait_ge(y_out, 4)
                for o in range(NC2):
                    for q in range(4):
                        pe.matmul(ps[:, (6 + 4 * o + q) % 8, :], A0("wz", o * P, P), ys[:, q * QUART:(q + 1) * QUART],
                                  start=True, stop=True).then_inc(z_done, 1)

                def all_max(k, ready):
                    pe.wait_ge(max_ready, ready)
                    pe.matmul(ps[0:1, 7, 0:P], gmax[k], F("ident"), start=True, stop=True).then_inc(max_row, 1)
                    pe.wait_ge(max_one, ready)
                    pe.matmul(ps[:, 7, 256:257], F("ones")[0:1, :], gone[k][0:1, :], start=True,
                              stop=True).then_inc(max_all, 1)

                pe.wait_ge(z_out, 8)
                all_max(0, 1)
                pe.wait_ge(wq_ready, 1)
                for q in range(4):
                    pe.wait_ge(parts_ready, q + 1)
                    k = 0
                    for part in (hi, lo):
                        for c in range(NC2):
                            o = c * TOK + q * QUART
                            mm = pe.matmul(ps[:, q, :], w1q[:, c, :], part[:, o:o + QUART], start=(k == 0), stop=(k == 3))
                            k += 1
                    mm.then_inc(conv_done, 1)
                all_max(1, 2)
                for k, (src, wgt) in enumerate(((hp1, dwq), (hp2, w2q))):
                    for q in range(4):
                        pe.wait_ge(parts_ready, 4 + 4 * k + q + 1)
                        for tap in range(9):
                            dy, dx = divmod(tap, 3)
                            mm = pe.matmul(ps[:, 4 * (1 - k) + q, :], wgt[:, tap, :],
                                           src[:, 2 * q:2 * q + 2, dy:dy + IMG, dx:dx + IMG],
                                           start=(tap == 0), stop=(tap == 8))
                        mm.then_inc(conv_done, 1)
                    all_max(2 + k, 3 + k)
                for q in range(4):
                    pe.wait_ge(parts_ready, 12 + q + 1)
                    for o in range(NC2):
                        n = 2 * q + o
                        pe.matmul(ps[:, (4 + n) % 8, :], w3q[:, o * P:(o + 1) * P], hq3[:, q * QUART:(q + 1) * QUART],
                                  start=True, stop=True).then_inc(conv_done, 1)
                for n in range(8):
                    pe.wait_ge(x2_ready, 2 * (n // 2) + 2)
                    for k in range(2):
                        t = 2 * n + k
                        for c in range(NC2):
                            mm = pe.transpose(ps[:, (4 + n) % 8, k * CH + c * P:k * CH + (c + 1) * P],
                                              x2[:, c, t * P:(t + 1) * P], F("ident"))
                    mm.then_inc(tok_done, 1)
                pe.wait_ge(tern_summed, 1)
                pe.wait_ge(tok_out_act, 1)
                pe.matmul(ps[:, 4, 0:1], F("ones"), tern_sum[:], start=True, stop=True).then_inc(tern_summed, 1)

            @block.scalar
            def _(act):
                act.wait_ge(w0_loaded, 16)
                for q in range(4):
                    act.wait_ge(theta_done, q + 1)
                    act.activation(th[:, q * QUART:(q + 1) * QUART], ps[:, q, :], ACT.Identity,
                                   bias=A0("theta_b")).then_inc(theta_out, 1)
                act.wait_ge(phi_done, 1)
                act.activation(ph[:, :], ps[:, 4, :], ACT.Identity, bias=A0("phi_b")).then_inc(phi_out, 1)
                act.wait_ge(w1_loaded, 16)
                act.activation(qsign[:], w1[:, 0:QUANT], ACT.Sign).then_inc(signs, 1)
                act.wait_ge(shifted, 1)
                act.activation(sc[:].rearrange("p n b m -> p (n b m)"), sc[:].rearrange("p n b m -> p (n b m)"), ACT.Exp,
                               scale=float(INTER) ** -0.5).then_inc(exped, 1)
                act.wait_ge(turned, 2)
                act.activation(at[:, 2:4, :].rearrange("p a n -> p (a n)"), ps[:, 1, :], ACT.Copy).then_inc(turned_out_act, 1)
                yb = ys[:, :].rearrange("p (h k r n) -> p h r k n", h=2, k=2, r=2)
                for hb in range(2):
                    act.wait_ge(y_done, hb + 1)
                    for par in range(2):
                        act.activation(yb[:, hb, par], ps[:, 2 + 2 * par + hb, :].rearrange("p (k n) -> p k n", k=2),
                                       ACT.Copy).then_inc(y_out, 1)
                for o in range(NC2):
                    for q in range(4):
                        act.wait_ge(z_done, 4 * o + q + 1)
                        act.activation(z[:, o, q * QUART:(q + 1) * QUART], ps[:, (6 + 4 * o + q) % 8, :], ACT.Identity,
                                       bias=A0("wz_b", o, 1)).then_inc(z_out, 1)
                act.wait_ge(z_affine, 1)
                for q in range(4):
                    for o in range(NC2):
                        sl = slice(q * QUART, (q + 1) * QUART)
                        act.wait_ge(x1_part, 2 * q + o + 1)
                        act.activation(x1[:, o, sl], x1[:, o, sl], ACT.Identity,
                                       bias=z_b[:, o:o + 1]).then_inc(x1_ready, 1)
                act.wait_ge(scale_ready, 1)
                for q in range(4):
                    sl = slice(q * QUART, (q + 1) * QUART)
                    act.activation(r256[:, :, sl], x1[:, :, sl], ACT.Copy, bias=ROUND_256, scale=isc[0]).then_inc(rounded, 1)
                    act.activation(r1[:, :, sl], x1[:, :, sl], ACT.Copy, bias=ROUND_1, scale=isc[0]).then_inc(rounded, 1)
                for k in range(1, 4):
                    act.wait_ge(scale_ready, k + 1)
                    for q in range(4):
                        sl = slice(q * QUART, (q + 1) * QUART)
                        src = ps[:, q, :] if k == 1 else h[:, sl]
                        act.activation(n256[:, sl], src, ACT.Copy, bias=ROUND_256, scale=fac[k]).then_inc(rounded, 1)
                        act.activation(n1[:, sl], src, ACT.Copy, bias=ROUND_1, scale=facn[k]).then_inc(rounded, 1)
                    if k < 3:
                        for q in range(4):
                            sl = slice(q * QUART, (q + 1) * QUART)
                            act.wait_ge(conv_done, 4 * k + q + 1)
                            act.activation(h[:, sl], ps[:, 4 * (2 - k) + q, :], ACT.Relu, bias=bnb[k - 1],
                                           scale=aff_a[k - 1]).then_inc(relu_out, 1)
                for q in range(4):
                    sl = slice(q * QUART, (q + 1) * QUART)
                    for o in range(NC2):
                        act.wait_ge(res_added, 2 * q + o + 1)
                        act.activation(x2[:, o, sl], pre[:, o, sl], ACT.Relu, bias=bnb[2][:, o:o + 1]).then_inc(x2_ready, 1)
                for n in range(0, 8, 2):
                    act.wait_ge(tok_done, n + 1)
                    act.activation(X[:, 2 * n:2 * n + 2, :].rearrange("p a n -> p (a n)"), ps[:, (4 + n) % 8, :],
                                   ACT.Copy).then_inc(tok_out_act, 1)

            @block.vector
            def _(dve):
                steps = [0]

                def settle(ins):
                    steps[0] += 1
                    ins.then_inc(dve_done, 1)
                    dve.wait_ge(dve_done, steps[0])

                for q in range(4):
                    dve.wait_ge(x_loaded[q], 32)
                    xq = xc[:, :, q * QUART:(q + 1) * QUART].rearrange("p c (n two) -> p c n two", two=2)
                    settle(dve.tensor_tensor(pool_w[:], xq[:, :, :, 0], xq[:, :, :, 1], ALU.max))
                    for c in range(NC2):
                        pw = pool_w[:, c, :].rearrange("p (g two w) -> p g two w", two=2, w=IMG // 2)
                        op = dve.tensor_tensor(
                            xp[:, c, q * P:(q + 1) * P].rearrange("p (g w) -> p g w", w=IMG // 2),
                            pw[:, :, 0, :], pw[:, :, 1, :], ALU.max)
                        if c == 0:
                            settle(op)
                        else:
                            op.then_inc(pooled, 1)
                    dve.wait_ge(pooled, q + 1)
                dve.wait_ge(w0_loaded, 16)
                dve.wait_ge(g_done, 1)
                dve.tensor_tensor(gt[:], ps[:, 5, :].rearrange("p (a n) -> p a n", a=4),
                                  A0("g_b").unsqueeze(1).broadcast_to([P, 4, INTER]), ALU.add).then_inc(g_out, 1)
                dve.wait_ge(scores_done, 2)
                s_ps = ps[:, 6:8, :].rearrange("p n (b m) -> p (n b) m", m=POOLED)
                sc3 = sc[:].rearrange("p n b m -> p (n b) m")
                wide = [P, 2 * BATCH, POOLED]
                settle(dve.tensor_reduce(sc_max[:], s_ps, AX.X, ALU.max))
                dve.tensor_tensor(sc3, s_ps, sc_max[:].unsqueeze(2).broadcast_to(wide), ALU.subtract).then_inc(shifted, 1)
                dve.wait_ge(w1_loaded, 16)
                settle(dve.tensor_scalar(qbits[:], w1[:, 0:QUANT], SQRT2, None, ALU.mult))
                settle(dve.tensor_scalar(qbits[:].bitcast(I32), qbits[:].bitcast(I32), 0x7F800000, None, ALU.bitwise_and))
                settle(dve.tensor_scalar(qbits[:], qbits[:], 2.0 ** -14, 1.0, ALU.max, ALU.min))
                dve.wait_ge(exped, 1)
                settle(dve.tensor_reduce(sc_sum[:], sc3, AX.X, ALU.add))
                settle(dve.reciprocal(sc_inv[:], sc_sum[:]))
                dve.tensor_tensor(sc3, sc3, sc_inv[:].unsqueeze(2).broadcast_to(wide), ALU.mult).then_inc(weights_ready, 1)
                dve.wait_ge(signs, 1)
                dve.wait_ge(fix_loaded, 16)

                def quantised(name, dst):
                    a_, n_ = W1[name]
                    m_, s_ = qbits[:, a_:a_ + n_], qsign[:, a_:a_ + n_]
                    return dve.tensor_tensor(dst, m_, s_, ALU.mult)

                quantised("w1", w1q[:].rearrange("p a n -> p (a n)"))
                quantised("w2", w2q[:].rearrange("p a n -> p (a n)"))
                quantised("w3", w3q[:])
                settle(quantised("peg", pegq[:]))
                for tap in range(9):
                    op = dve.tensor_scalar(dwq[:, tap, :], F("stack"), pegq[:, tap:tap + 1], None, ALU.mult)
                op.then_inc(wq_ready, 1)
                dve.wait_ge(turned, 1)
                dve.tensor_copy(at[:, 0:2, :].rearrange("p a n -> p (a n)"), ps[:, 0, :]).then_inc(turned_out_dve, 1)
                for k, v_ in enumerate(("v1", "v2", "v3")):
                    dve.tensor_scalar(inv_ve[k], A1(v_), EPS, None, ALU.add).then_inc(bn_ve, 1)
                dve.wait_ge(bn_pow, 3)
                for k in range(3):
                    op = dve.tensor_tensor(inv_g[k], inv_rs[k], A1(f"g{k + 1}"), ALU.mult)
                settle(op)
                for k in range(3):
                    op = dve.tensor_tensor(mi[k], inv_g[k], A1(f"m{k + 1}"), ALU.mult)
                settle(op)
                for k in range(3):
                    op = dve.tensor_tensor(bnb[k], A1(f"b{k + 1}"), mi[k], ALU.subtract)
                settle(op)
                settle(dve.tensor_tensor(pb1, inv_g[0], A1("peg_b"), ALU.mult))
                settle(dve.tensor_tensor(bnb[0], bnb[0], pb1, ALU.add))
                for o in range(NC2):
                    for q in range(4):
                        dve.wait_ge(z_out, 4 * o + q + 1)
                        op = dve.bn_stats(zst[:, o, q, :], z[:, o, q * QUART:(q + 1) * QUART])
                settle(op)
                for o in range(NC2):
                    op = dve.bn_aggr(zmv[:, o, :], zst[:, o].rearrange("p a n -> p (a n)"))
                settle(op)
                dve.tensor_scalar(z_ve, zmv[:, :, 1], EPS, None, ALU.add).then_inc(z_var, 1)
                dve.wait_ge(z_pow, 1)
                settle(dve.tensor_tensor(z_a, z_rstd, A0("gamma"), ALU.mult))
                settle(dve.tensor_tensor(z_t, z_a, zmv[:, :, 0], ALU.mult))
                dve.tensor_tensor(z_b, A0("beta"), z_t, ALU.subtract).then_inc(z_affine, 1)
                for q in range(4):
                    for o in range(NC2):
                        sl = slice(q * QUART, (q + 1) * QUART)
                        dve.scalar_tensor_tensor(x1[:, o, sl], z[:, o, sl], z_a[:, o:o + 1], xc[:, o, sl],
                                                 ALU.mult, ALU.add).then_inc(x1_part, 1)

                def scale_of(k, n, acc_scale=None):
                    dve.wait_ge(max_row, k + 1)
                    dve.tensor_reduce(gone[k][0:1, :], ps[0:1, 7, 0:P], AX.X, ALU.max).then_inc(max_one, 1)
                    dve.wait_ge(max_all, k + 1)
                    if acc_scale is not None:
                        settle(dve.tensor_tensor(scl[k], ps[:, 7, 256:257], acc_scale, ALU.mult))
                        settle(dve.tensor_scalar(scl[k], scl[k], MIN_ABS, 1.0 / QMAX, ALU.max, ALU.mult))
                    else:
                        settle(dve.tensor_scalar(scl[k], ps[:, 7, 256:257], MIN_ABS, 1.0 / QMAX, ALU.max, ALU.mult))
                    settle(dve.reciprocal(isc[k], scl[k]))
                    if k > 0:
                        if acc_scale is not None:
                            settle(dve.tensor_tensor(fac[k], isc[k], acc_scale, ALU.mult))
                        else:
                            settle(dve.tensor_copy(fac[k], isc[k]))
                        settle(dve.tensor_tensor(facn[k], fac[k], F("low_half"), ALU.mult))
                    if k in (1, 2):
                        settle(dve.tensor_tensor(aff_a[k - 1], inv_g[k - 1], scl[k], ALU.mult))
                    if k == 3:
                        settle(dve.tensor_scalar(aff_a[2], inv_g[2], scl[k], None, ALU.mult))

                for q in range(4):
                    dve.wait_ge(x1_ready, 2 * q + 2)
                    op = dve.tensor_reduce(maxes[0][:, q:q + 1], x1[:, :, q * QUART:(q + 1) * QUART], AX.XY, ALU.max,
                                           apply_absolute_value=True)
                settle(op)
                dve.tensor_reduce(gmax[0], maxes[0], AX.X, ALU.max).then_inc(max_ready, 1)
                scale_of(0, 1)
                dve.tensor_copy(fac[0], isc[0]).then_inc(scale_ready, 1)
                hi3 = hi.rearrange("p (c n) -> p c n", c=NC2)
                lo3 = lo.rearrange("p (c n) -> p c n", c=NC2)
                for q in range(4):
                    sl = slice(q * QUART, (q + 1) * QUART)
                    dve.wait_ge(rounded, 2 * q + 1)
                    settle(dve.tensor_scalar(hi3[:, :, sl], r256[:, :, sl], ROUND_256, None, ALU.subtract))
                    dve.wait_ge(rounded, 2 * q + 2)
                    dve.scalar_tensor_tensor(lo3[:, :, sl], r1[:, :, sl], ROUND_1, hi3[:, :, sl],
                                             ALU.subtract, ALU.subtract).then_inc(parts_ready, 1)
                dve.wait_ge(padded_zero, 2)
                for k in range(1, 4):
                    for q in range(4):
                        sl = slice(q * QUART, (q + 1) * QUART)
                        if k == 1:
                            dve.wait_ge(conv_done, q + 1)
                            op = dve.tensor_reduce(maxes[k][:, q:q + 1], ps[:, q, :], AX.X, ALU.max,
                                                   apply_absolute_value=True)
                        else:
                            dve.wait_ge(relu_out, 4 * (k - 2) + q + 1)
                            op = dve.tensor_reduce(maxes[k][:, q:q + 1], h[:, sl], AX.X, ALU.max,
                                                   apply_absolute_value=True)
                    settle(op)
                    dve.tensor_reduce(gmax[k], maxes[k], AX.X, ALU.max).then_inc(max_ready, 1)
                    scale_of(k, 1, scl[0] if k == 1 else None)
                    dve.tensor_copy(fac[0], fac[k]).then_inc(scale_ready, 1)
                    for q in range(4):
                        sl = slice(q * QUART, (q + 1) * QUART)
                        dve.wait_ge(rounded, 8 * k + 2 * q + 1)
                        settle(dve.tensor_scalar(n256[:, sl], n256[:, sl], F("half_sign"), F("half_shift"),
                                                 ALU.mult, ALU.add))
                        dve.wait_ge(rounded, 8 * k + 2 * q + 2)
                        if k == 3:
                            dve.tensor_tensor(hq3[:, sl], n1[:, sl], n256[:, sl], ALU.add).then_inc(parts_ready, 1)
                        else:
                            dst = (hp1 if k == 1 else hp2)[:, 2 * q:2 * q + 2, 1:1 + IMG, 1:1 + IMG]
                            shape = "p (b h w) -> p b h w"
                            dve.tensor_tensor(dst, n1[:, sl].rearrange(shape, b=2, h=IMG),
                                              n256[:, sl].rearrange(shape, b=2, h=IMG), ALU.add).then_inc(parts_ready, 1)
                for q in range(4):
                    sl = slice(q * QUART, (q + 1) * QUART)
                    for o in range(NC2):
                        n = 2 * q + o
                        dve.wait_ge(conv_done, 12 + n + 1)
                        dve.scalar_tensor_tensor(pre[:, o, sl], ps[:, (4 + n) % 8, :], aff_a[2][:, o:o + 1], x1[:, o, sl],
                                                 ALU.mult, ALU.add).then_inc(res_added, 1)
                for n in range(1, 8, 2):
                    dve.wait_ge(tok_done, n + 1)
                    dve.tensor_copy(X[:, 2 * n:2 * n + 2, :].rearrange("p a n -> p (a n)"), ps[:, (4 + n) % 8, :])\
                       .then_inc(tok_out_dve, 1)
                dve.wait_ge(wt_loaded, 16)
                dve.tensor_reduce(tern_sum[:], T("tern"), AX.X, ALU.add, apply_absolute_value=True)\
                   .then_inc(tern_summed, 1)
                dve.wait_ge(tern_summed, 2)
                tsc, tinv = gone[0], gone[1]
                settle(dve.tensor_scalar(tsc, ps[:, 4, 0:1], 1.0 / (CH * CH), EPS, ALU.mult, ALU.max))
                settle(dve.reciprocal(tinv, tsc))
                settle(dve.tensor_scalar(T("tern"), T("tern"), tinv, ROUND_1, ALU.mult, ALU.add))
                settle(dve.tensor_scalar(T("tern"), T("tern"), ROUND_1, -1.0, ALU.subtract, ALU.max))
                settle(dve.tensor_scalar(T("tern"), T("tern"), 1.0, tsc, ALU.min, ALU.mult))

        with ExitStack() as c2:
            def lb(name, shape, dt=F32):
                return sb(name, shape, dt, c2)

            xn = lb("xn", [P, 2, 2, CH])
            xnT = lb("xnT", [P, 2, NC2, PIX])
            xnT3 = lb("xnT3", [P, 2, NC2, PIX])
            xt = lb("xt", [P, 2, 2, CH])
            spare = lb("spare", [P, 1])
            stats = lb("stats", [P, 2, 2, 6])
            mv = lb("mv", [P, 2, 2, 2])
            ve = lb("ve", [P, 2, 2])
            rstd = lb("rstd", [P, 2, 2])
            bq_scaled = lb("bq_scaled", [P, NC2])
            qk = lb("qk", [P, 2, NC2, PIX])
            rest = lb("rest", [P, 2, NC2, PIX])
            parts = lb("parts", [P, 3, 2, NC2, PIX], BF16)
            QS = lb("QS", [P, 2, HEADS, PIX], BF16)
            KS = lb("KS", [P, 2, HEADS, PIX], BF16)
            V = lb("V", [P, 2, 2, HEADS, SLOT])
            nmax = lb("nmax", [P, UNITS, 4])
            Pr = lb("Pr", [P, PR_RING, 512])
            PT = lb("PT", [P, PT_RING, 512])
            OT = lb("OT", [P, 2, PIX])
            oinv = lb("oinv", [P, 2, 2, 4])
            attn = lb("attn", [P, 2, CH])
            attnT = lb("attnT", [P, NC2, PIX])
            lg = lb("lg", [P, 6, 2, EXPERTS])
            l1 = lb("l1", [P, 3, 2])
            gate = lb("gate", [P, 2, EXPERTS])
            gateT = lb("gateT", [EXPERTS, 2, P])
            acc = lb("acc", [P, 2, CH])
            accT = lb("accT", [P, NC2, PIX])
            res = lb("res", [P, 2, NC2, PIX])

            PHASES, CREDIT, TOTAL = phases()
            sems = {name: sem(name) for name in CREDIT}
            prepared = sem("prepared")
            bias_loaded = sem("bias_loaded")

            def wait(eng, at, name, piece, less=0):
                value = at.count(name, piece, less)
                if value is not None:
                    eng.wait_ge(sems[name], value)

            def full(eng, at, piece):
                b = 6 + piece[3] % 2 if piece[0] == "O1" else at.bank_of(piece)
                if b is not None:
                    wait(eng, at, f"bank_full{b}", piece)

            def drained(eng, at, piece, less=0):
                b = 6 + piece[3] % 2 if piece[0] == "O1" else at.bank_of(piece)
                if b is not None:
                    wait(eng, at, f"bank_drained{b}", piece, less)

            def bank(at, piece):
                return ps[:, at.phase.bank[piece], :]

            def drain(at, piece):
                return sems[f"bank_drained{at.phase.bank[piece]}"]

            def flat(ap):
                return ap.rearrange("p a n -> p (a n)")

            def which(stage):
                return stage % 2

            def normT(at, stage, batch):
                return xnT3[:, at.parity(batch)] if stage == 3 else xnT[:, which(stage)]

            def before(piece, by=1):
                return piece[0], piece[1], piece[2] - by, piece[3]

            def earlier_unit(kind, stage, batch, n, by, per):
                return kind, stage, batch + (n - by) // per, (n - by) % per

            def sync_piece(sp, at, piece):
                kind, stage, batch, n = piece
                if kind == "SPLIT":
                    if at.i is None:
                        wait(sp, at, "stack_loaded", before(piece))
                    wait(sp, at, "rest_ready", piece)
                    sp.dma_start(parts_dram[0].rearrange("k (c p) n -> p k c n", p=P), parts[:, 0])\
                        .then_inc(sems["parts_stored"], 16)
                    wait(sp, at, "part2_ready", piece)
                    sp.dma_start(parts_dram[1:3].rearrange("r k (c p) n -> p (r k c) n", p=P),
                                 parts[:, 1:3].rearrange("p r k c n -> p (r k c) n"))\
                        .then_inc(sems["parts_stored"], 16)
                    wait(sp, at, "parts_stored", piece)
                    for k, (stack, take) in enumerate(((QS, Q_PARTS), (KS, K_PARTS))):
                        for c, r in enumerate(take):
                            sp.dma_start(stack[DH * c:DH * (c + 1), at.parity(batch)],
                                         parts_dram[r, k].rearrange("(h d) n -> d h n", d=DH))\
                                .then_inc(sems["stack_loaded"], 16)
                if kind == "FO":
                    drained(sp, at, piece)
                    sp.dma_start(out[at.rows_out(batch), :, :].rearrange("b (c p) n -> p (b c) n", p=P),
                                 res[:, at.parity(batch)]).then_inc(sems["out_stored"], 16)

            def pool_piece(pool, at, piece):
                kind, stage, batch, n = piece
                if kind == "LNa":
                    wait(pool, at, "var_ready", piece)
                    pool.tensor_tensor(rstd[:, which(stage)], ve[:, which(stage)], F("minus_half"), ALU.pow)\
                        .then_inc(sems["rstd_ready"], 1)
                if kind == "XB":
                    wait(pool, at, "xn_ready", ("LNb", stage, batch, 0))
                    x_ = X_all[:, at.tiles(batch), :]
                    pool.tensor_tensor(x_, x_, T("bo0").unsqueeze(1).broadcast_to([P, 2, CH]), ALU.add)\
                        .then_inc(sems["x_biased"], 1)
                if kind == "SPLIT":
                    wait(pool, at, "rest_ready", piece)
                    wait(pool, at, "parts_stored", before(piece))
                    by_row = "p k c (m n) -> p (k c m) n"
                    pool.tensor_tensor(parts[:, 1].rearrange(by_row, n=P), rest[:].rearrange(by_row, n=P),
                                       F("ones").unsqueeze(1).broadcast_to([P, 2 * NC2 * 2, P]), ALU.mult)\
                        .then_inc(sems["part1_ready"], 1)
                    wait(pool, at, "part1_ready", piece)
                    pool.tensor_tensor(parts[:, 2], rest[:], parts[:, 1], ALU.subtract)\
                        .then_inc(sems["part2_ready"], 1)

            def tensor_piece(pe, at, piece):
                kind, stage, batch, n = piece
                par = at.parity(batch)
                if kind in JOBS:
                    drained(pe, at, piece, 1)
                    d = bank(at, piece)
                mm = None

                def turn4(src):
                    for c in range(NC2):
                        for t in range(2):
                            mm = pe.transpose(d[:, c * PIX + t * P:c * PIX + (t + 1) * P],
                                              src[:, t, c * P:(c + 1) * P], F("ident"))
                    return mm

                def rows(w, w_at, src):
                    for o in range(NC2):
                        for c in range(NC2):
                            mm = pe.matmul(d[:, o * PIX:(o + 1) * PIX],
                                           w[:, c * 3 * CH + w_at + o * P:c * 3 * CH + w_at + (o + 1) * P],
                                           src[:, c, :], start=(c == 0), stop=(c == 1))
                    return mm

                def toks(w, wstep, w_at, src, width=CH):
                    for t in range(2):
                        for c in range(NC2):
                            mm = pe.matmul(d[:, t * width:(t + 1) * width], src[:, c, t * P:(t + 1) * P],
                                           w[:, c * wstep + w_at:c * wstep + w_at + width],
                                           start=(c == 0), stop=(c == 1))
                    return mm

                if kind == "T":
                    wait(pe, at, "xn_ready", ("LNb", stage, batch, 0))
                    mm = turn4(xn[:, which(stage)])
                if kind in ("Q", "K", "V"):
                    drained(pe, at, ("T", stage, batch, 0))
                    w = T("in0" if stage == 0 else "in1")
                    if kind == "V":
                        mm = toks(w, 3 * CH, 2 * CH, normT(at, stage, batch))
                    else:
                        mm = rows(w, 0 if kind == "Q" else CH, normT(at, stage, batch))
                if kind == "S":
                    if n == 0:
                        wait(pe, at, "stack_loaded", ("SPLIT", stage, batch, 0))
                    g, part = n // 3, n % 3
                    r = slice(0, STACK + (BIAS_ROWS if stage == 0 else 0))
                    if part == 0:
                        pe.matmul(d, FB("ident"), FB("tri0"), start=True, stop=False, skip_group_check=True)
                        for j in range(4):
                            mm = pe.matmul(d[:, j * P:(j + 1) * P], QS[r, par, 4 * g + j, 0:P], KS[r, par, 4 * g + j, 0:P],
                                           start=False, stop=(j == 3), skip_group_check=True)
                    else:
                        pe.matmul(d.rearrange("p (j k n) -> p j k n", j=2, k=2)[:, :, 1, :], FB("ident"),
                                  FB("tri1").rearrange("p (j n) -> p j n", j=2), start=True, stop=False,
                                  skip_group_check=True)
                        for jj in range(2):
                            h = 4 * g + 2 * (part - 1) + jj
                            mm = pe.matmul(d[:, jj * PIX:(jj + 1) * PIX], QS[r, par, h, P:2 * P], KS[r, par, h, :],
                                           start=False, stop=(jj == 1), skip_group_check=True)
                if kind == "P":
                    drained(pe, at, ("S", stage, batch, n))
                    for k in range(4):
                        mm = pe.transpose(d[:, k * P:(k + 1) * P], Pr[:, n % PR_RING, k * P:(k + 1) * P], F("ident"))
                if kind == "O0":
                    o = ps[:, 6 + n % 2, :]
                    if n == 0:
                        drained(pe, at, ("V", stage, batch, 0))
                    drained(pe, at, ("P", stage, batch, 3 * n))
                    drained(pe, at, ("O1", stage, batch, n), 1)
                    for j in range(4):
                        pe.matmul(o[32 * j:32 * j + 32, 0:P], V[:, par, 0, 4 * n + j, :],
                                  PT[:, 3 * n % PT_RING, j * P:(j + 1) * P], start=True, stop=True)
                if kind == "O1":
                    o = ps[:, 6 + n % 2, :]
                    drained(pe, at, ("P", stage, batch, 3 * n + 1))
                    drained(pe, at, ("P", stage, batch, 3 * n + 2))
                    for kt in range(2):
                        for j in range(4):
                            k = 2 * (j % 2) + kt
                            mm = pe.matmul(o[32 * j:32 * j + 32, P:2 * P], V[:, par, kt, 4 * n + j, :],
                                           PT[:, (3 * n + 1 + j // 2) % PT_RING, k * P:(k + 1) * P],
                                           start=(kt == 0), stop=(kt == 1))
                    mm.then_inc(sems[f"bank_full{6 + n % 2}"], 1)
                if kind == "OX":
                    drained(pe, at, ("O1", stage, batch, n))
                    for t in range(2):
                        mm = pe.transpose(d[:, t * P:(t + 1) * P], OT[:, n % 2, t * P:(t + 1) * P], F("ident"))
                if kind == "AT":
                    drained(pe, at, ("OX", stage, batch, GROUPS - 1))
                    mm = turn4(attn)
                if kind == "PR":
                    drained(pe, at, ("AT", stage, batch, 0))
                    mm = toks(T("out0" if stage == 0 else "out1"), CH, 0, attnT)
                if kind in ("FF", "R"):
                    drained(pe, at, ("T", stage, batch, 0))
                    if kind == "FF":
                        mm = toks(T("tern"), CH, 0, normT(at, stage, batch))
                    else:
                        mm = toks(M("Wr"), EXPERTS, 0, normT(at, stage, batch), EXPERTS)
                if kind == "GT":
                    wait(pe, at, "gates_ready", ("RT", stage, batch, 0))
                    for t in range(2):
                        mm = pe.transpose(d[0:EXPERTS, t * P:(t + 1) * P], gate[:, t, :], F("ident"))
                if kind == "GB":
                    drained(pe, at, ("GT", stage, batch, 0))
                    for t in range(2):
                        mm = pe.matmul(d[:, t * CH:(t + 1) * CH], gateT[:, t, :], M("be")[0:EXPERTS, :],
                                       start=True, stop=True)
                if kind == "E":
                    t, e = n // 4, n % 4
                    for c in range(NC2):
                        mm = pe.matmul(d, normT(at, stage, batch)[:, c, t * P:(t + 1) * P],
                                       M("We", c * EXPERTS * CH + e * 2 * CH, 2 * CH), start=(c == 0), stop=(c == 1))
                if kind == "CT":
                    drained(pe, at, ("E", stage, batch, 3))
                    drained(pe, at, ("E", stage, batch, 7))
                    mm = turn4(acc)
                if kind == "FO":
                    drained(pe, at, ("CT", stage, batch, 0))
                    for o in range(NC2):
                        for c in range(NC2):
                            pe.matmul(d[:, o * PIX:(o + 1) * PIX], M("Wo", c * CH + o * P, P), accT[:, c, :],
                                      start=(c == 0), stop=False)
                        for t in range(2):
                            mm = pe.matmul(d[:, o * PIX + t * P:o * PIX + (t + 1) * P], xt[:, par, t, o * P:(o + 1) * P],
                                           F("ident"), start=False, stop=(t == 1))
                if kind in JOBS:
                    mm.then_inc(sems[f"bank_full{at.phase.bank[piece]}"], 1)

            def scalar_piece(act, at, piece):
                kind, stage, batch, n = piece
                par = at.parity(batch)

                def copy_out(dst):
                    full(act, at, piece)
                    act.activation(dst, bank(at, piece), ACT.Copy).then_inc(drain(at, piece), 1)

                if kind == "T":
                    full(act, at, {3: ("E", 3, batch - 2, 7), 1: ("FF", 1, batch - 1, 0)}.get(stage, ("V", stage, batch - 1, 0)))
                    copy_out(flat(normT(at, stage, batch)))
                if kind in ("Q", "K"):
                    if kind == "Q":
                        wait(act, at, "rest_ready", ("SPLIT", stage, batch - 1, 0))
                    full(act, at, piece)
                    dst = qk[:, "QK".index(kind)]
                    scale = DH ** -0.5 if kind == "Q" else 1.0
                    if stage == 0:
                        bias = bq_scaled if kind == "Q" else T("bk0")
                        for c in range(NC2):
                            op = act.activation(dst[:, c, :], bank(at, piece)[:, c * PIX:(c + 1) * PIX], ACT.Identity,
                                                scale=scale, bias=bias[:, c:c + 1])
                    else:
                        op = act.activation(flat(dst), bank(at, piece), ACT.Copy, scale=scale)
                    op.then_inc(drain(at, piece), 1)
                if kind == "S":
                    wait(act, at, "unit_max", piece)
                    full(act, at, earlier_unit("P", stage, batch, n, PR_RING, UNITS))
                    w_ = P if n % 3 == 0 else PIX
                    for k in range(512 // w_):
                        op = act.activation(Pr[:, n % PR_RING, k * w_:(k + 1) * w_], bank(at, piece)[:, k * w_:(k + 1) * w_],
                                            ACT.Exp, bias=nmax[:, n, k:k + 1])
                    op.then_inc(drain(at, piece), 1)
                if kind == "P" and n % 3 in PT_BY_ACT:
                    pt_free(act, at, piece)
                    copy_out(PT[:, n % PT_RING, :])
                if kind == "O1":
                    full(act, at, piece)
                    full(act, at, earlier_unit("OX", stage, batch, n, 2, GROUPS))
                    act.activation(OT[:, n % 2, :], ps[:, 6 + n % 2, 0:PIX], ACT.Copy)\
                        .then_inc(sems[f"bank_drained{6 + n % 2}"], 1)
                if kind == "AT":
                    full(act, at, ("PR", stage, batch - 1, 0))
                    copy_out(flat(attnT))
                if kind == "RT":
                    wait(act, at, "router_shifted", ("R", stage, batch, 0))
                    act.activation(lg[:, 5], lg[:, 1], ACT.Exp).then_inc(sems["router_exp"], 1)
                if kind == "GT":
                    full(act, at, piece)
                    act.activation(flat(gateT), bank(at, piece)[0:EXPERTS, 0:2 * P], ACT.Copy).then_inc(drain(at, piece), 1)
                if kind == "GB":
                    full(act, at, ("CT", stage, batch - 1, 0))
                    copy_out(flat(acc))
                if kind == "CT":
                    full(act, at, ("FO", stage, batch - 1, 0))
                    copy_out(flat(accT))
                if kind == "FO":
                    wait(act, at, "out_stored", before(piece, 2))
                    full(act, at, piece)
                    for o in range(NC2):
                        op = act.activation(res[:, par, o, :], bank(at, piece)[:, o * PIX:(o + 1) * PIX], ACT.Identity,
                                            bias=M("bo", o, 1))
                    op.then_inc(drain(at, piece), 1)

            def pt_free(eng, at, piece):
                kind, stage, batch, n = earlier_unit("P", piece[1], piece[2], piece[3], PT_RING, UNITS)
                full(eng, at, ("O1", stage, batch, n // 3))

            def vector_piece(dve, at, piece):
                kind, stage, batch, n = piece
                par = at.parity(batch)
                local = [0]

                def settle(ins):
                    local[0] += 1
                    ins.then_inc(sems["dve_step"], 1)
                    wait(dve, at, "dve_step", piece, SETTLED[kind] - local[0])

                def rows_of_x():
                    return xt[:, par] if stage == 3 else X_all[:, at.tiles(batch), :]

                if kind in ("LNa", "LNb"):
                    m, src = which(stage), rows_of_x()
                if kind == "LNa":
                    if stage % 2:
                        drained(dve, at, ("PR", stage - 1, batch, 0))
                        dve.memset(spare[:], 0.0)
                    for t in range(2):
                        op = dve.bn_stats(stats[:, m, t, :], src[:, t, :])
                    settle(op)
                    dve.memset(ve[:, m], EPS)
                    for t in range(2):
                        op = dve.bn_aggr(mv[:, m, t, :], stats[:, m, t, :])
                    settle(op)
                    dve.tensor_tensor(ve[:, m], ve[:, m], mv[:, m, :, 1], ALU.add).then_inc(sems["var_ready"], 1)
                if kind == "LNb":
                    wait(dve, at, "rstd_ready", ("LNa", stage, batch, 0))
                    full(dve, at, ("T", stage, batch - 1, 0))
                    for t in range(2):
                        op = dve.tensor_scalar(xn[:, m, t, :], src[:, t, :], mv[:, m, t, 0:1], rstd[:, m, t:t + 1],
                                               ALU.subtract, ALU.mult)
                    op.then_inc(sems["xn_ready"], 1)
                if kind == "SPLIT":
                    drained(dve, at, ("Q", stage, batch, 0))
                    drained(dve, at, ("K", stage, batch, 0))
                    wait(dve, at, "parts_stored", before(piece))
                    settle(dve.tensor_copy(parts[:, 0], qk[:]))
                    wait(dve, at, "part2_ready", before(piece))
                    dve.tensor_tensor(rest[:], qk[:], parts[:, 0], ALU.subtract).then_inc(sems["rest_ready"], 1)
                if kind == "V":
                    full(dve, at, piece)
                    full(dve, at, ("O1", stage, batch - 2, GROUPS - 1))
                    for t in range(2):
                        dst = V[:, par, t, :, 0:DH]
                        src = bank(at, piece)[:, t * CH:(t + 1) * CH].rearrange("p (h d) -> p h d", d=DH)
                        if stage == 0:
                            op = dve.tensor_tensor(dst, src, T("bv0").rearrange("p (h d) -> p h d", d=DH), ALU.add)
                        else:
                            op = dve.tensor_copy(dst, src)
                    op.then_inc(drain(at, piece), 1)
                if kind == "S":
                    full(dve, at, piece)
                    w_ = P if n % 3 == 0 else PIX
                    dve.tensor_reduce(nmax[:, n, 0:512 // w_], bank(at, piece).rearrange("p (j n) -> p j n", n=w_),
                                      AX.X, ALU.max, negate=True).then_inc(sems["unit_max"], 1)
                if kind == "P" and n % 3 not in PT_BY_ACT:
                    pt_free(dve, at, piece)
                    full(dve, at, piece)
                    dve.tensor_copy(PT[:, n % PT_RING, :], bank(at, piece)).then_inc(drain(at, piece), 1)
                if kind == "OX":
                    full(dve, at, piece)
                    if n == 0:
                        full(dve, at, ("AT", stage, batch - 1, 0))
                    o4 = bank(at, piece)[:, 0:2 * P].rearrange("p (t j s) -> p t j s", t=2, j=4)
                    settle(dve.reciprocal(oinv[:, n % 2], o4[:, :, :, DH]))
                    dve.tensor_tensor(attn[:, :, 4 * DH * n:4 * DH * (n + 1)].rearrange("p t (j d) -> p t j d", j=4),
                                      o4[:, :, :, 0:DH], oinv[:, n % 2].unsqueeze(3).broadcast_to([P, 2, 4, DH]),
                                      ALU.mult).then_inc(drain(at, piece), 1)
                if kind in ("PR", "FF"):
                    full(dve, at, piece)
                    if kind == "PR" and stage == 0:
                        wait(dve, at, "x_biased", ("XB", 0, batch, 0))
                    if kind == "PR" and stage == 2:
                        full(dve, at, ("FO", 3, batch - 2, 0))
                    old = flat(X_all[:, at.tiles(batch), :])
                    dve.tensor_tensor(flat(xt[:, par]) if stage == 2 else old, bank(at, piece), old, ALU.add)\
                       .then_inc(drain(at, piece), 1)

                L, D, C, one, two, E = (lg[:, k] for k in range(6))
                m, su = l1[:, 1, :], l1[:, 2, :]

                def wide(v):
                    return v.unsqueeze(2).broadcast_to([P, 2, EXPERTS])

                def first_largest(D, one):
                    settle(dve.scalar_tensor_tensor(C, D, 0.0, F("tie").rearrange("p (t e) -> p t e", t=2),
                                                    ALU.is_equal, ALU.mult))
                    settle(dve.tensor_reduce(m, C, AX.X, ALU.max))
                    settle(dve.tensor_tensor(one, C, wide(m), ALU.is_equal))

                if kind == "R":
                    full(dve, at, piece)
                    dve.tensor_tensor(L, bank(at, piece)[:, 0:2 * EXPERTS].rearrange("p (t e) -> p t e", t=2),
                                      M("br").rearrange("p (t e) -> p t e", t=2), ALU.add).then_inc(drain(at, piece), 1)
                    drained(dve, at, piece)
                    settle(dve.tensor_reduce(l1[:, 0, :], L, AX.X, ALU.max))
                    dve.tensor_tensor(D, L, wide(l1[:, 0, :]), ALU.subtract).then_inc(sems["router_shifted"], 1)
                if kind == "RT":
                    wait(dve, at, "router_shifted", ("R", stage, batch, 0))
                    first_largest(D, one)
                    wait(dve, at, "router_exp", piece)
                    settle(dve.scalar_tensor_tensor(L, one, MASKED, D, ALU.mult, ALU.add))
                    settle(dve.tensor_reduce(m, L, AX.X, ALU.max))
                    settle(dve.tensor_tensor(L, L, wide(m), ALU.subtract))
                    first_largest(L, two)
                    settle(dve.tensor_tensor(one, one, two, ALU.add))
                    settle(dve.tensor_reduce(su, E, AX.X, ALU.add))
                    settle(dve.reciprocal(m, su))
                    settle(dve.tensor_tensor(one, one, E, ALU.mult))
                    dve.tensor_tensor(gate[:], one, wide(m), ALU.mult).then_inc(sems["gates_ready"], 1)
                if kind == "E":
                    t, e = n // 4, n % 4
                    if e == 0:
                        drained(dve, at, ("GB", stage, batch, 0))
                    else:
                        drained(dve, at, ("E", stage, batch, n - 1))
                    full(dve, at, piece)
                    for k in range(2):
                        op = dve.scalar_tensor_tensor(acc[:, t, :], bank(at, piece)[:, k * CH:(k + 1) * CH],
                                                      gate[:, t, 2 * e + k:2 * e + k + 1], acc[:, t, :], ALU.mult, ALU.add)
                        if k == 0:
                            settle(op)
                    op.then_inc(drain(at, piece), 1)
                assert local[0] == SETTLED.get(kind, 0), piece

            def walk(eng, phase, piece_of):
                if not phase.bodies:
                    for piece in phase.pieces:
                        piece_of(eng, Spot(phase), piece)
                    return
                with eng.Fori(0, phase.bodies // 2) as i:
                    for half in range(2):
                        for piece in phase.pieces:
                            piece_of(eng, Spot(phase, i, half), piece)

            with nc.Block() as block:
                @block.sync
                def _(sp):
                    for k, stack in enumerate((QS, KS)):
                        for par in range(2):
                            sp.dma_start(stack[STACK:STACK + BIAS_ROWS, par], bias_in[:, k].bitcast(BF16))\
                              .then_inc(bias_loaded, 16)
                    for name in TRANSFERS:
                        sp.sem_inc(sems[name], CREDIT[name])
                    sp.wait_ge(bias_loaded, 64)

                @block.gpsimd
                def _(pool):
                    pool.memset(V[:], 0.0).then_inc(prepared, 1)
                    pool.wait_ge(prepared, 1)
                    pool.memset(V[:].rearrange("p a t h s -> p (a t h) s")[:, :, DH:DH + 1], 1.0)

                @block.vector
                def _(dve):
                    for k, name in enumerate(CREDIT):
                        if name not in TRANSFERS:
                            dve.sem_inc(sems[name], CREDIT[name])
                    dve.wait_ge(wt_loaded, 16)
                    dve.tensor_scalar(bq_scaled[:], T("bq0"), DH ** -0.5, None, ALU.mult)
                    dve.memset(X_all[:, 0:2 * LEAD, :], 0.0)
                    dve.memset(X_all[:, 2 * (LEAD + BATCH):, :], 0.0)
                    dve.memset(Pr[:], 1.0)
                    dve.memset(PT[:], 1.0)
                    dve.memset(ps[:, 6:8, 0:PIX], 1.0)
                    for buffer in (xt, xnT3, attn, gate):
                        dve.memset(buffer[:], 0.0)

            for phase in PHASES:
                with nc.Block() as block:
                    @block.sync
                    def _(sp):
                        walk(sp, phase, sync_piece)
                        if phase is PHASES[-1]:
                            sp.wait_ge(sems["out_stored"], TOTAL["out_stored"])
                            sp.wait_ge(sems["stack_loaded"], TOTAL["stack_loaded"])

                    @block.gpsimd
                    def _(pool):
                        walk(pool, phase, pool_piece)

                    @block.tensor
                    def _(pe):
                        if phase is PHASES[0]:
                            pe.wait_ge(fixb_loaded, 16)
                            pe.wait_ge(wm_loaded, 16)
                        walk(pe, phase, tensor_piece)

                    @block.scalar
                    def _(act):
                        walk(act, phase, scalar_piece)

                    @block.vector
                    def _(dve):
                        walk(dve, phase, vector_piece)




def bf16_bits(np, v):
    u = np.ascontiguousarray(v, np.float32).view(np.uint32)
    return ((u + 0x7FFF + (u >> 16 & 1)) >> 16).astype(np.uint16)


def _fixed(np):
    fix = np.zeros((P, FIX_N), np.float32)

    def put(name, v):
        a, n = FIX[name]
        fix[:, a:a + n] = v

    r = np.arange(P)
    put("ident", np.eye(P))
    put("ones", 1.0)
    lower = (r >= WID)[:, None]
    put("stack", (r[:, None] % WID) == (r[None, :] % WID))
    put("tie", np.tile(EXPERTS - np.arange(EXPERTS), 2)[None, :])
    put("low_half", lower)
    put("half_sign", np.where(lower, -1.0, 1.0))
    put("half_shift", np.where(lower, 1.0, -1.0) * ROUND_256 - ROUND_1)
    put("minus_half", -0.5)

    fb = np.zeros((P, FIXB_N), np.float32)

    def putb(name, v):
        a, n = FIXB[name]
        fb[:v.shape[0], a:a + n] = v

    tri = np.where(r[None, :] <= r[:, None], 0.0, MASKED)
    putb("ident", np.eye(P))
    putb("tri0", np.tile(tri, (1, 4)))
    putb("tri1", np.tile(tri, (1, 2)))
    def parts(v):
        out, v = [], np.asarray(v, np.float32)
        for _ in range(3):
            h = (bf16_bits(np, v).astype(np.uint32) << 16).view(np.float32)
            out.append(h)
            v = v - h
        return np.stack(out)

    first = 2.0 ** -(2.0 ** -(np.log2(HEADS) - 3))
    slopes = np.asarray([first * first ** h for h in range(HEADS)], np.float32)[:, None]
    where = np.arange(PIX, dtype=np.float32)[None, :]
    all_ = (3, HEADS, PIX)
    bias = np.zeros((BIAS_ROWS, 2, HEADS, PIX), np.float32)
    bias[:3, 0], bias[3:, 0] = np.ones(all_), np.broadcast_to(-where, all_)
    bias[:3, 1], bias[3:, 1] = parts(slopes * where), parts(np.broadcast_to(slopes, all_[1:]))
    return fix, bf16_bits(np, fb), bf16_bits(np, bias)


def kernel(**inputs):
    import numpy as np
    import concourse.bacc as _bacc
    from concourse import mybir as _mybir
    from concourse.bass_utils import run_bass_kernel_spmd as _run

    v = {k: np.asarray(a) for k, a in inputs.items()}
    f32 = np.float32

    def chunks(w):
        return w.reshape(-1, P, w.shape[1]).transpose(1, 0, 2).reshape(P, -1)

    def cols(vec):
        return vec.reshape(-1, P).T

    def twice(a):
        return np.concatenate([a, a], 0)

    def pack(layout, total, **parts):
        buf = np.zeros((P, total), f32)
        for name, a in parts.items():
            at, n = layout[name]
            buf[:, at:at + n] = a
        return buf

    w0 = pack(W0, W0_N, theta=chunks(v["L0_conv_theta_w"].T), phi=chunks(v["L0_conv_phi_w"].T),
              g=chunks(v["L0_conv_g_w"].T), wz=v["L0_conv_wz_w"].T, g_b=v["L0_conv_g_b"][None, :],
              theta_b=cols(v["L0_conv_theta_b"]), phi_b=cols(v["L0_conv_phi_b"]), wz_b=cols(v["L0_conv_wz_b"]),
              gamma=cols(v["L0_conv_bn_gamma"]), beta=cols(v["L0_conv_bn_beta"]))
    c1 = v["L1_conv_w1"].reshape(WID, CH).T
    c2 = v["L1_conv_w2"].transpose(1, 2, 3, 0).reshape(WID, 9, WID)
    inner = {}
    for k in (1, 2):
        for p in "gbmv":
            inner[f"{p}{k}"] = twice(v[f"L1_conv_bn{k}_{p}"][:, None])
    for p in "gbmv":
        inner[f"{p}3"] = cols(v[f"L1_conv_bn3_{p}"])
    w1 = pack(W1, W1_N, w1=chunks(np.concatenate([c1, c1], 1)),
              w2=twice(np.concatenate([c2, c2], 2).reshape(WID, -1)),
              w3=twice(v["L1_conv_w3"].reshape(CH, WID).T), peg=twice(v["L1_conv_peg_w"].reshape(WID, 9)),
              peg_b=twice(v["L1_conv_peg_b"][:, None]), **inner)
    b_in = v["L2_attn_b_in"]
    wt = pack(WT, WT_N, in0=chunks(v["L2_attn_w_in"]), out0=chunks(v["L2_attn_w_out"]),
              in1=chunks(np.concatenate([v[f"L3_attn_w_{p}"].T for p in "qkv"], 1)),
              out1=chunks(v["L3_attn_w_o"].T), tern=chunks(v["L2_ffn_weight"].T), bv0=b_in[None, 2 * CH:],
              bo0=v["L2_attn_b_out"][None, :], bq0=cols(b_in[:CH]), bk0=cols(b_in[CH:2 * CH]))
    be = np.zeros((P, CH), f32)
    be[:EXPERTS] = v["L3_ffn_be"]
    wm = pack(WM, WM_N, We=chunks(v["L3_ffn_We"].transpose(2, 0, 1).reshape(CH, EXPERTS * CH)),
              Wr=chunks(v["L3_ffn_Wr"].T), Wo=chunks(v["L3_ffn_Wo"].T), be=be, bo=cols(v["L3_ffn_bo"]),
              br=np.tile(v["L3_ffn_br"], 2)[None, :])
    fix, fixb, bias = _fixed(np)
    arrays = {"x_dram": np.ascontiguousarray(v["x"].reshape(BATCH, CH, PIX)), "fix_dram": fix, "fixb_dram": fixb,
              "bias_dram": bias,
              "w0_dram": w0, "w1_dram": w1, "wt_dram": wt, "wm_dram": wm}

    nc = _bacc.Bacc("TRN2", target_bir_lowering=False, num_devices=1)
    args = [nc.dram_tensor(n, a.shape, _mybir.dt.from_np(a.dtype), kind="ExternalInput").ap() for n, a in arrays.items()]
    parts_dram = nc.dram_tensor("parts_dram", (3, 2, CH, PIX), _mybir.dt.bfloat16, kind="Internal").ap()
    out = nc.dram_tensor("out_dram", (OUT_LEAD + BATCH, CH, PIX), _mybir.dt.float32, kind="ExternalOutput").ap()
    build(nc, *args, parts_dram, out)
    r = _run(nc, [arrays], core_ids=[0])
    return r.results[0]["out_dram"][OUT_LEAD:].reshape(BATCH, CH, IMG, IMG)
```

```python
from contextlib import ExitStack

import concourse.bass as bass
from concourse import mybir

F32 = mybir.dt.float32
BF16 = mybir.dt.bfloat16
I32 = mybir.dt.int32
ALU = mybir.AluOpType
ACT = mybir.ActivationFunctionType
AX = mybir.AxisListType

P = 128
BATCH, CH, IMG = 8, 256, 16
PIX = IMG * IMG
TOK = BATCH * PIX
NC2 = CH // P
INTER = 128
POOLED = PIX // 4
QUART = TOK // 4
WID = 64
PAD = IMG + 2
HEADS, DH = 16, 16
GROUPS = 4
EXPERTS = 8
SLOT = 32

QMAX = 2.0 ** 15 - 1.0
MIN_ABS = 1e-12
ROUND_1 = 1.5 * 2.0 ** 23
ROUND_256 = 1.5 * 2.0 ** 31
SQRT2 = 1.4142135
EPS = 1e-5
MASKED = -1e30
QUARTERS = (2, 0, 3, 1)



def columns(*fields):
    at, out = 0, {}
    for name, width in fields:
        out[name] = (at, width)
        at += width
    return out, at


FIX, FIX_N = columns(("ident", P), ("ones", P), ("stack", P), ("tie", 2 * EXPERTS),
                     ("low_half", 1), ("half_sign", 1), ("half_shift", 1), ("minus_half", 2))
FIXB, FIXB_N = columns(("ident", P), ("tri0", 4 * P), ("tri1", 2 * P))
W0, W0_N = columns(("theta", NC2 * INTER), ("phi", NC2 * INTER), ("g", NC2 * INTER), ("wz", CH), ("g_b", INTER),
                   ("theta_b", 1), ("phi_b", 1), ("wz_b", NC2), ("gamma", NC2), ("beta", NC2))
W1, W1_N = columns(("w1", NC2 * P), ("w2", 9 * P), ("w3", CH), ("peg", 9), ("peg_b", 1),
                   ("g1", 1), ("b1", 1), ("m1", 1), ("v1", 1), ("g2", 1), ("b2", 1), ("m2", 1), ("v2", 1),
                   ("g3", 2), ("b3", 2), ("m3", 2), ("v3", 2))
QUANT = W1["peg_b"][0]
WT, WT_N = columns(("in0", NC2 * 3 * CH), ("out0", NC2 * CH), ("in1", NC2 * 3 * CH), ("out1", NC2 * CH),
                   ("tern", NC2 * CH), ("bv0", CH), ("bo0", CH), ("bq0", NC2), ("bk0", NC2))
WM, WM_N = columns(("We", NC2 * EXPERTS * CH), ("Wr", NC2 * EXPERTS), ("Wo", NC2 * CH), ("be", CH), ("bo", NC2),
                   ("br", 2 * EXPERTS))

UNITS = 3 * GROUPS
RING = 6
LEAD, TAIL = 2, 2
OUT_LEAD = 1
PEELED = 2
PR_RING, PT_RING = 4, 6
PT_BY_ACT = (1,)
Q_PARTS = (0, 0, 1, 1, 0, 2)
K_PARTS = (0, 1, 0, 1, 2, 0)
STACK = DH * len(Q_PARTS)
BIAS_ROWS = 6



def attention_slots(s):
    slots = []
    for t in range(UNITS):
        p = [("S", s, 0, t)]

        def late(kind, step, index):
            p.append((kind, s, 0 if step < UNITS else -1, index))

        u = (t - 3) % UNITS
        late("P", u + 3, u)
        v = (t - 5) % UNITS
        if v % 3 == 0:
            late("O0", v + 5, v // 3)
        if v % 3 == 2:
            late("O1", v + 5, v // 3)
        g, r = divmod((t - 9) % UNITS, 3)
        if r == 0:
            late("OX", 3 * g + 9, g)
        slots.append(p)
    return slots


LONG = ("V", "PR", "FF", "E")
FLOW = {
    0: (("LNa", 0, 0, -17), ("LNb", 0, 0, -15), ("XB", 0, 0, -13), ("T", 0, 0, -14), ("Q", 0, 0, -12),
        ("SPLIT", 0, 0, -11), ("K", 0, 0, -9), ("SPLIT", 0, 1, -8), ("V", 0, 0, -6), ("AT", 0, 0, 19),
        ("PR", 0, 0, 21), ("LNa", 1, 0, 24), ("LNb", 1, 0, 25), ("T", 1, 0, 25), ("FF", 1, 0, 29)),
    2: (("LNa", 2, 0, -17), ("LNb", 2, 0, -15), ("T", 2, 0, -14), ("Q", 2, 0, -12), ("SPLIT", 2, 0, -11),
        ("K", 2, 0, -9), ("SPLIT", 2, 1, -8), ("V", 2, 0, -6), ("AT", 2, 0, 19), ("PR", 2, 0, 20),
        ("LNa", 3, 0, 21), ("LNb", 3, 0, 22), ("T", 3, 0, 23), ("R", 3, 0, 24), ("RT", 3, 0, 24),
        ("RT", 3, 1, 25), ("RT", 3, 2, 26), ("RT", 3, 3, 27), ("GT", 3, 0, 28), ("E", 3, 0, 28),
        ("GB", 3, 0, 29), ("E", 3, 1, 29), ("E", 3, 2, 29), ("E", 3, 3, 30), ("E", 3, 4, 31), ("E", 3, 5, 33),
        ("E", 3, 6, 33), ("E", 3, 7, 34), ("CT", 3, 0, 36), ("FO", 3, 0, 37)),
}


def body(s):
    tensor = [(slot, []) for slot in attention_slots(s)]
    others = [([slot[0]], [], slot[1:]) for slot in attention_slots(s)]
    for kind, stage, index, slot in FLOW[s]:
        t, piece = slot % UNITS, (kind, stage, -(slot // UNITS), index)
        tensor[t][1].append(piece)
        if kind in LONG and t + 1 < UNITS:
            others[t + 1][1].append(piece)
        else:
            others[t][2].append(piece)
    return tensor, others


def listed(slots, batch=0, keep=lambda b: True):
    return [(k, s, batch + d, n) for groups in slots for group in groups for k, s, d, n in group if keep(batch + d)]


def start(s):
    pieces = listed(body(s)[1])
    order = [(k, st, batch, n) for batch, ahead in ((0, 2), (0, 1), (1, 2)) for k, st, d, n in pieces if d == ahead]
    ahead = [p for p in order if p[0] == "LNa"]
    lead = [ahead[0], ("LNb", s, 0, 0)] + [("XB", 0, 0, 0)] * (s == 0) + ahead[1:]
    return lead + [p for p in order if p not in lead]


NORMS_FIRST = 4


def change(order):
    out = []
    for b in range(BATCH - PEELED, BATCH + PEELED):
        for first, second in zip(body(0)[order], body(2)[order]):
            for g0, g2 in zip(first, second):
                out += listed([[g0]], b, lambda batch: batch < BATCH)
                out += listed([[g2]], b - BATCH, lambda batch: batch >= 0)
    return out


def finish(s):
    return [p for b in range(BATCH, BATCH + 3) for p in listed(body(s)[1], b, lambda batch: batch < BATCH)]


JOBS = ("S", "P", "OX", "T", "Q", "K", "V", "AT", "PR", "FF", "R", "GT", "GB", "E", "CT", "FO")
SETTLED = {"LNa": 2, "OX": 1, "R": 1, "RT": 3, "E": 1}
TRANSFERS = ("parts_stored", "stack_loaded", "out_stored")


def settled(piece):
    return SETTLED.get(piece[0], 0) + (piece[0] == "RT" and piece[3] == 3)


def signals(piece, bank):
    kind, n = piece[0], piece[3]
    out = []
    if kind in JOBS:
        out += [(f"bank_full{bank}", 1), (f"bank_drained{bank}", 1)]
    if kind == "O1":
        out += [(f"bank_full{6 + n % 2}", 1), (f"bank_drained{6 + n % 2}", 1)]
    if kind in SETTLED:
        out.append(("dve_step", settled(piece)))
    out += {"LNa": [("var_ready", 1), ("rstd_ready", 1)], "LNb": [("xn_ready", 1)], "XB": [("x_biased", 1)],
            "S": [("unit_max", 1)], "FO": [("out_stored", 16)],
            "SPLIT": [("rest_ready", 1), ("second_ready", 1), ("third_ready", 1), ("parts_stored", 16),
                      ("stack_loaded", 16 * len(Q_PARTS))],
            "R": [("router_shifted", 1)], "RT": {0: [("router_exp", 1)], 3: [("gates_ready", 1)]}.get(n, [])}.get(kind, [])
    return out


class Phase:

    def __init__(self, pieces, counts, bodies=0, first=0, loop=None):
        self.tensor, self.others = pieces
        self.loop = loop
        self.first = first
        self.base, self.bodies = dict(counts), bodies
        self.bank, self.after, self.per = {}, {}, {}
        jobs = 0
        for p in self.tensor:
            if p[0] in JOBS:
                self.bank[p] = jobs % RING
                jobs += 1
            self.add(p, [(name, k) for name, k in signals(p, self.bank.get(p)) if name.startswith("bank")])
        for p in self.others:
            self.add(p, [(name, k) for name, k in signals(p, self.bank.get(p)) if not name.startswith("bank")])
        assert not bodies or jobs % RING == 0
        for name, k in self.per.items():
            counts[name] = counts.get(name, 0) + k * max(bodies, 1)

    def add(self, piece, signalled):
        for name, k in signalled:
            self.per[name] = self.per.get(name, 0) + k
            self.after[piece, name] = self.per[name]


def phases():
    credit = {}
    for s in (0, 2):
        for name, k in Phase([listed(slots) for slots in body(s)], {}).per.items():
            credit[name] = max(credit.get(name, 0), 3 * k)
    counts = dict(credit)

    def straight(tensor, others, after=None):
        return Phase((tensor, others), counts, loop=after)

    def loop(s, first):
        return Phase([listed(slots) for slots in body(s)], counts, BATCH - PEELED, first)

    opening = straight(start(0), start(0))
    first = loop(0, 0)
    between = straight(change(0), change(1), first)
    second = loop(2, PEELED)
    return [opening, first, between, second, straight(finish(2), finish(2), second)], credit, counts


class Spot:

    def __init__(self, phase, i=None, half=0):
        self.phase, self.i, self.half = phase, i, half
        self.asked = {}

    def parity(self, batch):
        return (self.half + batch) % 2

    def tiles(self, batch):
        if self.i is None:
            return slice(2 * (batch + LEAD), 2 * (batch + LEAD) + 2)
        return bass.ds(self.i * 4 + 2 * (self.phase.first + self.half + batch + LEAD), 2)

    def rows_out(self, batch):
        if self.i is None:
            return slice(batch + OUT_LEAD, batch + OUT_LEAD + 1)
        return bass.ds(self.i * 2 + (self.phase.first + self.half + batch + OUT_LEAD), 1)

    def places(self, piece):
        kind, stage, batch, n = piece
        if self.i is not None:
            return [(back, (kind, stage, batch + back, n)) for back in range(4)]
        return [(0, piece)] + [(0, (kind, stage - 2, batch + BATCH, n))] * (stage >= 2 and batch < 0)

    def in_loop_before(self, piece, table, key=lambda p: p):
        loop = self.phase.loop
        for _, (kind, stage, batch, n) in self.places(piece):
            for b in range(loop.bodies if loop else 0):
                p = kind, stage, batch - loop.first - b, n
                if key(p) in table(loop):
                    return b, p
        return None

    def bank_of(self, piece):
        for back, p in self.places(piece):
            if p in self.phase.bank:
                return self.phase.bank[p]
        done = self.in_loop_before(piece, lambda loop: loop.bank)
        return self.phase.loop.bank[done[1]] if done else None

    def reach(self, name, piece, less=0):
        ph = self.phase
        for back, p in self.places(piece):
            if (p, name) in ph.after:
                value = ph.base.get(name, 0) + (self.half - back) * ph.per[name] * (self.i is not None)
                value += ph.after[p, name] - less
                assert value >= 1, (name, piece)
                return value
        done = self.in_loop_before(piece, lambda loop: loop.after, lambda p: (p, name))
        if done:
            return ph.loop.base.get(name, 0) + done[0] * ph.loop.per[name] + ph.loop.after[done[1], name] - less
        return ph.base[name] if name in TRANSFERS else None

    def asks_more(self, name, piece, less):
        value = self.reach(name, piece, less)
        if value is None or value <= self.asked.get(name, 0):
            return False
        self.asked[name] = value
        return True

    def count(self, name, piece, less=0):
        value = self.reach(name, piece, less)
        in_loop = self.i is not None and any((p, name) in self.phase.after for back, p in self.places(piece))
        return self.i * (2 * self.phase.per[name]) + value if in_loop else value


def build(nc, x_in, fix_in, fixb_in, bias_in, w0_in, w1_in, wt_in, wm_in, parts_dram, out):
    ctx = ExitStack()
    with ctx:
        def sb(name, shape, dt=F32, c=ctx):
            return c.enter_context(nc.sbuf_tensor(name, shape, dt))

        def sem(name):
            return ctx.enter_context(nc.semaphore(name))

        ps = ctx.enter_context(nc.psum_tensor("ps", [P, 8, 512], F32))

        fix = sb("fix", [P, FIX_N])
        fixb = sb("fixb", [P, FIXB_N], BF16)
        wt = sb("wt", [P, WT_N])
        wm = sb("wm", [P, WM_N])
        X_all = sb("X", [P, 2 * (LEAD + BATCH + TAIL), CH])
        X = X_all[:, 2 * LEAD:2 * (LEAD + BATCH), :]

        def F(name, lo=0, n=None):
            at, w = FIX[name]
            return fix[:, at + lo:at + lo + (w - lo if n is None else n)]

        def FB(name, lo=0, n=None):
            at, w = FIXB[name]
            return fixb[:, at + lo:at + lo + (w - lo if n is None else n)]

        def T(name, lo=0, n=None):
            at, w = WT[name]
            return wt[:, at + lo:at + lo + (w - lo if n is None else n)]

        def M(name, lo=0, n=None):
            at, w = WM[name]
            return wm[:, at + lo:at + lo + (w - lo if n is None else n)]

        fix_loaded = sem("fix_loaded")
        fixb_loaded = sem("fixb_loaded")
        w0_loaded = sem("w0_loaded")
        w1_loaded = sem("w1_loaded")
        x_loaded = [sem(f"x_loaded{q}") for q in range(4)]
        wt_loaded = sem("wt_loaded")
        wm_loaded = sem("wm_loaded")
        dve_done = sem("dve_done")
        tern_summed = sem("tern_summed")

        with ExitStack() as c1:
            def eb(name, shape, dt=F32):
                return sb(name, shape, dt, c1)

            w0 = eb("w0", [P, W0_N])
            w1 = eb("w1", [P, W1_N])
            xc = eb("xc", [P, NC2, TOK])
            z = eb("z", [P, NC2, TOK])
            x1 = eb("x1", [P, NC2, TOK])
            th = eb("th", [P, TOK])
            ys = eb("ys", [P, TOK])
            pool_w = eb("pool_w", [P, NC2, QUART // 2])
            xp = eb("xp", [P, NC2, BATCH * POOLED])
            ph = eb("ph", [P, BATCH * POOLED])
            gt = eb("gt", [P, 4, INTER])
            sc = eb("sc", [P, 2, BATCH, POOLED])
            at = eb("at", [P, 4, PIX])
            sc_max = eb("sc_max", [P, 2 * BATCH])
            sc_sum = eb("sc_sum", [P, 2 * BATCH])
            sc_inv = eb("sc_inv", [P, 2 * BATCH])
            zst = eb("zst", [P, NC2, 4, 6])
            zmv = eb("zmv", [P, NC2, 2])
            small = eb("small", [P, 112])
            tern_sum = eb("tern_sum", [P, 1])
            qbits = eb("qbits", [P, QUANT])
            qsign = eb("qsign", [P, QUANT])
            w1q = eb("w1q", [P, NC2, P], BF16)
            w2q = eb("w2q", [P, 9, P], BF16)
            w3q = eb("w3q", [P, CH], BF16)
            pegq = eb("pegq", [P, 9])
            dwq = eb("dwq", [P, 9, P], BF16)
            hp1 = eb("hp1", [P, BATCH, PAD, PAD], BF16)
            hp2 = eb("hp2", [P, BATCH, PAD, PAD], BF16)
            hq3 = eb("hq3", [P, TOK], BF16)

            hi = ys[:, :].bitcast(BF16)
            lo = th[:, :].bitcast(BF16)
            r1 = z
            r256 = xc
            n1 = z[:, 0, :]
            n256 = z[:, 1, :]
            h = xc[:, 0, :]
            pre = xc
            x2 = z

            def A0(name, lo_=0, n=None):
                a_, w_ = W0[name]
                return w0[:, a_ + lo_:a_ + lo_ + (w_ - lo_ if n is None else n)]

            def A1(name, lo_=0, n=None):
                a_, w_ = W1[name]
                return w1[:, a_ + lo_:a_ + lo_ + (w_ - lo_ if n is None else n)]

            cols = iter(range(112))

            def col(n=1):
                c = [next(cols) for _ in range(n)]
                return small[:, c[0]:c[0] + n]

            z_ve, z_rstd, z_a, z_b = col(2), col(2), col(2), col(2)
            z_t = col(2)
            inv_ve = [col(1), col(1), col(2)]
            inv_rs = [col(1), col(1), col(2)]
            inv_g = [col(1), col(1), col(2)]
            mi = [col(1), col(1), col(2)]
            bnb = [col(1), col(1), col(2)]
            pb1 = col(1)
            aff_a = [col(1), col(1), col(2)]
            maxes = [col(8)] + [col(4) for _ in range(3)]
            gmax = [col(1) for _ in range(4)]
            tern_scale, tern_inv = col(1), col(1)
            top = [col(1) for _ in range(4)]
            scl = [col(1) for _ in range(4)]
            isc = [col(1) for _ in range(4)]
            fac = [isc[0], col(1), isc[2], isc[3]]
            facn = col(1), col(1), col(1), col(1)

            theta_done = sem("theta_done")
            theta_out = sem("theta_out")
            pooled = sem("pooled")
            phi_done = sem("phi_done")
            phi_out = sem("phi_out")
            g_done = sem("g_done")
            g_out = sem("g_out")
            scores_done = sem("scores_done")
            shifted = sem("shifted")
            exped = sem("exped")
            weights_ready = sem("weights_ready")
            turned = sem("turned")
            turned_out_dve = sem("turned_out_dve")
            turned_out_act = sem("turned_out_act")
            y_done = sem("y_done")
            y_out = sem("y_out")
            z_done = sem("z_done")
            z_out = sem("z_out")
            z_var = sem("z_var")
            z_pow = sem("z_pow")
            z_affine = sem("z_affine")
            z_scaled = sem("z_scaled")
            x1_by_pool = sem("x1_by_pool")
            signs = sem("signs")
            wq_ready = sem("wq_ready")
            padded_zero = sem("padded_zero")
            bn_ve = sem("bn_ve")
            bn_pow = sem("bn_pow")
            max_ready = sem("max_ready")
            max_rows = sem("max_rows")
            tern_scaled = sem("tern_scaled")
            scale_ready = sem("scale_ready")
            rounded = sem("rounded")
            parts_ready = sem("parts_ready")
            conv_done = sem("conv_done")
            relu_out = sem("relu_out")
            res_added = sem("res_added")
            x2_ready = sem("x2_ready")
            tok_done = sem("tok_done")
            tok_out_dve = sem("tok_out_dve")
            tok_out_act = sem("tok_out_act")

            block = c1.enter_context(nc.Block())

            @block.sync
            def _(sp):
                sp.dma_start(w0[:], w0_in).then_inc(w0_loaded, 16)
                for q in range(4):
                    for c in range(NC2):
                        sp.dma_start(
                            xc[:, c, q * QUART:(q + 1) * QUART].rearrange("p (b n) -> p b n", b=2),
                            x_in[2 * q:2 * q + 2, c * P:(c + 1) * P, :].rearrange("b p n -> p b n"),
                        ).then_inc(x_loaded[q], 16)
                sp.dma_start(fix[:], fix_in).then_inc(fix_loaded, 16)
                sp.dma_start(w1[:], w1_in).then_inc(w1_loaded, 16)
                sp.dma_start(fixb[:], fixb_in.bitcast(BF16)).then_inc(fixb_loaded, 16)
                sp.dma_start(wt[:], wt_in).then_inc(wt_loaded, 16)
                sp.dma_start(wm[:], wm_in).then_inc(wm_loaded, 16)

            @block.gpsimd
            def _(pool):
                pool.memset(hp1[:], 0.0).then_inc(padded_zero, 1)
                pool.memset(hp2[:], 0.0).then_inc(padded_zero, 1)
                pool.wait_ge(fix_loaded, 16)
                pool.wait_ge(bn_ve, 3)
                for k in range(3):
                    pool.tensor_tensor(inv_rs[k], inv_ve[k], F("minus_half", 0, 2 if k == 2 else 1),
                                       ALU.pow).then_inc(bn_pow, 1)
                def z_deviation(o):
                    pool.wait_ge(z_var, o + 1)
                    pool.tensor_tensor(z_rstd[:, o:o + 1], z_ve[:, o:o + 1], F("minus_half", 0, 1), ALU.pow)\
                        .then_inc(z_pow, 1)

                def add_x(o, n):
                    q = QUARTERS[n]
                    pool.wait_ge(z_scaled, 4 * o + n + 1)
                    x_ = x1[:, o, q * QUART:(q + 1) * QUART]
                    pool.tensor_tensor(x_, x_, xc[:, o, q * QUART:(q + 1) * QUART], ALU.add).then_inc(x1_by_pool, 1)

                z_deviation(0)
                add_x(0, 0)
                z_deviation(1)
                add_x(0, 2)
                add_x(1, 0)
                add_x(1, 2)

            @block.tensor
            def _(pe):
                pe.wait_ge(w0_loaded, 16)
                for q in range(4):
                    pe.wait_ge(x_loaded[q], 32)
                    for c in range(NC2):
                        mm = pe.matmul(ps[:, q, :], A0("theta", c * P, P), xc[:, c, q * QUART:(q + 1) * QUART],
                                       start=(c == 0), stop=(c == 1))
                    mm.then_inc(theta_done, 1)
                pe.wait_ge(pooled, 4)
                for c in range(NC2):
                    mm = pe.matmul(ps[:, 4, :], A0("phi", c * P, P), xp[:, c, :], start=(c == 0), stop=(c == 1))
                mm.then_inc(phi_done, 1)
                for q in range(4):
                    for c in range(NC2):
                        mm = pe.matmul(ps[:, 5, q * P:(q + 1) * P], xp[:, c, q * P:(q + 1) * P], A0("g", c * P, P),
                                       start=(c == 0), stop=(c == 1))
                mm.then_inc(g_done, 1)
                pe.wait_ge(theta_out, 4)
                pe.wait_ge(phi_out, 1)
                for n in range(2):
                    for b in range(BATCH):
                        mm = pe.matmul(ps[:, 6 + n, b * POOLED:(b + 1) * POOLED],
                                       th[:, b * PIX + n * P:b * PIX + (n + 1) * P],
                                       ph[:, b * POOLED:(b + 1) * POOLED], start=True, stop=True)
                    mm.then_inc(scores_done, 1)
                pe.wait_ge(weights_ready, 1)
                pe.wait_ge(fix_loaded, 16)
                for p in range(4):
                    for n in range(2):
                        mm = pe.transpose(ps[:, p // 2, (p % 2) * PIX + n * P:(p % 2) * PIX + (n + 1) * P],
                                          sc[:, n, 2 * p:2 * p + 2, :].rearrange("p b m -> p (b m)"), F("ident"))
                    if p % 2:
                        mm.then_inc(turned, 1)
                pe.wait_ge(g_out, 1)
                for hb in range(2):
                    pe.wait_ge(turned_out_act if hb else turned_out_dve, 1)
                    for k in range(2):
                        p = 2 * hb + k
                        for par in range(2):
                            r = par * POOLED
                            mm = pe.matmul(ps[:, 2 + 2 * par + hb, k * PIX:(k + 1) * PIX],
                                           gt[r:r + POOLED, p, :], at[r:r + POOLED, p, :], start=True, stop=True)
                    mm.then_inc(y_done, 1)
                pe.wait_ge(tern_summed, 1)
                pe.matmul(ps[:, 1, 0:1], F("ones"), tern_sum[:], start=True, stop=True).then_inc(tern_summed, 1)
                pe.wait_ge(y_out, 4)
                for o in range(NC2):
                    for q in range(4):
                        if o == 0 and q == 3:
                            pe.wait_ge(tern_scaled, 1)
                        pe.matmul(ps[:, (6 + 4 * o + q) % 8, :], A0("wz", o * P, P), ys[:, q * QUART:(q + 1) * QUART],
                                  start=True, stop=True).then_inc(z_done, 1)

                def all_max(k, ready):
                    pe.wait_ge(max_ready, ready)
                    pe.matmul(ps[:, 7, 0:P], gmax[k].broadcast_to([P, P]), F("ident"), start=True, stop=True)\
                      .then_inc(max_rows, 1)

                pe.wait_ge(z_out, 8)
                all_max(0, 1)
                pe.wait_ge(wq_ready, 1)
                for q in range(4):
                    pe.wait_ge(parts_ready, q + 1)
                    k = 0
                    for part in (hi, lo):
                        for c in range(NC2):
                            o = c * TOK + q * QUART
                            mm = pe.matmul(ps[:, q, :], w1q[:, c, :], part[:, o:o + QUART], start=(k == 0), stop=(k == 3))
                            k += 1
                    mm.then_inc(conv_done, 1)
                all_max(1, 2)
                for k, (src, wgt) in enumerate(((hp1, dwq), (hp2, w2q))):
                    for q in range(4):
                        pe.wait_ge(parts_ready, 4 + 4 * k + q + 1)
                        for tap in range(9):
                            dy, dx = divmod(tap, 3)
                            mm = pe.matmul(ps[:, 4 * (1 - k) + q, :], wgt[:, tap, :],
                                           src[:, 2 * q:2 * q + 2, dy:dy + IMG, dx:dx + IMG],
                                           start=(tap == 0), stop=(tap == 8))
                        mm.then_inc(conv_done, 1)
                    all_max(2 + k, 3 + k)
                for q in range(4):
                    pe.wait_ge(parts_ready, 12 + q + 1)
                    for o in range(NC2):
                        n = 2 * q + o
                        pe.matmul(ps[:, (4 + n) % 8, :], w3q[:, o * P:(o + 1) * P], hq3[:, q * QUART:(q + 1) * QUART],
                                  start=True, stop=True).then_inc(conv_done, 1)
                for n in range(8):
                    pe.wait_ge(x2_ready, 2 * (n // 2) + 2)
                    for k in range(2):
                        t = 2 * n + k
                        for c in range(NC2):
                            mm = pe.transpose(ps[:, (4 + n) % 8, k * CH + c * P:k * CH + (c + 1) * P],
                                              x2[:, c, t * P:(t + 1) * P], F("ident"))
                    mm.then_inc(tok_done, 1)

            @block.scalar
            def _(act):
                act.wait_ge(w0_loaded, 16)
                for q in range(4):
                    act.wait_ge(theta_done, q + 1)
                    act.activation(th[:, q * QUART:(q + 1) * QUART], ps[:, q, :], ACT.Identity,
                                   bias=A0("theta_b")).then_inc(theta_out, 1)
                act.wait_ge(phi_done, 1)
                act.activation(ph[:, :], ps[:, 4, :], ACT.Identity, bias=A0("phi_b")).then_inc(phi_out, 1)
                act.wait_ge(w1_loaded, 16)
                act.activation(qsign[:], w1[:, 0:QUANT], ACT.Sign).then_inc(signs, 1)
                act.wait_ge(shifted, 1)
                act.activation(sc[:].rearrange("p n b m -> p (n b m)"), sc[:].rearrange("p n b m -> p (n b m)"), ACT.Exp,
                               scale=float(INTER) ** -0.5).then_inc(exped, 1)
                act.wait_ge(turned, 2)
                act.activation(at[:, 2:4, :].rearrange("p a n -> p (a n)"), ps[:, 1, :], ACT.Copy).then_inc(turned_out_act, 1)
                yb = ys[:, :].rearrange("p (h k r n) -> p h r k n", h=2, k=2, r=2)
                for hb in range(2):
                    act.wait_ge(y_done, hb + 1)
                    for par in range(2):
                        act.activation(yb[:, hb, par], ps[:, 2 + 2 * par + hb, :].rearrange("p (k n) -> p k n", k=2),
                                       ACT.Copy).then_inc(y_out, 1)
                def z_to_sbuf(o, q):
                    act.wait_ge(z_done, 4 * o + q + 1)
                    act.activation(z[:, o, q * QUART:(q + 1) * QUART], ps[:, (6 + 4 * o + q) % 8, :], ACT.Identity,
                                   bias=A0("wz_b", o, 1)).then_inc(z_out, 1)

                def scale_z(o, n):
                    sl = slice(QUARTERS[n] * QUART, (QUARTERS[n] + 1) * QUART)
                    act.wait_ge(z_affine, o + 1)
                    act.activation(x1[:, o, sl], z[:, o, sl], ACT.Identity, scale=z_a[:, o:o + 1],
                                   bias=z_b[:, o:o + 1]).then_inc(z_scaled, 1)

                for q in range(4):
                    z_to_sbuf(0, q)
                z_to_sbuf(1, 0)
                z_to_sbuf(1, 1)
                scale_z(0, 0)
                z_to_sbuf(1, 2)
                z_to_sbuf(1, 3)
                scale_z(0, 1)
                scale_z(0, 2)
                scale_z(0, 3)
                for n in range(4):
                    scale_z(1, n)
                act.wait_ge(scale_ready, 1)
                for q in range(4):
                    sl = slice(q * QUART, (q + 1) * QUART)
                    act.activation(r256[:, :, sl], x1[:, :, sl], ACT.Copy, bias=ROUND_256, scale=isc[0]).then_inc(rounded, 1)
                    act.activation(r1[:, :, sl], x1[:, :, sl], ACT.Copy, bias=ROUND_1, scale=isc[0]).then_inc(rounded, 1)
                for k in range(1, 4):
                    act.wait_ge(scale_ready, k + 1)
                    for q in range(4):
                        sl = slice(q * QUART, (q + 1) * QUART)
                        src = ps[:, q, :] if k == 1 else h[:, sl]
                        act.activation(n256[:, sl], src, ACT.Copy, bias=ROUND_256, scale=fac[k]).then_inc(rounded, 1)
                        act.activation(n1[:, sl], src, ACT.Copy, bias=ROUND_1, scale=facn[k]).then_inc(rounded, 1)
                    if k < 3:
                        for q in range(4):
                            sl = slice(q * QUART, (q + 1) * QUART)
                            act.wait_ge(conv_done, 4 * k + q + 1)
                            act.activation(h[:, sl], ps[:, 4 * (2 - k) + q, :], ACT.Relu, bias=bnb[k - 1],
                                           scale=aff_a[k - 1]).then_inc(relu_out, 1)
                for q in range(4):
                    sl = slice(q * QUART, (q + 1) * QUART)
                    for o in range(NC2):
                        act.wait_ge(res_added, 2 * q + o + 1)
                        act.activation(x2[:, o, sl], pre[:, o, sl], ACT.Relu, bias=bnb[2][:, o:o + 1]).then_inc(x2_ready, 1)
                for n in range(0, 8, 2):
                    act.wait_ge(tok_done, n + 1)
                    act.activation(X[:, 2 * n:2 * n + 2, :].rearrange("p a n -> p (a n)"), ps[:, (4 + n) % 8, :],
                                   ACT.Copy).then_inc(tok_out_act, 1)

            @block.vector
            def _(dve):
                steps = [0]

                def settle(ins):
                    steps[0] += 1
                    ins.then_inc(dve_done, 1)
                    dve.wait_ge(dve_done, steps[0])

                for q in range(4):
                    dve.wait_ge(x_loaded[q], 32)
                    xq = xc[:, :, q * QUART:(q + 1) * QUART].rearrange("p c (n two) -> p c n two", two=2)
                    settle(dve.tensor_tensor(pool_w[:], xq[:, :, :, 0], xq[:, :, :, 1], ALU.max))
                    for c in range(NC2):
                        pw = pool_w[:, c, :].rearrange("p (g two w) -> p g two w", two=2, w=IMG // 2)
                        op = dve.tensor_tensor(
                            xp[:, c, q * P:(q + 1) * P].rearrange("p (g w) -> p g w", w=IMG // 2),
                            pw[:, :, 0, :], pw[:, :, 1, :], ALU.max)
                        if c == 0:
                            settle(op)
                        else:
                            op.then_inc(pooled, 1)
                    dve.wait_ge(pooled, q + 1)
                dve.wait_ge(w1_loaded, 16)
                settle(dve.tensor_scalar(qbits[:], w1[:, 0:QUANT], SQRT2, None, ALU.mult))
                settle(dve.tensor_scalar(qbits[:].bitcast(I32), qbits[:].bitcast(I32), 0x7F800000, None, ALU.bitwise_and))
                settle(dve.tensor_scalar(qbits[:], qbits[:], 2.0 ** -14, 1.0, ALU.max, ALU.min))
                dve.wait_ge(w0_loaded, 16)
                dve.wait_ge(g_done, 1)
                dve.tensor_tensor(gt[:], ps[:, 5, :].rearrange("p (a n) -> p a n", a=4),
                                  A0("g_b").unsqueeze(1).broadcast_to([P, 4, INTER]), ALU.add).then_inc(g_out, 1)
                dve.wait_ge(signs, 1)
                dve.wait_ge(fix_loaded, 16)

                def quantised(name, dst):
                    a_, n_ = W1[name]
                    m_, s_ = qbits[:, a_:a_ + n_], qsign[:, a_:a_ + n_]
                    return dve.tensor_tensor(dst, m_, s_, ALU.mult)

                quantised("w1", w1q[:].rearrange("p a n -> p (a n)"))
                quantised("w2", w2q[:].rearrange("p a n -> p (a n)"))
                quantised("w3", w3q[:])
                settle(quantised("peg", pegq[:]))
                dve.wait_ge(scores_done, 2)
                s_ps = ps[:, 6:8, :].rearrange("p n (b m) -> p (n b) m", m=POOLED)
                sc3 = sc[:].rearrange("p n b m -> p (n b) m")
                wide = [P, 2 * BATCH, POOLED]
                settle(dve.tensor_reduce(sc_max[:], s_ps, AX.X, ALU.max))
                dve.tensor_tensor(sc3, s_ps, sc_max[:].unsqueeze(2).broadcast_to(wide), ALU.subtract).then_inc(shifted, 1)
                dve.wait_ge(exped, 1)
                settle(dve.tensor_reduce(sc_sum[:], sc3, AX.X, ALU.add))
                settle(dve.reciprocal(sc_inv[:], sc_sum[:]))
                dve.tensor_tensor(sc3, sc3, sc_inv[:].unsqueeze(2).broadcast_to(wide), ALU.mult).then_inc(weights_ready, 1)
                for tap in range(9):
                    op = dve.tensor_scalar(dwq[:, tap, :], F("stack"), pegq[:, tap:tap + 1], None, ALU.mult)
                op.then_inc(wq_ready, 1)
                dve.wait_ge(turned, 1)
                dve.tensor_copy(at[:, 0:2, :].rearrange("p a n -> p (a n)"), ps[:, 0, :]).then_inc(turned_out_dve, 1)
                for k, v_ in enumerate(("v1", "v2", "v3")):
                    dve.tensor_scalar(inv_ve[k], A1(v_), EPS, None, ALU.add).then_inc(bn_ve, 1)
                dve.wait_ge(bn_pow, 3)
                for k in range(3):
                    op = dve.tensor_tensor(inv_g[k], inv_rs[k], A1(f"g{k + 1}"), ALU.mult)
                settle(op)
                for k in range(3):
                    op = dve.tensor_tensor(mi[k], inv_g[k], A1(f"m{k + 1}"), ALU.mult)
                settle(op)
                for k in range(3):
                    op = dve.tensor_tensor(bnb[k], A1(f"b{k + 1}"), mi[k], ALU.subtract)
                settle(op)
                settle(dve.tensor_tensor(pb1, inv_g[0], A1("peg_b"), ALU.mult))
                settle(dve.tensor_tensor(bnb[0], bnb[0], pb1, ALU.add))
                dve.wait_ge(wt_loaded, 16)
                dve.tensor_reduce(tern_sum[:], T("tern"), AX.X, ALU.add, apply_absolute_value=True)\
                   .then_inc(tern_summed, 1)
                dve.wait_ge(tern_summed, 2)
                dve.tensor_scalar(tern_scale, ps[:, 1, 0:1], 1.0 / (CH * CH), EPS, ALU.mult, ALU.max)\
                   .then_inc(tern_scaled, 1)
                dve.wait_ge(tern_scaled, 1)
                settle(dve.reciprocal(tern_inv, tern_scale))
                settle(dve.tensor_scalar(T("tern"), T("tern"), tern_inv, ROUND_1, ALU.mult, ALU.add))
                settle(dve.tensor_scalar(T("tern"), T("tern"), ROUND_1, -1.0, ALU.subtract, ALU.max))
                settle(dve.tensor_scalar(T("tern"), T("tern"), 1.0, tern_scale, ALU.min, ALU.mult))
                def stats_of(o, quarters):
                    for q in quarters:
                        dve.wait_ge(z_out, 4 * o + q + 1)
                        op = dve.bn_stats(zst[:, o, q, :], z[:, o, q * QUART:(q + 1) * QUART])
                    return op

                def variance(o):
                    settle(dve.bn_aggr(zmv[:, o, :], zst[:, o].rearrange("p a n -> p (a n)")))
                    dve.tensor_scalar(z_ve[:, o:o + 1], zmv[:, o, 1:2], EPS, None, ALU.add).then_inc(z_var, 1)

                def affine_z(o):
                    c = slice(o, o + 1)
                    dve.wait_ge(z_pow, o + 1)
                    settle(dve.tensor_tensor(z_a[:, c], z_rstd[:, c], A0("gamma", o, 1), ALU.mult))
                    settle(dve.tensor_tensor(z_t[:, c], z_a[:, c], zmv[:, o, 0:1], ALU.mult))
                    dve.tensor_tensor(z_b[:, c], A0("beta", o, 1), z_t[:, c], ALU.subtract).then_inc(z_affine, 1)

                def add_x(o, n):
                    q = QUARTERS[n]
                    dve.wait_ge(z_scaled, 4 * o + n + 1)
                    x_ = x1[:, o, q * QUART:(q + 1) * QUART]
                    settle(dve.tensor_tensor(x_, x_, xc[:, o, q * QUART:(q + 1) * QUART], ALU.add))

                def max_x(o, n):
                    q = QUARTERS[n]
                    if n % 2 == 0:
                        dve.wait_ge(x1_by_pool, 2 * o + n // 2 + 1)
                    return dve.tensor_reduce(maxes[0][:, 4 * o + n:4 * o + n + 1], x1[:, o, q * QUART:(q + 1) * QUART],
                                             AX.X, ALU.max, apply_absolute_value=True)

                settle(stats_of(0, range(4)))
                variance(0)
                stats_of(1, range(2))
                affine_z(0)
                settle(stats_of(1, range(2, 4)))
                variance(1)
                max_x(0, 0)
                affine_z(1)
                add_x(0, 1)
                max_x(0, 1)
                add_x(0, 3)
                max_x(0, 3)
                max_x(0, 2)
                for n in (1, 0, 3, 2):
                    if n % 2:
                        add_x(1, n)
                    last_max = max_x(1, n)

                def scale_of(k, n, acc_scale=None):
                    dve.wait_ge(max_rows, k + 1)
                    settle(dve.tensor_reduce(top[k], ps[:, 7, 0:P], AX.X, ALU.max))
                    if acc_scale is not None:
                        settle(dve.tensor_tensor(scl[k], top[k], acc_scale, ALU.mult))
                        settle(dve.tensor_scalar(scl[k], scl[k], MIN_ABS, 1.0 / QMAX, ALU.max, ALU.mult))
                    else:
                        settle(dve.tensor_scalar(scl[k], top[k], MIN_ABS, 1.0 / QMAX, ALU.max, ALU.mult))
                    settle(dve.reciprocal(isc[k], scl[k]))
                    if acc_scale is not None:
                        settle(dve.tensor_tensor(fac[k], isc[k], acc_scale, ALU.mult))
                    dve.tensor_tensor(facn[k], fac[k], F("low_half"), ALU.mult).then_inc(scale_ready, 1)

                def affine_of(k):
                    if k == 3:
                        settle(dve.tensor_scalar(aff_a[2], inv_g[2], scl[k], None, ALU.mult))
                    else:
                        settle(dve.tensor_tensor(aff_a[k - 1], inv_g[k - 1], scl[k], ALU.mult))

                settle(last_max)
                dve.tensor_reduce(gmax[0], maxes[0], AX.X, ALU.max).then_inc(max_ready, 1)
                scale_of(0, 1)
                hi3 = hi.rearrange("p (c n) -> p c n", c=NC2)
                lo3 = lo.rearrange("p (c n) -> p c n", c=NC2)
                for q in range(4):
                    sl = slice(q * QUART, (q + 1) * QUART)
                    dve.wait_ge(rounded, 2 * q + 1)
                    settle(dve.tensor_scalar(hi3[:, :, sl], r256[:, :, sl], ROUND_256, None, ALU.subtract))
                    dve.wait_ge(rounded, 2 * q + 2)
                    dve.scalar_tensor_tensor(lo3[:, :, sl], r1[:, :, sl], ROUND_1, hi3[:, :, sl],
                                             ALU.subtract, ALU.subtract).then_inc(parts_ready, 1)
                dve.wait_ge(padded_zero, 2)
                for k in range(1, 4):
                    for q in range(4):
                        sl = slice(q * QUART, (q + 1) * QUART)
                        if k == 1:
                            dve.wait_ge(conv_done, q + 1)
                            op = dve.tensor_reduce(maxes[k][:, q:q + 1], ps[:, q, :], AX.X, ALU.max,
                                                   apply_absolute_value=True)
                        else:
                            dve.wait_ge(relu_out, 4 * (k - 2) + q + 1)
                            op = dve.tensor_reduce(maxes[k][:, q:q + 1], h[:, sl], AX.X, ALU.max,
                                                   apply_absolute_value=True)
                    settle(op)
                    dve.tensor_reduce(gmax[k], maxes[k], AX.X, ALU.max).then_inc(max_ready, 1)
                    scale_of(k, 1, scl[0] if k == 1 else None)
                    affine_of(k)
                    for q in range(4):
                        sl = slice(q * QUART, (q + 1) * QUART)
                        dve.wait_ge(rounded, 8 * k + 2 * q + 1)
                        settle(dve.tensor_scalar(n256[:, sl], n256[:, sl], F("half_sign"), F("half_shift"),
                                                 ALU.mult, ALU.add))
                        dve.wait_ge(rounded, 8 * k + 2 * q + 2)
                        if k == 3:
                            dve.tensor_tensor(hq3[:, sl], n1[:, sl], n256[:, sl], ALU.add).then_inc(parts_ready, 1)
                        else:
                            dst = (hp1 if k == 1 else hp2)[:, 2 * q:2 * q + 2, 1:1 + IMG, 1:1 + IMG]
                            shape = "p (b h w) -> p b h w"
                            dve.tensor_tensor(dst, n1[:, sl].rearrange(shape, b=2, h=IMG),
                                              n256[:, sl].rearrange(shape, b=2, h=IMG), ALU.add).then_inc(parts_ready, 1)
                for q in range(4):
                    sl = slice(q * QUART, (q + 1) * QUART)
                    for o in range(NC2):
                        n = 2 * q + o
                        dve.wait_ge(conv_done, 12 + n + 1)
                        dve.scalar_tensor_tensor(pre[:, o, sl], ps[:, (4 + n) % 8, :], aff_a[2][:, o:o + 1], x1[:, o, sl],
                                                 ALU.mult, ALU.add).then_inc(res_added, 1)
                for n in range(1, 8, 2):
                    dve.wait_ge(tok_done, n + 1)
                    dve.tensor_copy(X[:, 2 * n:2 * n + 2, :].rearrange("p a n -> p (a n)"), ps[:, (4 + n) % 8, :])\
                       .then_inc(tok_out_dve, 1)

        with ExitStack() as c2:
            def lb(name, shape, dt=F32):
                return sb(name, shape, dt, c2)

            xn = lb("xn", [P, 2, 2, CH])
            xnT = lb("xnT", [P, 2, NC2, PIX])
            xnT3 = lb("xnT3", [P, 2, NC2, PIX])
            xt = lb("xt", [P, 2, 2, CH])
            spare = lb("spare", [P, 1])
            stats = lb("stats", [P, 2, 2, 6])
            mv = lb("mv", [P, 2, 2, 2])
            ve = lb("ve", [P, 2, 2])
            rstd = lb("rstd", [P, 2, 2])
            bq_scaled = lb("bq_scaled", [P, NC2])
            qk = lb("qk", [P, 2, NC2, PIX])
            rest = lb("rest", [P, 2, NC2, PIX])
            parts = lb("parts", [P, 2, 3, NC2, PIX], BF16)
            QS = lb("QS", [P, 2, HEADS, PIX], BF16)
            KS = lb("KS", [P, 2, HEADS, PIX], BF16)
            V = lb("V", [P, 2, 2, HEADS, SLOT])
            nmax = lb("nmax", [P, UNITS, 4])
            Pr = lb("Pr", [P, PR_RING, 512])
            PT = lb("PT", [P, PT_RING, 512])
            OT = lb("OT", [P, 2, PIX])
            oinv = lb("oinv", [P, 2, 2, 4])
            attn = lb("attn", [P, 2, CH])
            attnT = lb("attnT", [P, NC2, PIX])
            lg = lb("lg", [P, 6, 2, EXPERTS])
            l1 = lb("l1", [P, 3, 2])
            gate = lb("gate", [P, 2, EXPERTS])
            gateT = lb("gateT", [EXPERTS, 2, P])
            acc = lb("acc", [P, 2, CH])
            accT = lb("accT", [P, NC2, PIX])
            res = lb("res", [P, 2, NC2, PIX])

            PHASES, CREDIT, TOTAL = phases()
            sems = {name: sem(name) for name in CREDIT}
            prepared = sem("prepared")
            bias_loaded = sem("bias_loaded")

            def wait(eng, at, name, piece, less=0):
                if at.asks_more(name, piece, less):
                    eng.wait_ge(sems[name], at.count(name, piece, less))

            def full(eng, at, piece):
                b = 6 + piece[3] % 2 if piece[0] == "O1" else at.bank_of(piece)
                if b is not None:
                    wait(eng, at, f"bank_full{b}", piece)

            def drained(eng, at, piece, less=0):
                b = 6 + piece[3] % 2 if piece[0] == "O1" else at.bank_of(piece)
                if b is not None:
                    wait(eng, at, f"bank_drained{b}", piece, less)

            def bank(at, piece):
                return ps[:, at.phase.bank[piece], :]

            def drain(at, piece):
                return sems[f"bank_drained{at.phase.bank[piece]}"]

            def flat(ap):
                return ap.rearrange("p a n -> p (a n)")

            def which(stage):
                return stage % 2

            def normT(at, stage, batch):
                return xnT3[:, at.parity(batch)] if stage == 3 else xnT[:, which(stage)]

            def before(piece, by=1):
                return piece[0], piece[1], piece[2] - by, piece[3]

            def earlier_unit(kind, stage, batch, n, by, per):
                return kind, stage, batch + (n - by) // per, (n - by) % per

            def read_back(sp, at, stage, batch, n):
                wait(sp, at, "parts_stored", ("SPLIT", stage, batch, 1 if at.phase is PHASES[0] else n))
                for c, r in enumerate((Q_PARTS, K_PARTS)[n]):
                    sp.dma_start((QS, KS)[n][DH * c:DH * (c + 1), at.parity(batch)],
                                 parts_dram[n, r].rearrange("(h d) n -> d h n", d=DH))\
                        .then_inc(sems["stack_loaded"], 16)

            def sync_piece(sp, at, piece):
                kind, stage, batch, n = piece
                if kind == "SPLIT":
                    if at.i is None and n == 0:
                        wait(sp, at, "stack_loaded", ("SPLIT", stage, batch - 1, 1))
                    wait(sp, at, "third_ready", piece)
                    sp.dma_start(parts_dram[n].rearrange("r (c p) n -> p (r c) n", p=P),
                                 parts[:, n].rearrange("p r c n -> p (r c) n"))\
                        .then_inc(sems["parts_stored"], 16)
                    if at.phase is not PHASES[0]:
                        read_back(sp, at, stage, batch, n)
                    elif n == 1:
                        read_back(sp, at, stage, batch, 0)
                        read_back(sp, at, stage, batch, 1)
                if kind == "FO":
                    if at.i is None:
                        wait(sp, at, "out_stored", before(piece))
                    drained(sp, at, piece)
                    sp.dma_start(out[at.rows_out(batch), :, :].rearrange("b (c p) n -> p (b c) n", p=P),
                                 res[:, at.parity(batch)]).then_inc(sems["out_stored"], 16)

            def pool_piece(pool, at, piece):
                kind, stage, batch, n = piece
                if kind == "LNa":
                    wait(pool, at, "var_ready", piece)
                    pool.tensor_tensor(rstd[:, which(stage)], ve[:, which(stage)], F("minus_half"), ALU.pow)\
                        .then_inc(sems["rstd_ready"], 1)
                if kind == "XB":
                    wait(pool, at, "xn_ready", ("LNb", stage, batch, 0))
                    x_ = X_all[:, at.tiles(batch), :]
                    pool.tensor_tensor(x_, x_, T("bo0").unsqueeze(1).broadcast_to([P, 2, CH]), ALU.add)\
                        .then_inc(sems["x_biased"], 1)
                if kind == "SPLIT" and at.phase is not PHASES[0]:
                    split(pool, at, piece, False)

            def split(eng, at, piece, copies):
                kind, stage, batch, n = piece
                drained(eng, at, ("QK"[n], stage, batch, 0))
                first, second, third = (parts[:, n, r] for r in range(3))
                by_row = "p c (m n) -> p (c m) n"
                eng.tensor_tensor(rest[:, n], qk[:, n], first, ALU.subtract).then_inc(sems["rest_ready"], 1)
                wait(eng, at, "rest_ready", piece)
                wait(eng, at, "parts_stored", before(piece))
                if copies:
                    eng.tensor_copy(second, rest[:, n]).then_inc(sems["second_ready"], 1)
                else:
                    eng.tensor_tensor(second.rearrange(by_row, n=P), rest[:, n].rearrange(by_row, n=P),
                                      F("ones").unsqueeze(1).broadcast_to([P, NC2 * 2, P]), ALU.mult)\
                       .then_inc(sems["second_ready"], 1)
                wait(eng, at, "second_ready", piece)
                eng.tensor_tensor(third, rest[:, n], second, ALU.subtract).then_inc(sems["third_ready"], 1)

            def tensor_piece(pe, at, piece):
                kind, stage, batch, n = piece
                par = at.parity(batch)
                if kind in JOBS:
                    drained(pe, at, piece, 1)
                    d = bank(at, piece)
                mm = None

                def turn4(src):
                    for c in range(NC2):
                        for t in range(2):
                            mm = pe.transpose(d[:, c * PIX + t * P:c * PIX + (t + 1) * P],
                                              src[:, t, c * P:(c + 1) * P], F("ident"))
                    return mm

                def rows(w, w_at, src):
                    for o in range(NC2):
                        for c in range(NC2):
                            mm = pe.matmul(d[:, o * PIX:(o + 1) * PIX],
                                           w[:, c * 3 * CH + w_at + o * P:c * 3 * CH + w_at + (o + 1) * P],
                                           src[:, c, :], start=(c == 0), stop=(c == 1))
                    return mm

                def toks(w, wstep, w_at, src, width=CH):
                    for t in range(2):
                        for c in range(NC2):
                            mm = pe.matmul(d[:, t * width:(t + 1) * width], src[:, c, t * P:(t + 1) * P],
                                           w[:, c * wstep + w_at:c * wstep + w_at + width],
                                           start=(c == 0), stop=(c == 1))
                    return mm

                if kind == "T":
                    wait(pe, at, "xn_ready", ("LNb", stage, batch, 0))
                    mm = turn4(xn[:, which(stage)])
                if kind in ("Q", "K", "V"):
                    drained(pe, at, ("T", stage, batch, 0))
                    w = T("in0" if stage == 0 else "in1")
                    if kind == "V":
                        mm = toks(w, 3 * CH, 2 * CH, normT(at, stage, batch))
                    else:
                        mm = rows(w, 0 if kind == "Q" else CH, normT(at, stage, batch))
                if kind == "S":
                    if n == 0:
                        wait(pe, at, "stack_loaded", ("SPLIT", stage, batch, 1))
                    g, part = n // 3, n % 3
                    r = slice(0, STACK + (BIAS_ROWS if stage == 0 else 0))
                    if part == 0:
                        pe.matmul(d, FB("ident"), FB("tri0"), start=True, stop=False, skip_group_check=True)
                        for j in range(4):
                            mm = pe.matmul(d[:, j * P:(j + 1) * P], QS[r, par, 4 * g + j, 0:P], KS[r, par, 4 * g + j, 0:P],
                                           start=False, stop=(j == 3), skip_group_check=True)
                    else:
                        pe.matmul(d.rearrange("p (j k n) -> p j k n", j=2, k=2)[:, :, 1, :], FB("ident"),
                                  FB("tri1").rearrange("p (j n) -> p j n", j=2), start=True, stop=False,
                                  skip_group_check=True)
                        for jj in range(2):
                            h = 4 * g + 2 * (part - 1) + jj
                            mm = pe.matmul(d[:, jj * PIX:(jj + 1) * PIX], QS[r, par, h, P:2 * P], KS[r, par, h, :],
                                           start=False, stop=(jj == 1), skip_group_check=True)
                if kind == "P":
                    drained(pe, at, ("S", stage, batch, n))
                    for k in range(4):
                        mm = pe.transpose(d[:, k * P:(k + 1) * P], Pr[:, n % PR_RING, k * P:(k + 1) * P], F("ident"))
                if kind == "O0":
                    o = ps[:, 6 + n % 2, :]
                    drained(pe, at, ("P", stage, batch, 3 * n))
                    if n == 0:
                        drained(pe, at, ("V", stage, batch, 0))
                    drained(pe, at, ("O1", stage, batch, n), 1)
                    for j in range(4):
                        pe.matmul(o[32 * j:32 * j + 32, 0:P], V[:, par, 0, 4 * n + j, :],
                                  PT[:, 3 * n % PT_RING, j * P:(j + 1) * P], start=True, stop=True)
                if kind == "O1":
                    o = ps[:, 6 + n % 2, :]
                    drained(pe, at, ("P", stage, batch, 3 * n + 1))
                    drained(pe, at, ("P", stage, batch, 3 * n + 2))
                    for kt in range(2):
                        for j in range(4):
                            k = 2 * (j % 2) + kt
                            mm = pe.matmul(o[32 * j:32 * j + 32, P:2 * P], V[:, par, kt, 4 * n + j, :],
                                           PT[:, (3 * n + 1 + j // 2) % PT_RING, k * P:(k + 1) * P],
                                           start=(kt == 0), stop=(kt == 1))
                    mm.then_inc(sems[f"bank_full{6 + n % 2}"], 1)
                if kind == "OX":
                    drained(pe, at, ("O1", stage, batch, n))
                    for t in range(2):
                        mm = pe.transpose(d[:, t * P:(t + 1) * P], OT[:, n % 2, t * P:(t + 1) * P], F("ident"))
                if kind == "AT":
                    drained(pe, at, ("OX", stage, batch, GROUPS - 1))
                    mm = turn4(attn)
                if kind == "PR":
                    drained(pe, at, ("AT", stage, batch, 0))
                    mm = toks(T("out0" if stage == 0 else "out1"), CH, 0, attnT)
                if kind in ("FF", "R"):
                    drained(pe, at, ("T", stage, batch, 0))
                    if kind == "FF":
                        mm = toks(T("tern"), CH, 0, normT(at, stage, batch))
                    else:
                        mm = toks(M("Wr"), EXPERTS, 0, normT(at, stage, batch), EXPERTS)
                if kind == "GT":
                    wait(pe, at, "gates_ready", ("RT", stage, batch, 3))
                    for t in range(2):
                        mm = pe.transpose(d[0:EXPERTS, t * P:(t + 1) * P], gate[:, t, :], F("ident"))
                if kind == "GB":
                    drained(pe, at, ("GT", stage, batch, 0))
                    for t in range(2):
                        mm = pe.matmul(d[:, t * CH:(t + 1) * CH], gateT[:, t, :], M("be")[0:EXPERTS, :],
                                       start=True, stop=True)
                if kind == "E":
                    t, e = n // 4, n % 4
                    for c in range(NC2):
                        mm = pe.matmul(d, normT(at, stage, batch)[:, c, t * P:(t + 1) * P],
                                       M("We", c * EXPERTS * CH + e * 2 * CH, 2 * CH), start=(c == 0), stop=(c == 1))
                if kind == "CT":
                    drained(pe, at, ("E", stage, batch, 7))
                    drained(pe, at, ("E", stage, batch, 3))
                    mm = turn4(acc)
                if kind == "FO":
                    drained(pe, at, ("CT", stage, batch, 0))
                    for o in range(NC2):
                        for c in range(NC2):
                            pe.matmul(d[:, o * PIX:(o + 1) * PIX], M("Wo", c * CH + o * P, P), accT[:, c, :],
                                      start=(c == 0), stop=False)
                        for t in range(2):
                            mm = pe.matmul(d[:, o * PIX + t * P:o * PIX + (t + 1) * P], xt[:, par, t, o * P:(o + 1) * P],
                                           F("ident"), start=False, stop=(t == 1))
                if kind in JOBS:
                    mm.then_inc(sems[f"bank_full{at.phase.bank[piece]}"], 1)

            def scalar_piece(act, at, piece):
                kind, stage, batch, n = piece
                par = at.parity(batch)

                def copy_out(dst):
                    act.activation(dst, bank(at, piece), ACT.Copy).then_inc(drain(at, piece), 1)

                if kind == "T":
                    full(act, at, piece)
                    full(act, at, {3: ("E", 3, batch - 2, 7), 1: ("FF", 1, batch - 1, 0)}.get(stage, ("V", stage, batch - 1, 0)))
                    copy_out(flat(normT(at, stage, batch)))
                if kind in ("Q", "K"):
                    k = "QK".index(kind)
                    full(act, at, piece)
                    wait(act, at, "rest_ready", ("SPLIT", stage, batch - 1, k))
                    wait(act, at, "parts_stored", ("SPLIT", stage, batch - 1, k))
                    scale = DH ** -0.5 if kind == "Q" else 1.0
                    for dst in (qk[:, k], parts[:, k, 0]):
                        if stage == 0:
                            bias = bq_scaled if kind == "Q" else T("bk0")
                            for c in range(NC2):
                                op = act.activation(dst[:, c, :], bank(at, piece)[:, c * PIX:(c + 1) * PIX], ACT.Identity,
                                                    scale=scale, bias=bias[:, c:c + 1])
                        else:
                            op = act.activation(flat(dst), bank(at, piece), ACT.Copy, scale=scale)
                    op.then_inc(drain(at, piece), 1)
                if kind == "S":
                    wait(act, at, "unit_max", piece)
                    full(act, at, earlier_unit("P", stage, batch, n, PR_RING, UNITS))
                    w_ = P if n % 3 == 0 else PIX
                    for k in range(512 // w_):
                        op = act.activation(Pr[:, n % PR_RING, k * w_:(k + 1) * w_], bank(at, piece)[:, k * w_:(k + 1) * w_],
                                            ACT.Exp, bias=nmax[:, n, k:k + 1])
                    op.then_inc(drain(at, piece), 1)
                if kind == "P" and n % 3 in PT_BY_ACT:
                    full(act, at, piece)
                    pt_free(act, at, piece)
                    copy_out(PT[:, n % PT_RING, :])
                if kind == "O1":
                    full(act, at, piece)
                    full(act, at, earlier_unit("OX", stage, batch, n, 2, GROUPS))
                    act.activation(OT[:, n % 2, :], ps[:, 6 + n % 2, 0:PIX], ACT.Copy)\
                        .then_inc(sems[f"bank_drained{6 + n % 2}"], 1)
                if kind == "AT":
                    full(act, at, piece)
                    full(act, at, ("PR", stage, batch - 1, 0))
                    copy_out(flat(attnT))
                if kind == "RT" and n == 0:
                    wait(act, at, "router_shifted", ("R", stage, batch, 0))
                    act.activation(lg[:, 5], lg[:, 1], ACT.Exp).then_inc(sems["router_exp"], 1)
                if kind == "GT":
                    full(act, at, piece)
                    act.activation(flat(gateT), bank(at, piece)[0:EXPERTS, 0:2 * P], ACT.Copy).then_inc(drain(at, piece), 1)
                if kind == "GB":
                    full(act, at, piece)
                    full(act, at, ("CT", stage, batch - 1, 0))
                    copy_out(flat(acc))
                if kind == "CT":
                    full(act, at, piece)
                    full(act, at, ("FO", stage, batch - 1, 0))
                    copy_out(flat(accT))
                if kind == "FO":
                    full(act, at, piece)
                    wait(act, at, "out_stored", before(piece, 2))
                    for o in range(NC2):
                        op = act.activation(res[:, par, o, :], bank(at, piece)[:, o * PIX:(o + 1) * PIX], ACT.Identity,
                                            bias=M("bo", o, 1))
                    op.then_inc(drain(at, piece), 1)

            def pt_free(eng, at, piece):
                kind, stage, batch, n = earlier_unit("P", piece[1], piece[2], piece[3], PT_RING, UNITS)
                full(eng, at, ("O1", stage, batch, n // 3))

            def vector_piece(dve, at, piece):
                kind, stage, batch, n = piece
                par = at.parity(batch)
                local = [0]

                def settle(ins):
                    local[0] += 1
                    ins.then_inc(sems["dve_step"], 1)
                    wait(dve, at, "dve_step", piece, settled(piece) - local[0])

                def rows_of_x():
                    return xt[:, par] if stage == 3 else X_all[:, at.tiles(batch), :]

                if kind in ("LNa", "LNb"):
                    m, src = which(stage), rows_of_x()
                if kind == "LNa":
                    if stage % 2:
                        drained(dve, at, ("PR", stage - 1, batch, 0))
                        dve.memset(spare[:], 0.0)
                    for t in range(2):
                        op = dve.bn_stats(stats[:, m, t, :], src[:, t, :])
                    settle(op)
                    dve.memset(ve[:, m], EPS)
                    for t in range(2):
                        op = dve.bn_aggr(mv[:, m, t, :], stats[:, m, t, :])
                    settle(op)
                    dve.tensor_tensor(ve[:, m], ve[:, m], mv[:, m, :, 1], ALU.add).then_inc(sems["var_ready"], 1)
                if kind == "LNb":
                    wait(dve, at, "rstd_ready", ("LNa", stage, batch, 0))
                    full(dve, at, ("T", stage, batch - 1, 0))
                    for t in range(2):
                        op = dve.tensor_scalar(xn[:, m, t, :], src[:, t, :], mv[:, m, t, 0:1], rstd[:, m, t:t + 1],
                                               ALU.subtract, ALU.mult)
                    op.then_inc(sems["xn_ready"], 1)
                if kind == "SPLIT" and at.phase is PHASES[0]:
                    split(dve, at, piece, True)
                if kind == "V":
                    full(dve, at, piece)
                    full(dve, at, ("O1", stage, batch - 2, GROUPS - 1))
                    for t in range(2):
                        dst = V[:, par, t, :, 0:DH]
                        src = bank(at, piece)[:, t * CH:(t + 1) * CH].rearrange("p (h d) -> p h d", d=DH)
                        if stage == 0:
                            op = dve.tensor_tensor(dst, src, T("bv0").rearrange("p (h d) -> p h d", d=DH), ALU.add)
                        else:
                            op = dve.tensor_copy(dst, src)
                    op.then_inc(drain(at, piece), 1)
                if kind == "S":
                    full(dve, at, piece)
                    w_ = P if n % 3 == 0 else PIX
                    dve.tensor_reduce(nmax[:, n, 0:512 // w_], bank(at, piece).rearrange("p (j n) -> p j n", n=w_),
                                      AX.X, ALU.max, negate=True).then_inc(sems["unit_max"], 1)
                if kind == "P" and n % 3 not in PT_BY_ACT:
                    pt_free(dve, at, piece)
                    full(dve, at, piece)
                    dve.tensor_copy(PT[:, n % PT_RING, :], bank(at, piece)).then_inc(drain(at, piece), 1)
                if kind == "OX":
                    full(dve, at, piece)
                    if n == 0:
                        full(dve, at, ("AT", stage, batch - 1, 0))
                    o4 = bank(at, piece)[:, 0:2 * P].rearrange("p (t j s) -> p t j s", t=2, j=4)
                    settle(dve.reciprocal(oinv[:, n % 2], o4[:, :, :, DH]))
                    dve.tensor_tensor(attn[:, :, 4 * DH * n:4 * DH * (n + 1)].rearrange("p t (j d) -> p t j d", j=4),
                                      o4[:, :, :, 0:DH], oinv[:, n % 2].unsqueeze(3).broadcast_to([P, 2, 4, DH]),
                                      ALU.mult).then_inc(drain(at, piece), 1)
                if kind in ("PR", "FF"):
                    full(dve, at, piece)
                    if kind == "PR" and stage == 0:
                        wait(dve, at, "x_biased", ("XB", 0, batch, 0))
                    if kind == "PR" and stage == 2:
                        full(dve, at, ("FO", 3, batch - 2, 0))
                    old = flat(X_all[:, at.tiles(batch), :])
                    dve.tensor_tensor(flat(xt[:, par]) if stage == 2 else old, bank(at, piece), old, ALU.add)\
                       .then_inc(drain(at, piece), 1)

                L, D, C, one, two, E = (lg[:, k] for k in range(6))
                m, su = l1[:, 1, :], l1[:, 2, :]

                def wide(v):
                    return v.unsqueeze(2).broadcast_to([P, 2, EXPERTS])

                def first_largest(D, one):
                    settle(dve.scalar_tensor_tensor(C, D, 0.0, F("tie").rearrange("p (t e) -> p t e", t=2),
                                                    ALU.is_equal, ALU.mult))
                    settle(dve.tensor_reduce(m, C, AX.X, ALU.max))
                    settle(dve.tensor_tensor(one, C, wide(m), ALU.is_equal))

                if kind == "R":
                    full(dve, at, piece)
                    dve.tensor_tensor(L, bank(at, piece)[:, 0:2 * EXPERTS].rearrange("p (t e) -> p t e", t=2),
                                      M("br").rearrange("p (t e) -> p t e", t=2), ALU.add).then_inc(drain(at, piece), 1)
                    drained(dve, at, piece)
                    settle(dve.tensor_reduce(l1[:, 0, :], L, AX.X, ALU.max))
                    dve.tensor_tensor(D, L, wide(l1[:, 0, :]), ALU.subtract).then_inc(sems["router_shifted"], 1)
                if kind == "RT" and n == 0:
                    wait(dve, at, "router_shifted", ("R", stage, batch, 0))
                    first_largest(D, one)
                if kind == "RT" and n == 1:
                    settle(dve.scalar_tensor_tensor(L, one, MASKED, D, ALU.mult, ALU.add))
                    settle(dve.tensor_reduce(m, L, AX.X, ALU.max))
                    settle(dve.tensor_tensor(L, L, wide(m), ALU.subtract))
                if kind == "RT" and n == 2:
                    first_largest(L, two)
                if kind == "RT" and n == 3:
                    wait(dve, at, "router_exp", ("RT", stage, batch, 0))
                    settle(dve.tensor_tensor(one, one, two, ALU.add))
                    settle(dve.tensor_reduce(su, E, AX.X, ALU.add))
                    settle(dve.reciprocal(m, su))
                    settle(dve.tensor_tensor(one, one, E, ALU.mult))
                    dve.tensor_tensor(gate[:], one, wide(m), ALU.mult).then_inc(sems["gates_ready"], 1)
                if kind == "E":
                    t, e = n // 4, n % 4
                    if e == 0:
                        drained(dve, at, ("GB", stage, batch, 0))
                    else:
                        drained(dve, at, ("E", stage, batch, n - 1))
                    full(dve, at, piece)
                    for k in range(2):
                        op = dve.scalar_tensor_tensor(acc[:, t, :], bank(at, piece)[:, k * CH:(k + 1) * CH],
                                                      gate[:, t, 2 * e + k:2 * e + k + 1], acc[:, t, :], ALU.mult, ALU.add)
                        if k == 0:
                            settle(op)
                    op.then_inc(drain(at, piece), 1)
                assert local[0] == settled(piece), piece

            def walk(eng, group, piece_of, part=slice(None)):
                for phase in group:
                    pieces = (phase.tensor if piece_of is tensor_piece else phase.others)[part]
                    if not phase.bodies:
                        for piece in pieces:
                            piece_of(eng, Spot(phase), piece)
                    else:
                        with eng.Fori(0, phase.bodies // 2) as i:
                            for half in range(2):
                                for piece in pieces:
                                    piece_of(eng, Spot(phase, i, half), piece)

            for group in (PHASES[0:1], PHASES[1:3], PHASES[3:5]):
                with nc.Block() as block:
                    opening = group[0] is PHASES[0]
                    norms, rest_of = slice(0, NORMS_FIRST), slice(NORMS_FIRST if opening else 0, None)

                    @block.sync
                    def _(sp):
                        if opening:
                            for k, stack in enumerate((QS, KS)):
                                for par in range(2):
                                    sp.dma_start(stack[STACK:STACK + BIAS_ROWS, par], bias_in[:, k].bitcast(BF16))\
                                      .then_inc(bias_loaded, 16)
                            for name in TRANSFERS:
                                sp.sem_inc(sems[name], CREDIT[name])
                        walk(sp, group, sync_piece)
                        if opening:
                            sp.wait_ge(bias_loaded, 64)
                        if group[-1] is PHASES[-1]:
                            sp.wait_ge(sems["out_stored"], TOTAL["out_stored"])
                            sp.wait_ge(sems["stack_loaded"], TOTAL["stack_loaded"])

                    @block.gpsimd
                    def _(pool):
                        if opening:
                            walk(pool, group, pool_piece, norms)
                            pool.memset(X_all[:, 0:2 * LEAD, :], 0.0)
                            pool.memset(X_all[:, 2 * (LEAD + BATCH):, :], 0.0)
                            pool.memset(Pr[:], 1.0)
                            pool.memset(PT[:], 1.0)
                            for buffer in (xt[:], xnT[:, 1], xnT3[:], attn[:], accT[:]):
                                pool.memset(buffer, 0.0)
                            pool.memset(V[:, 1, :, :, 0:DH], 0.0)
                            pool.memset(V[:, :, :, :, DH:].rearrange("p a t h s -> p (a t h) s"), 0.0).then_inc(prepared, 1)
                            pool.wait_ge(prepared, 2)
                            pool.memset(V[:].rearrange("p a t h s -> p (a t h) s")[:, :, DH:DH + 1], 1.0)
                        walk(pool, group, pool_piece, rest_of)

                    @block.tensor
                    def _(pe):
                        if opening:
                            pe.wait_ge(fixb_loaded, 16)
                            pe.wait_ge(wm_loaded, 16)
                        walk(pe, group, tensor_piece)

                    @block.scalar
                    def _(act):
                        if opening:
                            act.wait_ge(prepared, 1)
                        walk(act, group, scalar_piece)

                    @block.vector
                    def _(dve):
                        if opening:
                            for name in CREDIT:
                                if name not in TRANSFERS:
                                    dve.sem_inc(sems[name], CREDIT[name])
                            dve.wait_ge(wt_loaded, 16)
                            dve.tensor_scalar(bq_scaled[:], T("bq0"), DH ** -0.5, None, ALU.mult).then_inc(prepared, 1)
                            walk(dve, group, vector_piece, norms)
                            dve.memset(ps[:, 6:8, 0:PIX], 1.0)
                        walk(dve, group, vector_piece, rest_of)




def bf16_bits(np, v):
    u = np.ascontiguousarray(v, np.float32).view(np.uint32)
    return ((u + 0x7FFF + (u >> 16 & 1)) >> 16).astype(np.uint16)


def _fixed(np):
    fix = np.zeros((P, FIX_N), np.float32)

    def put(name, v):
        a, n = FIX[name]
        fix[:, a:a + n] = v

    r = np.arange(P)
    put("ident", np.eye(P))
    put("ones", 1.0)
    lower = (r >= WID)[:, None]
    put("stack", (r[:, None] % WID) == (r[None, :] % WID))
    put("tie", np.tile(EXPERTS - np.arange(EXPERTS), 2)[None, :])
    put("low_half", lower)
    put("half_sign", np.where(lower, -1.0, 1.0))
    put("half_shift", np.where(lower, 1.0, -1.0) * ROUND_256 - ROUND_1)
    put("minus_half", -0.5)

    fb = np.zeros((P, FIXB_N), np.float32)

    def putb(name, v):
        a, n = FIXB[name]
        fb[:v.shape[0], a:a + n] = v

    tri = np.where(r[None, :] <= r[:, None], 0.0, MASKED)
    putb("ident", np.eye(P))
    putb("tri0", np.tile(tri, (1, 4)))
    putb("tri1", np.tile(tri, (1, 2)))
    def parts(v):
        out, v = [], np.asarray(v, np.float32)
        for _ in range(3):
            h = (bf16_bits(np, v).astype(np.uint32) << 16).view(np.float32)
            out.append(h)
            v = v - h
        return np.stack(out)

    first = 2.0 ** -(2.0 ** -(np.log2(HEADS) - 3))
    slopes = np.asarray([first * first ** h for h in range(HEADS)], np.float32)[:, None]
    where = np.arange(PIX, dtype=np.float32)[None, :]
    all_ = (3, HEADS, PIX)
    bias = np.zeros((BIAS_ROWS, 2, HEADS, PIX), np.float32)
    bias[:3, 0], bias[3:, 0] = np.ones(all_), np.broadcast_to(-where, all_)
    bias[:3, 1], bias[3:, 1] = parts(slopes * where), parts(np.broadcast_to(slopes, all_[1:]))
    return fix, bf16_bits(np, fb), bf16_bits(np, bias)


def kernel(**inputs):
    import numpy as np
    import concourse.bacc as _bacc
    from concourse import mybir as _mybir
    from concourse.bass_utils import run_bass_kernel_spmd as _run

    v = {k: np.asarray(a) for k, a in inputs.items()}
    f32 = np.float32

    def chunks(w):
        return w.reshape(-1, P, w.shape[1]).transpose(1, 0, 2).reshape(P, -1)

    def cols(vec):
        return vec.reshape(-1, P).T

    def twice(a):
        return np.concatenate([a, a], 0)

    def pack(layout, total, **parts):
        buf = np.zeros((P, total), f32)
        for name, a in parts.items():
            at, n = layout[name]
            buf[:, at:at + n] = a
        return buf

    w0 = pack(W0, W0_N, theta=chunks(v["L0_conv_theta_w"].T), phi=chunks(v["L0_conv_phi_w"].T),
              g=chunks(v["L0_conv_g_w"].T), wz=v["L0_conv_wz_w"].T, g_b=v["L0_conv_g_b"][None, :],
              theta_b=cols(v["L0_conv_theta_b"]), phi_b=cols(v["L0_conv_phi_b"]), wz_b=cols(v["L0_conv_wz_b"]),
              gamma=cols(v["L0_conv_bn_gamma"]), beta=cols(v["L0_conv_bn_beta"]))
    c1 = v["L1_conv_w1"].reshape(WID, CH).T
    c2 = v["L1_conv_w2"].transpose(1, 2, 3, 0).reshape(WID, 9, WID)
    inner = {}
    for k in (1, 2):
        for p in "gbmv":
            inner[f"{p}{k}"] = twice(v[f"L1_conv_bn{k}_{p}"][:, None])
    for p in "gbmv":
        inner[f"{p}3"] = cols(v[f"L1_conv_bn3_{p}"])
    w1 = pack(W1, W1_N, w1=chunks(np.concatenate([c1, c1], 1)),
              w2=twice(np.concatenate([c2, c2], 2).reshape(WID, -1)),
              w3=twice(v["L1_conv_w3"].reshape(CH, WID).T), peg=twice(v["L1_conv_peg_w"].reshape(WID, 9)),
              peg_b=twice(v["L1_conv_peg_b"][:, None]), **inner)
    b_in = v["L2_attn_b_in"]
    wt = pack(WT, WT_N, in0=chunks(v["L2_attn_w_in"]), out0=chunks(v["L2_attn_w_out"]),
              in1=chunks(np.concatenate([v[f"L3_attn_w_{p}"].T for p in "qkv"], 1)),
              out1=chunks(v["L3_attn_w_o"].T), tern=chunks(v["L2_ffn_weight"].T), bv0=b_in[None, 2 * CH:],
              bo0=v["L2_attn_b_out"][None, :], bq0=cols(b_in[:CH]), bk0=cols(b_in[CH:2 * CH]))
    be = np.zeros((P, CH), f32)
    be[:EXPERTS] = v["L3_ffn_be"]
    wm = pack(WM, WM_N, We=chunks(v["L3_ffn_We"].transpose(2, 0, 1).reshape(CH, EXPERTS * CH)),
              Wr=chunks(v["L3_ffn_Wr"].T), Wo=chunks(v["L3_ffn_Wo"].T), be=be, bo=cols(v["L3_ffn_bo"]),
              br=np.tile(v["L3_ffn_br"], 2)[None, :])
    fix, fixb, bias = _fixed(np)
    arrays = {"x_dram": np.ascontiguousarray(v["x"].reshape(BATCH, CH, PIX)), "fix_dram": fix, "fixb_dram": fixb,
              "bias_dram": bias,
              "w0_dram": w0, "w1_dram": w1, "wt_dram": wt, "wm_dram": wm}

    nc = _bacc.Bacc("TRN2", target_bir_lowering=False, num_devices=1)
    args = [nc.dram_tensor(n, a.shape, _mybir.dt.from_np(a.dtype), kind="ExternalInput").ap() for n, a in arrays.items()]
    parts_dram = nc.dram_tensor("parts_dram", (2, 3, CH, PIX), _mybir.dt.bfloat16, kind="Internal").ap()
    out = nc.dram_tensor("out_dram", (OUT_LEAD + BATCH, CH, PIX), _mybir.dt.float32, kind="ExternalOutput").ap()
    build(nc, *args, parts_dram, out)
    r = _run(nc, [arrays], core_ids=[0])
    return r.results[0]["out_dram"][OUT_LEAD:].reshape(BATCH, CH, IMG, IMG)
```
